# Optimizing a Trainium2 kernel written in Bass

```python
import numpy as np
import jax
import jax.numpy as jnp

def _softmax(x, axis=-1):
    return jax.nn.softmax(x, axis=axis)

def _gelu(x):
    return jax.nn.gelu(x, approximate=True)

def _silu(x):
    return jax.nn.silu(x)

def _sigmoid(x):
    return jax.nn.sigmoid(x)

def _layernorm(x, axis=-1, eps=1e-05):
    m = jnp.mean(x, axis=axis, keepdims=True)
    v = jnp.var(x, axis=axis, keepdims=True)
    return (x - m) / jnp.sqrt(v + eps)

def _scatter_add(tgt, idx, src, axis=0):
    return tgt.at[idx].add(src)

def _segment_sum(src, seg, n):
    return jax.ops.segment_sum(src, seg, n)
kernel_name = 'mk_seq_preln_d2_jaxref_r8_a4e663'

def setup_inputs(seed: int=0):
    np.random.seed(seed)
    _w = jnp.asarray

    def _L0_attn_setup():
        import jax, jax.numpy as jnp
        import numpy as np
        HEADS = 32
        key = jax.random.key(seed)
        ks = jax.random.split(key, 5)
        H = 512
        B, S = (2, 256)
        w_scale = 1.0 / np.sqrt(H)
        return {'x': jax.random.normal(ks[0], (B, S, H), dtype=jnp.float32), 'attn_qkvw': jax.random.normal(ks[1], (H, 3 * H), dtype=jnp.float32) * w_scale, 'attn_qkvb': jax.random.normal(ks[2], (3 * H,), dtype=jnp.float32) * 0.02, 'attn_ow': jax.random.normal(ks[3], (H, H), dtype=jnp.float32) * w_scale, 'attn_ob': jax.random.normal(ks[4], (H,), dtype=jnp.float32) * 0.02}
    _L0_attn_in = _L0_attn_setup()

    def _L0_ffn_setup():
        import jax, jax.numpy as jnp
        import numpy as np
        BLOCK = 32

        def _dequantize(q_scales, q_vals):
            OUT, n_blocks = q_scales.shape
            codes = q_vals.astype(jnp.float32) - 128.0
            w = q_scales[:, :, None] * codes
            return w.reshape(OUT, n_blocks * BLOCK)
        key = jax.random.key(seed)
        k1, k2, k3, k4 = jax.random.split(key, 4)
        B, S, IN, OUT = (2, 512, 512, 512)
        n_blocks = IN // BLOCK
        x = jax.random.normal(k1, (B, S, IN), dtype=jnp.float32)
        q_scales = jax.random.uniform(k2, (OUT, n_blocks), dtype=jnp.float32) * 0.05
        q_vals = jax.random.randint(k3, (OUT, n_blocks, BLOCK), 0, 32, dtype=jnp.int32)
        bias = jax.random.normal(k4, (OUT,), dtype=jnp.float32)
        return {'x': x, 'q_scales': q_scales, 'q_vals': q_vals, 'bias': bias}
    _L0_ffn_in = _L0_ffn_setup()

    def _L1_attn_setup():
        import jax, jax.numpy as jnp
        import numpy as np
        NEG_INF = -1e+30

        def rotary_pos_emb(x):
            B, T, H, D = x.shape
            exponents = (jnp.arange(0, D, 2)[:D // 2] // D).astype(jnp.float32)
            freqs = 1.0 / jnp.power(jnp.float32(1000.0), exponents)
            theta = jnp.arange(T, dtype=jnp.float32)[:, None] * freqs[None, :]
            cos = jnp.cos(theta)[None, :, None, :]
            sin = jnp.sin(theta)[None, :, None, :]
            xr = x.astype(jnp.float32).reshape(B, T, H, D // 2, 2)
            x0, x1 = (xr[..., 0], xr[..., 1])
            out = jnp.stack([x0 * cos - x1 * sin, x0 * sin + x1 * cos], axis=-1)
            return out.reshape(B, T, H, D).astype(x.dtype)

        def attention_fwd(x, wq, wk, wv, wo, n_heads=32):
            B, T, C = x.shape
            hd = C // n_heads
            xq = (x @ wq.T).reshape(B, T, n_heads, hd)
            xk = (x @ wk.T).reshape(B, T, n_heads, hd)
            xv = (x @ wv.T).reshape(B, T, n_heads, hd)
            xq = rotary_pos_emb(xq)
            xk = rotary_pos_emb(xk)
            scale = hd ** (-0.5)
            scores = jnp.einsum('bqhd,bkhd->bhqk', xq, xk) * scale
            causal = jnp.tril(jnp.ones((T, T), dtype=bool))
            scores = jnp.where(causal[None, None], scores, NEG_INF)
            probs = jax.nn.softmax(scores.astype(jnp.float32), axis=-1).astype(xq.dtype)
            out = jnp.einsum('bhqk,bkhd->bqhd', probs, xv).reshape(B, T, C)
            return out @ wo.T
        key = jax.random.key(seed)
        ks = jax.random.split(key, 5)
        B, T, C = (2, 256, 512)
        s = 0.02
        return {'x': jax.random.normal(ks[0], (B, T, C), jnp.float32), 'wq': jax.random.normal(ks[1], (C, C), jnp.float32) * s, 'wk': jax.random.normal(ks[2], (C, C), jnp.float32) * s, 'wv': jax.random.normal(ks[3], (C, C), jnp.float32) * s, 'wo': jax.random.normal(ks[4], (C, C), jnp.float32) * s}
    _L1_attn_in = _L1_attn_setup()

    def _L1_ffn_setup():
        import jax, jax.numpy as jnp
        import numpy as np
        import math
        D = 512
        TOKENS = (4, 256)
        P = 0.8

        def conn_dense(kernel, x):
            w = jnp.where(kernel, jnp.asarray(1.0, x.dtype), jnp.asarray(-1.0, x.dtype))
            return x @ w

        def ei_dense(x, kernel, scale, p):
            in_dim = x.shape[-1]
            ne = round(in_dim * p)
            x_exc = x[..., :ne]
            x_inh = x[..., ne:]
            xx = jnp.concatenate([x_exc, -p / (1.0 - p) * x_inh], axis=-1)
            return scale * conn_dense(kernel, xx)
        key = jax.random.key(seed)
        ks = jax.random.split(key, 4)
        x = jax.random.normal(ks[0], (*TOKENS, D), dtype=jnp.float32)
        k0 = jax.random.bernoulli(ks[1], 0.5, (D, D))
        k1 = jax.random.bernoulli(ks[2], 0.5, (D, D))
        k2 = jax.random.bernoulli(ks[3], 0.5, (D, D))
        s = jnp.asarray(1.0 / math.sqrt(D), dtype=jnp.float32)
        return {'x': x, 'k0': k0, 's0': s, 'k1': k1, 's1': s, 'k2': k2, 's2': s}
    _L1_ffn_in = _L1_ffn_setup()
    _d = {'L0_attn_x': _L0_attn_in['x'], 'L0_attn_attn_qkvw': _L0_attn_in['attn_qkvw'], 'L0_attn_attn_qkvb': _L0_attn_in['attn_qkvb'], 'L0_attn_attn_ow': _L0_attn_in['attn_ow'], 'L0_attn_attn_ob': _L0_attn_in['attn_ob'], 'L0_ffn_q_scales': _L0_ffn_in['q_scales'], 'L0_ffn_q_vals': _L0_ffn_in['q_vals'], 'L0_ffn_bias': _L0_ffn_in['bias'], 'L1_attn_wq': _L1_attn_in['wq'], 'L1_attn_wk': _L1_attn_in['wk'], 'L1_attn_wv': _L1_attn_in['wv'], 'L1_attn_wo': _L1_attn_in['wo'], 'L1_ffn_k0': _L1_ffn_in['k0'], 'L1_ffn_s0': _L1_ffn_in['s0'], 'L1_ffn_k1': _L1_ffn_in['k1'], 'L1_ffn_s1': _L1_ffn_in['s1'], 'L1_ffn_k2': _L1_ffn_in['k2'], 'L1_ffn_s2': _L1_ffn_in['s2']}
    _x0 = _d['L0_attn_x']
    _d['L0_attn_x'] = jax.random.normal(jax.random.fold_in(jax.random.key(seed), 1), (4, 512, 512), dtype=_x0.dtype)
    del _x0
    return _d

def reference(L0_attn_x, L0_attn_attn_qkvw, L0_attn_attn_qkvb, L0_attn_attn_ow, L0_attn_attn_ob, L0_ffn_q_scales, L0_ffn_q_vals, L0_ffn_bias, L1_attn_wq, L1_attn_wk, L1_attn_wv, L1_attn_wo, L1_ffn_k0, L1_ffn_s0, L1_ffn_k1, L1_ffn_s1, L1_ffn_k2, L1_ffn_s2):

    def _L0_attn_ref(x, attn_qkvw, attn_qkvb, attn_ow, attn_ob):
        import jax, jax.numpy as jnp
        import numpy as np
        HEADS = 32
        B, S, H = x.shape
        hd = H // HEADS
        scale = 1.0 / np.sqrt(hd)
        qkv = x @ attn_qkvw + attn_qkvb
        qkv = qkv.reshape(B, S, 3, HEADS, hd)
        q = jnp.transpose(qkv[:, :, 0], (0, 2, 1, 3))
        k = jnp.transpose(qkv[:, :, 1], (0, 2, 1, 3))
        v = jnp.transpose(qkv[:, :, 2], (0, 2, 1, 3))
        scores = jnp.einsum('bhqd,bhkd->bhqk', q, k) * scale
        probs = jax.nn.softmax(scores, axis=-1)
        ctx = jnp.einsum('bhqk,bhkd->bhqd', probs, v)
        ctx = jnp.transpose(ctx, (0, 2, 1, 3)).reshape(B, S, H)
        return ctx @ attn_ow + attn_ob

    def _L0_ffn_ref(x, q_scales, q_vals, bias):
        import jax, jax.numpy as jnp
        import numpy as np
        BLOCK = 32

        def _dequantize(q_scales, q_vals):
            OUT, n_blocks = q_scales.shape
            codes = q_vals.astype(jnp.float32) - 128.0
            w = q_scales[:, :, None] * codes
            return w.reshape(OUT, n_blocks * BLOCK)
        W = _dequantize(q_scales, q_vals)
        out = jnp.einsum('bsi,oi->bso', x, W) + bias
        return out

    def _L1_attn_ref(x, wq, wk, wv, wo):
        import jax, jax.numpy as jnp
        import numpy as np
        NEG_INF = -1e+30

        def rotary_pos_emb(x):
            B, T, H, D = x.shape
            exponents = (jnp.arange(0, D, 2)[:D // 2] // D).astype(jnp.float32)
            freqs = 1.0 / jnp.power(jnp.float32(1000.0), exponents)
            theta = jnp.arange(T, dtype=jnp.float32)[:, None] * freqs[None, :]
            cos = jnp.cos(theta)[None, :, None, :]
            sin = jnp.sin(theta)[None, :, None, :]
            xr = x.astype(jnp.float32).reshape(B, T, H, D // 2, 2)
            x0, x1 = (xr[..., 0], xr[..., 1])
            out = jnp.stack([x0 * cos - x1 * sin, x0 * sin + x1 * cos], axis=-1)
            return out.reshape(B, T, H, D).astype(x.dtype)

        def attention_fwd(x, wq, wk, wv, wo, n_heads=32):
            B, T, C = x.shape
            hd = C // n_heads
            xq = (x @ wq.T).reshape(B, T, n_heads, hd)
            xk = (x @ wk.T).reshape(B, T, n_heads, hd)
            xv = (x @ wv.T).reshape(B, T, n_heads, hd)
            xq = rotary_pos_emb(xq)
            xk = rotary_pos_emb(xk)
            scale = hd ** (-0.5)
            scores = jnp.einsum('bqhd,bkhd->bhqk', xq, xk) * scale
            causal = jnp.tril(jnp.ones((T, T), dtype=bool))
            scores = jnp.where(causal[None, None], scores, NEG_INF)
            probs = jax.nn.softmax(scores.astype(jnp.float32), axis=-1).astype(xq.dtype)
            out = jnp.einsum('bhqk,bkhd->bqhd', probs, xv).reshape(B, T, C)
            return out @ wo.T
        return attention_fwd(x, wq, wk, wv, wo)

    def _L1_ffn_ref(x, k0, s0, k1, s1, k2, s2):
        import jax, jax.numpy as jnp
        import numpy as np
        import math
        D = 512
        TOKENS = (4, 256)
        P = 0.8

        def conn_dense(kernel, x):
            w = jnp.where(kernel, jnp.asarray(1.0, x.dtype), jnp.asarray(-1.0, x.dtype))
            return x @ w

        def ei_dense(x, kernel, scale, p):
            in_dim = x.shape[-1]
            ne = round(in_dim * p)
            x_exc = x[..., :ne]
            x_inh = x[..., ne:]
            xx = jnp.concatenate([x_exc, -p / (1.0 - p) * x_inh], axis=-1)
            return scale * conn_dense(kernel, xx)
        h = s0 * conn_dense(k0, x)
        h = jax.nn.relu(h) * 2.0
        h = ei_dense(h, k1, s1, P)
        h = jax.nn.relu(h) * 2.0
        return ei_dense(h, k2, s2, P)
    x = L0_attn_x
    x = x + _L0_attn_ref(_layernorm(x, axis=-1), L0_attn_attn_qkvw, L0_attn_attn_qkvb, L0_attn_attn_ow, L0_attn_attn_ob)
    x = x + _L0_ffn_ref(_layernorm(x, axis=-1), L0_ffn_q_scales, L0_ffn_q_vals, L0_ffn_bias)
    x = x + _L1_attn_ref(_layernorm(x, axis=-1), L1_attn_wq, L1_attn_wk, L1_attn_wv, L1_attn_wo)
    x = x + _L1_ffn_ref(_layernorm(x, axis=-1), L1_ffn_k0, L1_ffn_s0, L1_ffn_k1, L1_ffn_s1, L1_ffn_k2, L1_ffn_s2)
    return x

_drawn_inputs = setup_inputs


def setup_inputs(seed=0):
    import zlib

    import numpy as np

    out = dict(_drawn_inputs(seed))
    spreads = {}
    factors = {'L0_attn_attn_qkvb': 3.559,
     'L0_attn_attn_ob': 3.063,
     'L1_attn_wq': 8.0,
     'L1_attn_wk': 8.0,
     'L1_attn_wv': 8.0,
     'L1_attn_wo': 8.0}
    for name, (base, spread) in spreads.items():
        noise = np.random.default_rng([zlib.crc32(name.encode()), seed]).standard_normal(out[name].shape)
        drawn = base * np.exp(spread * noise) if base else spread * noise
        out[name] = jnp.asarray(drawn.astype(out[name].dtype))
    for name, factor in factors.items():
        out[name] = (out[name] * factor).astype(out[name].dtype)
    return out
```

```python
from contextlib import ExitStack

import numpy as np

import concourse.bass as bass
from concourse import mybir

B, T, C = 4, 512, 512
HEADS = 32
HD = C // HEADS
P = 128
KT = C // P
QT = T // P
TILES = B * QT
GROUPS = B * KT
GH = P // HD
QH = 4
PARTS = 3
NEG = -1e30
SCALE = HD ** -0.5
EPS = 1e-5
EXC = round(C * 0.8)
INH = 0.8 / (1.0 - 0.8)

Q_BLOCKS = (0, 1, 2, 0, 1, 0)
K_BLOCKS = (0, 0, 0, 1, 1, 2)
QK_ROWS = HD * len(Q_BLOCKS)
MAX_ROWS = QK_ROWS + PARTS

ALU = mybir.AluOpType
ACT = mybir.ActivationFunctionType
F32 = mybir.dt.float32
F32R = mybir.dt.float32r
BF16 = mybir.dt.bfloat16
I32 = mybir.dt.int32
U8 = mybir.dt.uint8
AX_X = mybir.AxisListType.X

IDENT, MASK_S, MASK_ST = 0, P, 2 * P
COS, SIN, NSIN = 3 * P, 3 * P + QT, 3 * P + 2 * QT
SGN_MUL, SGN_ADD = 3 * P + 3 * QT, 3 * P + 3 * QT + KT
CONSTS = 3 * P + 3 * QT + 2 * KT


def table_of_constants():
    c = np.zeros((P, CONSTS), np.float32)
    r = np.arange(P)
    c[:, IDENT:IDENT + P] = np.eye(P)
    c[:, MASK_S:MASK_S + P] = np.where(r[None, :] > r[:, None], NEG, 0.0)
    c[:, MASK_ST:MASK_ST + P] = np.where(r[:, None] > r[None, :], NEG, 0.0)
    pos = np.arange(T, dtype=np.float32).reshape(QT, P).T
    c[:, COS:COS + QT] = np.cos(pos)
    c[:, SIN:SIN + QT] = np.sin(pos)
    c[:, NSIN:NSIN + QT] = -np.sin(pos)
    w = np.where(np.arange(C) < EXC, 1.0, -INH).astype(np.float32).reshape(KT, P).T
    c[:, SGN_MUL:SGN_MUL + KT] = 2.0 * w
    c[:, SGN_ADD:SGN_ADD + KT] = -w
    return c


def wait(eng, sem, value):
    if not (isinstance(value, int) and value <= 0):
        eng.wait_ge(sem, value)


def gated_wait(dve, gate, sem, value):
    dve.wait_ge(sem, value)
    dve.memset(gate[:, :], 0.0)


class Memory:

    def __init__(self, nc, ctx, tag):
        self.nc, self.ctx, self.tag, self.sems = nc, ctx, tag, []

    def sb(self, name, shape, dt=F32):
        return self.ctx.enter_context(self.nc.sbuf_tensor(f"{self.tag}_{name}", shape, dt))

    def bank(self, name):
        return self.ctx.enter_context(self.nc.psum_tensor(f"{self.tag}_{name}", [P, 512], F32))

    def sem(self, name):
        s = self.ctx.enter_context(self.nc.semaphore(f"{self.tag}_{name}"))
        self.sems.append(s)
        return s

    def clear_sems(self):
        with self.nc.Block() as block:
            @block.sync
            def _(sp):
                for s in self.sems:
                    sp.sem_clear(s)


def three_pass(pe, out, lhs_hi, lhs_lo, rhs_hi, rhs_lo, first, last):
    pe.matmul(out, lhs_hi, rhs_hi, start=first, stop=False)
    pe.matmul(out, lhs_hi, rhs_lo, start=False, stop=False)
    return pe.matmul(out, lhs_lo, rhs_hi, start=False, stop=last)


def over_batches(eng, tile):
    for qt in range(QT):
        tile(0, qt, True, True)
    with eng.Fori(1, B - 1) as b:
        for qt in range(QT):
            tile(b, qt, True, True)
    for qt in range(QT):
        tile(B - 1, qt, qt < QT - 1, qt < QT - 2)


def pre_phase(nc, layer, io, X, V, parts_dram, const):
    rope = layer == 1
    W3 = 3 * C
    with ExitStack() as ctx:
        m = Memory(nc, ctx, f"pre{layer}")
        w_raw = m.sb("w_raw", [P, 2, W3])
        w_hi = m.sb("w_hi", [P, KT, W3], F32R)
        w_lo = m.sb("w_lo", [P, KT, W3], F32R)
        bias = None if rope else m.sb("bias", [P, W3])
        eps = m.sb("eps", [P, 1])
        gate = m.sb("gate", [P, 1])
        xn = m.sb("xn", [P, 2, C])
        xT_hi = m.sb("xT_hi", [P, 2, C], F32R)
        xT_lo = m.sb("xT_lo", [P, 2, C], F32R)
        stats = m.sb("stats", [P, 2, 6])
        mean_var = m.sb("mean_var", [P, 2, 2])
        std = m.sb("std", [P, 2, 1])
        rstd = m.sb("rstd", [P, 2, 1])
        qk = m.sb("qk", [P, 2, 2, C])
        turned = m.sb("turned", [P, 2, C])
        rest = m.sb("rest", [P, 2, C])
        parts = m.sb("parts", [P, 2, 2, PARTS, KT, 2 * P], BF16)

        xT_bank = m.bank("xT")
        out_bank = [m.bank(n) for n in ("q", "k", "v")]
        qkT_bank = [m.bank("qT"), m.bank("kT")]

        w_in = [m.sem(f"w_in{i}") for i in range(2)]
        bias_in, x_in = m.sem("bias_in"), m.sem("x_in")
        eps_set, w_hi_done, w_lo_done = m.sem("eps_set"), m.sem("w_hi_done"), m.sem("w_lo_done")
        ln_step, std_done, xn_done = m.sem("ln_step"), m.sem("std_done"), m.sem("xn_done")
        xT_done, xh_done, xl_done = m.sem("xT_done"), m.sem("xh_done"), m.sem("xl_done")
        mm_done = [m.sem(f"mm_{n}") for n in "qkv"]
        turn_done = [m.sem(f"turn_{n}") for n in "qk"]
        ev_done = [m.sem(f"evac_{n}") for n in "qkv"]
        qkT_done = [m.sem(f"{n}T_done") for n in "qk"]
        h_done = [m.sem(f"{n}h_done") for n in "qk"]
        r_done = [m.sem(f"{n}r_done") for n in "qk"]
        m_done = [m.sem(f"{n}m_done") for n in "qk"]
        l_done = [m.sem(f"{n}l_done") for n in "qk"]
        parts_out = [m.sem(f"parts_out{n}") for n in range(2)]

        x_dram = io["L0_attn_x"].rearrange("b (t p) c -> b p t c", p=P)

        def xtile(j):
            return X[:, bass.ds(j * C, C)]

        def vslice(b, kt):
            return V[:, bass.ds(b * (QT * C), QT * C)].rearrange("p (g k c) -> p g k c", g=KT, k=QT)[:, :, kt, :]

        with nc.Block() as block:

            @block.sync
            def _(sp):
                if layer == 0:
                    sp.dma_start(X[:, 0:QT * C].rearrange("p (t c) -> p t c", t=QT), x_dram[0]).then_inc(x_in, 16)
                for k in range(KT):
                    if k >= 2:
                        sp.wait_ge(w_lo_done, k - 1)
                    if rope:
                        for n, name in enumerate(("L1_attn_wq", "L1_attn_wk", "L1_attn_wv")):
                            sp.dma_start(w_raw[:, k % 2, n * C:(n + 1) * C], io[name][k * P:(k + 1) * P, :])\
                              .then_inc(w_in[k % 2], 16)
                    else:
                        sp.dma_start(w_raw[:, k % 2, :], io["L0_attn_attn_qkvw"][k * P:(k + 1) * P, :])\
                          .then_inc(w_in[k % 2], 16)
                if not rope:
                    sp.dma_start(bias[:, :], io["L0_attn_attn_qkvb"].to_broadcast([P, W3])).then_inc(bias_in, 16)
                    for b in range(1, B):
                        sp.wait_ge(x_in, 16 * b)
                        sp.dma_start(X[:, b * QT * C:(b + 1) * QT * C].rearrange("p (t c) -> p t c", t=QT),
                                     x_dram[b]).then_inc(x_in, 16)
                with sp.Fori(0, B) as b:
                    for pair in range(2):
                        for n in range(2):
                            sp.wait_ge(l_done[n], 4 * b + 2 * pair + 2)
                            for part in range(PARTS):
                                dst = parts_dram[bass.ds(4 * b, KT), n, part, :, pair * 256:pair * 256 + 256]
                                sp.dma_start(dst.rearrange("g p t -> p g t"), parts[:, pair, n, part, :, :])\
                                  .then_inc(parts_out[pair], 16)
                for pair in range(2):
                    sp.wait_ge(parts_out[pair], B * 96)

            @block.scalar
            def _(act):

                def ln_std(j, par):
                    act.wait_ge(ln_step, 3 * j + 2)
                    act.activation(std[:, par, :], mean_var[:, par, 1:2], ACT.Sqrt, bias=eps[:, 0:1])\
                       .then_inc(std_done, 1)

                def x_high(j, par):
                    act.wait_ge(xT_done, j + 1)
                    act.activation(xT_hi[:, par, :], xT_bank[:, :], ACT.Copy).then_inc(xh_done, 1)

                def tile(b, kt, xt, ln):
                    j = 4 * b + kt
                    if xt:
                        x_high(j + 1, (kt + 1) % 2)
                    if rope:
                        for n in range(2):
                            act.wait_ge(mm_done[n], j + 1)
                            act.activation(turned[:, n, :], out_bank[n][:, :], ACT.Copy,
                                           scale=const[:, COS + kt:COS + kt + 1]).then_inc(turn_done[n], 1)
                    if ln:
                        ln_std(j + 2, kt % 2)
                    if rope:
                        act.wait_ge(mm_done[2], j + 1)
                        act.activation(vslice(b, kt), out_bank[2][:, :].rearrange("p (g c) -> p g c", g=KT), ACT.Copy)\
                           .then_inc(ev_done[2], 1)
                    pair, at = kt // 2, kt % 2 * P
                    for n in range(2):
                        act.wait_ge(qkT_done[n], j + 1)
                        if kt % 2 == 0:
                            wait(act, parts_out[pair], 96 * b)
                        act.activation(parts[:, pair, n, 0, :, at:at + P],
                                       qkT_bank[n][:, :].rearrange("p (g t) -> p g t", g=KT), ACT.Copy)\
                           .then_inc(h_done[n], 1)
                        act.wait_ge(r_done[n], j + 1)
                        act.activation(parts[:, pair, n, 1, :, at:at + P],
                                       rest[:, n, :].rearrange("p (g t) -> p g t", g=KT), ACT.Copy)\
                           .then_inc(m_done[n], 1)

                act.wait_ge(eps_set, 1)
                ln_std(0, 0)
                ln_std(1, 1)
                for k in range(KT):
                    act.wait_ge(w_in[k % 2], (48 if rope else 16) * (k // 2 + 1))
                    act.activation(w_hi[:, k, :], w_raw[:, k % 2, :], ACT.Copy).then_inc(w_hi_done, 1)
                x_high(0, 0)
                over_batches(act, tile)

            @block.vector
            def _(dve):
                dve.memset(eps[:, :], EPS).then_inc(eps_set, 1)

                def ln(j, par, batch):
                    if layer == 0:
                        gated_wait(dve, gate, x_in, 16 * (batch + 1))
                    dve.bn_stats(stats[:, par, :], xtile(j)).then_inc(ln_step, 1)
                    gated_wait(dve, gate, ln_step, 3 * j + 1)
                    dve.bn_aggr(mean_var[:, par, :], stats[:, par, :]).then_inc(ln_step, 1)
                    dve.wait_ge(std_done, j + 1)
                    dve.reciprocal(rstd[:, par, :], std[:, par, :]).then_inc(ln_step, 1)
                    dve.wait_ge(ln_step, 3 * j + 3)
                    wait(dve, xT_done, j - 1)
                    dve.tensor_scalar(xn[:, par, :], xtile(j), mean_var[:, par, 0:1], rstd[:, par, 0:1],
                                      ALU.subtract, ALU.mult).then_inc(xn_done, 1)

                def x_low(j, par):
                    dve.wait_ge(xh_done, j + 1)
                    dve.tensor_tensor(xT_lo[:, par, :], xT_bank[:, :], xT_hi[:, par, :], ALU.subtract)\
                       .then_inc(xl_done, 1)

                def evacuate(b, kt, n):
                    j = 4 * b + kt
                    par = kt % 2
                    dve.wait_ge(mm_done[n], j + 1)
                    if n == 2:
                        dve.tensor_tensor(vslice(b, kt), out_bank[2][:, :].rearrange("p (g c) -> p g c", g=KT),
                                          bias[:, 2 * C:3 * C].rearrange("p (g c) -> p g c", g=KT), ALU.add)\
                           .then_inc(ev_done[2], 1)
                    elif not rope:
                        dve.tensor_tensor(qk[:, n, par, :], out_bank[n][:, :], bias[:, n * C:(n + 1) * C], ALU.add)\
                           .then_inc(ev_done[n], 1)
                    else:
                        dve.wait_ge(turn_done[n], j + 1)
                        x = out_bank[n][:, :].rearrange("p (i e) -> p e i", e=2)
                        t = turned[:, n, :].rearrange("p (i e) -> p e i", e=2)
                        o = qk[:, n, par, :].rearrange("p (i e) -> p e i", e=2)
                        dve.scalar_tensor_tensor(o[:, 0, :], x[:, 1, :], const[:, NSIN + kt:NSIN + kt + 1],
                                                 t[:, 0, :], ALU.mult, ALU.add)
                        dve.scalar_tensor_tensor(o[:, 1, :], x[:, 0, :], const[:, SIN + kt:SIN + kt + 1],
                                                 t[:, 1, :], ALU.mult, ALU.add).then_inc(ev_done[n], 1)

                def split(b, kt, n):
                    j = 4 * b + kt
                    pair, at = kt // 2, kt % 2 * P
                    piece = rest[:, n, :].rearrange("p (g t) -> p g t", g=KT)
                    dve.wait_ge(h_done[n], j + 1)
                    dve.tensor_tensor(piece, qkT_bank[n][:, :].rearrange("p (g t) -> p g t", g=KT),
                                      parts[:, pair, n, 0, :, at:at + P], ALU.subtract).then_inc(r_done[n], 1)
                    dve.wait_ge(m_done[n], j + 1)
                    dve.tensor_tensor(parts[:, pair, n, 2, :, at:at + P], piece,
                                      parts[:, pair, n, 1, :, at:at + P], ALU.subtract).then_inc(l_done[n], 1)

                def tile(b, kt, next_x, next_ln):
                    j = 4 * b + kt
                    if next_x:
                        x_low(j + 1, (kt + 1) % 2)
                    evacuate(b, kt, 0)
                    evacuate(b, kt, 1)
                    if next_ln:
                        ln(j + 2, kt % 2, b + (kt + 2) // 4)
                    if not rope:
                        evacuate(b, kt, 2)
                    split(b, kt, 0)
                    split(b, kt, 1)

                ln(0, 0, 0)
                ln(1, 1, 0)
                for k in range(KT):
                    dve.wait_ge(w_hi_done, k + 1)
                    dve.tensor_tensor(w_lo[:, k, :], w_raw[:, k % 2, :], w_hi[:, k, :], ALU.subtract)\
                       .then_inc(w_lo_done, 1)
                x_low(0, 0)
                if not rope:
                    dve.wait_ge(bias_in, 16)
                over_batches(dve, tile)

            @block.tensor
            def _(pe):
                ident = const[:, IDENT:IDENT + P]

                def x_transpose(j, par):
                    pe.wait_ge(xn_done, j + 1)
                    wait(pe, xl_done, j)
                    for k in range(KT):
                        t = pe.transpose(xT_bank[:, k * P:(k + 1) * P], xn[:, par, k * P:(k + 1) * P], ident)
                    t.then_inc(xT_done, 1)

                def project(j, par, n):
                    wait(pe, ev_done[n], j)
                    for k in range(KT):
                        mm = three_pass(pe, out_bank[n][:, :], xT_hi[:, par, k * P:(k + 1) * P],
                                        xT_lo[:, par, k * P:(k + 1) * P], w_hi[:, k, n * C:(n + 1) * C],
                                        w_lo[:, k, n * C:(n + 1) * C], k == 0, k == KT - 1)
                    mm.then_inc(mm_done[n], 1)

                def qk_transpose(j, par, n):
                    pe.wait_ge(ev_done[n], j + 1)
                    wait(pe, r_done[n], j)
                    for g in range(KT):
                        t = pe.transpose(qkT_bank[n][:, g * P:(g + 1) * P], qk[:, n, par, g * P:(g + 1) * P], ident)
                    t.then_inc(qkT_done[n], 1)

                def tile(b, kt, next_x, _):
                    j, par = 4 * b + kt, kt % 2
                    if next_x:
                        x_transpose(j + 1, 1 - par)
                    pe.wait_ge(xl_done, j + 1)
                    project(j, par, 0)
                    project(j, par, 1)
                    qk_transpose(j, par, 0)
                    project(j, par, 2)
                    qk_transpose(j, par, 1)

                x_transpose(0, 0)
                pe.wait_ge(w_lo_done, KT)
                over_batches(pe, tile)

        m.clear_sems()


def attention_phase(nc, layer, heads, parts_dram, const):
    causal = layer == 1
    STEPS = 2 * QT
    SPAN = 1 if causal else 2
    with ExitStack() as stack:
        m = Memory(nc, stack, f"att{layer}")
        q_rows = m.sb("q_rows", [P, 4, QH, T], BF16)
        k_rows = m.sb("k_rows", [P, 4, QH, T], BF16)
        v_group = m.sb("v_group", [P, 2, QT, GH, 2 * HD])
        probs = m.sb("probs", [P, 2, QH, T])
        row_max = m.sb("row_max", [P, 2, QT, QH])
        max_rest = m.sb("max_rest", [P, QT, QH])
        zeros = m.sb("zeros", [P, QT, QH])
        max_parts = m.sb("max_parts", [P, QT, PARTS, QH], BF16)
        max_rows = m.sb("max_rows", [PARTS * QH, 2, T], BF16)
        sums = m.sb("sums", [P, QT, QH])
        o_rows = m.sb("o_rows", [P, T])
        identb = m.sb("identb", [P, P], BF16)
        maskb = m.sb("maskb", [P, 2, P], BF16)

        s_banks = stack.enter_context(nc.psum_tensor(f"att{layer}_s", [P, QT, 512], F32))
        st_bank = [m.bank(f"st{i}") for i in range(2)]
        o_bank = m.bank("o")
        t_bank = m.bank("t")
        t_half = t_bank[:, :].bitcast(BF16)

        consts_set, ones_set = m.sem("consts_set"), m.sem("ones_set")
        qk_in = [m.sem(f"qk_in{i}") for i in range(4)]
        s_tile, s_max = m.sem("s_tile"), m.sem("s_max")
        part_step, parts_ready, maxT_done = m.sem("part_step"), m.sem("parts_ready"), m.sem("maxT_done")
        max_copied = m.sem("max_copied")
        max_in = [m.sem(f"max_in{i}") for i in range(2)]
        st_tile, exp_done, pv_done = m.sem("st_tile"), m.sem("exp_done"), m.sem("pv_done")
        v_ready, o_copied, oT_done = m.sem("v_ready"), m.sem("o_copied"), m.sem("oT_done")
        sums_done, ctx_done = m.sem("sums_done"), m.sem("ctx_done")
        QK_DMAS = 2 * len(Q_BLOCKS)

        def loads(t, par):
            return 8 * QK_DMAS * (t - par) + 16 * QK_DMAS

        with nc.Block() as block:

            def over_groups(eng, group, head, tail):
                for t in range(head):
                    group(t, t % 2)
                pairs = (GROUPS - head - tail) // 2
                with eng.Fori(0, pairs) as i:
                    group(2 * i + head, head % 2)
                    group(2 * i + head + 1, (head + 1) % 2)
                for t in range(head + 2 * pairs, GROUPS):
                    group(t, t % 2)

            @block.sync
            def _(sp):
                def load(t, par, quad):
                    buf = 2 * par + quad
                    for rows, n, blocks in ((q_rows, 0, Q_BLOCKS), (k_rows, 1, K_BLOCKS)):
                        for i, part in enumerate(blocks):
                            src = parts_dram[bass.ds(t, 1), n, part, quad * 64:quad * 64 + 64, :]
                            sp.dma_start(rows[i * HD:(i + 1) * HD, buf, :, :],
                                         src.rearrange("o (h d) t -> d (o h) t", d=HD)).then_inc(qk_in[buf], 16)

                def place_max(v, par, quad):
                    sp.wait_ge(max_copied, v + 1)
                    for part in range(PARTS):
                        sp.dma_start(q_rows[QK_ROWS + part:QK_ROWS + part + 1, 2 * par + quad, :, :],
                                     max_rows[part * QH:(part + 1) * QH, quad, :]).then_inc(max_in[quad], 16)

                def group(t, par):
                    static = isinstance(t, int)
                    place_max(2 * t + 1, par, 1)
                    if not static or t + 2 < GROUPS:
                        sp.wait_ge(st_tile, 16 * (2 * t + 1))
                        load(t + 2, par, 0)
                    if not static or t + 1 < GROUPS:
                        place_max(2 * t + 2, 1 - par, 0)
                    if not static or t + 2 < GROUPS:
                        sp.wait_ge(st_tile, 16 * (2 * t + 2))
                        load(t + 2, par, 1)

                for t in range(2):
                    for quad in range(2):
                        load(t, t, quad)
                place_max(0, 0, 0)
                over_groups(sp, group, 1, 3)

            @block.gpsimd
            def _(pool):
                for par in range(2):
                    pool.memset(v_group[:, par, :, :, :], 1.0).then_inc(ones_set, 1)
                for buf in range(4):
                    pool.wait_ge(ones_set, 2 + buf)
                    pool.memset(k_rows[QK_ROWS:MAX_ROWS, buf, :, :], -1.0).then_inc(ones_set, 1)
                pool.wait_ge(ones_set, 6)
                pool.memset(zeros[:, :, :], 0.0).then_inc(ones_set, 1)
                pool.wait_ge(ones_set, 7)

                def max_split(v, quad):
                    pool.wait_ge(s_max, 16 * (v + 1))
                    wait(pool, maxT_done, v)
                    pool.tensor_tensor(max_parts[:, :, 0, :], row_max[:, quad, :, :], zeros[:, :, :], ALU.add)\
                        .then_inc(part_step, 1)
                    pool.wait_ge(part_step, 3 * v + 1)
                    pool.tensor_tensor(max_rest[:, :, :], row_max[:, quad, :, :], max_parts[:, :, 0, :], ALU.subtract)\
                        .then_inc(part_step, 1)
                    pool.wait_ge(part_step, 3 * v + 2)
                    pool.tensor_tensor(max_parts[:, :, 1, :], max_rest[:, :, :], zeros[:, :, :], ALU.add)\
                        .then_inc(part_step, 1)
                    pool.wait_ge(part_step, 3 * v + 3)
                    pool.tensor_tensor(max_parts[:, :, 2, :], max_rest[:, :, :], max_parts[:, :, 1, :], ALU.subtract)\
                        .then_inc(parts_ready, 1)

                def group(t, par):
                    wait(pool, pv_done, STEPS * (t - 1))
                    src = heads[:, bass.ds(t * C, C)].rearrange("p (k h d) -> p k h d", k=QT, h=GH)
                    for k in range(QT):
                        copy = pool.tensor_copy(v_group[:, par, k, :, 0:HD], src[:, k, :, :])
                    copy.then_inc(v_ready, 1)
                    if not isinstance(t, int) or t + 1 < GROUPS:
                        max_split(2 * t + 2, 0)
                        max_split(2 * t + 3, 1)

                max_split(0, 0)
                max_split(1, 1)
                over_groups(pool, group, 3, 1)

            @block.vector
            def _(dve):
                dve.tensor_copy(identb[:, :], const[:, IDENT:IDENT + P]).then_inc(consts_set, 1)
                dve.tensor_copy(maskb[:, :, :], const[:, MASK_S:MASK_S + 2 * P].rearrange("p (a c) -> p a c", a=2))\
                   .then_inc(consts_set, 1)

                def head_max(v, quad, h):
                    for qt in range(0, QT, SPAN):
                        n = (qt + 1) * P if causal else T
                        dve.wait_ge(s_tile, 16 * v + 4 * h + qt + SPAN)
                        dve.reduce_max(row_max[:, quad, qt:qt + SPAN, h:h + 1], s_banks[:, qt:qt + SPAN, 0:n], AX_X)\
                           .then_inc(s_max, SPAN)

                def normalize(v, t, quad):
                    dve.wait_ge(oT_done, v + 1)
                    o = t_bank[:, :].rearrange("p (q h d) -> p q h d", q=QT, h=QH)
                    dve.reciprocal(sums[:, :, :], o[:, :, :, HD]).then_inc(sums_done, 1)
                    dve.wait_ge(sums_done, v + 1)
                    dst = heads[:, bass.ds(t * C, C)].rearrange("p (q c) -> p q c", q=QT)
                    dst = dst[:, :, quad * 64:quad * 64 + 64].rearrange("p q (h d) -> p q h d", h=QH)
                    inv = sums[:, :, :].unsqueeze(3).to_broadcast([P, QT, QH, HD])
                    dve.tensor_tensor(dst, o[:, :, :, 0:HD], inv, ALU.mult).then_inc(ctx_done, 1)

                def group(t, par):
                    static = isinstance(t, int)
                    for s in range(STEPS):
                        if not static or t + 1 < GROUPS:
                            head_max(2 * t + 2 + s // QH, s // QH, s % QH)
                        if s == 2 and not (static and t == 0):
                            normalize(2 * t - 1, t - 1, 1)
                        if s == 6:
                            normalize(2 * t, t, 0)

                for s in range(STEPS):
                    head_max(s // QH, s // QH, s % QH)
                over_groups(dve, group, 1, 1)
                normalize(2 * GROUPS - 1, GROUPS - 1, 1)

            @block.scalar
            def _(act):
                def copy_max(v, quad):
                    act.wait_ge(maxT_done, v + 1)
                    act.activation(max_rows[:, quad, :], t_half[0:PARTS * QH, 0:T], ACT.Copy).then_inc(max_copied, 1)

                def copy_out(v, step):
                    act.wait_ge(pv_done, step + 1)
                    act.activation(o_rows[:, :], o_bank[:, :], ACT.Copy).then_inc(o_copied, 1)

                def group(t, par):
                    first = isinstance(t, int) and t == 0
                    last = isinstance(t, int) and t + 1 == GROUPS
                    for s in range(STEPS):
                        k = s % QT
                        q0 = k * P if causal else 0
                        for h in range(QH):
                            act.wait_ge(st_tile, 4 * STEPS * t + 4 * s + h + 1)
                            act.activation(probs[:, s % 2, h, q0:T], st_bank[h % 2][:, q0:T], ACT.Exp, scale=SCALE)\
                               .then_inc(exp_done, 1)
                            if s == 1 and h == 0 and not first:
                                copy_out(2 * t - 1, STEPS * t - 1)
                            if s == 2 and h == 0:
                                copy_max(2 * t + 1, 1)
                            if s == 5 and h == 0:
                                copy_out(2 * t, STEPS * t + 3)
                            if s == 6 and h == 0 and not last:
                                copy_max(2 * t + 2, 0)

                copy_max(0, 0)
                over_groups(act, group, 1, 1)
                copy_out(2 * GROUPS - 1, STEPS * GROUPS - 1)

            @block.tensor
            def _(pe):
                pe.wait_ge(consts_set, 2)
                pe.wait_ge(ones_set, 6)

                def score_tile(v, buf, h, qt):
                    n = (qt + 1) * P if causal else T
                    wait(pe, s_max, 16 * v + 4 * h + qt - qt % SPAN + SPAN - QT)
                    mm = pe.matmul(s_banks[:, qt, 0:n], q_rows[0:QK_ROWS, buf, h, qt * P:(qt + 1) * P],
                                   k_rows[0:QK_ROWS, buf, h, 0:n], start=True, stop=not causal)
                    if causal:
                        mm = pe.matmul(s_banks[:, qt, n - P:n], identb[:, :], maskb[:, 0, :], start=False, stop=True)
                    mm.then_inc(s_tile, 1)

                def shifted_tile(t, s, buf, h):
                    k = s % QT
                    q0 = k * P if causal else 0
                    wait(pe, exp_done, 4 * STEPS * t + 4 * s + h - 1)
                    mm = pe.matmul(st_bank[h % 2][:, q0:T], k_rows[0:MAX_ROWS, buf, h, k * P:(k + 1) * P],
                                   q_rows[0:MAX_ROWS, buf, h, q0:T], start=True, stop=not causal)
                    if causal:
                        mm = pe.matmul(st_bank[h % 2][:, q0:q0 + P], identb[:, :], maskb[:, 1, :], start=False, stop=True)
                    mm.then_inc(st_tile, 1)

                def weigh(t, par, s):
                    k = s % QT
                    q0 = k * P if causal else 0
                    step = STEPS * t + s
                    if k == 0:
                        wait(pe, o_copied, 2 * t + s // QT)
                        pe.wait_ge(v_ready, t + 1)
                    pe.wait_ge(exp_done, 4 * step + 4)
                    for h in range(QH):
                        mm = pe.matmul(o_bank[32 * h:32 * h + 32, q0:T], v_group[:, par, k, s // QT * QH + h, :],
                                       probs[:, s % 2, h, q0:T], start=(k == 0), stop=(k == QT - 1))
                    mm.then_inc(pv_done, 1)

                def max_transpose(v):
                    pe.wait_ge(parts_ready, v + 1)
                    wait(pe, max_copied, v)
                    wait(pe, ctx_done, v - 2)
                    for qt in range(QT):
                        t = pe.transpose(t_half[0:PARTS * QH, qt * P:(qt + 1) * P],
                                         max_parts[:, qt, :, :], identb[:, :])
                    t.then_inc(maxT_done, 1)

                def out_transpose(v, maxima):
                    pe.wait_ge(o_copied, v + 1)
                    pe.wait_ge(max_copied, maxima)
                    wait(pe, ctx_done, v)
                    for qt in range(QT):
                        t = pe.transpose(t_bank[:, qt * P:(qt + 1) * P], o_rows[:, qt * P:(qt + 1) * P],
                                         const[:, IDENT:IDENT + P])
                    t.then_inc(oT_done, 1)

                def group(t, par):
                    first = isinstance(t, int) and t == 0
                    last = isinstance(t, int) and t + 1 == GROUPS
                    for s in range(STEPS):
                        quad = s // QT
                        if s % QT == 0:
                            if not last:
                                pe.wait_ge(qk_in[2 * (1 - par) + quad], loads(t + 1, 1 - par))
                            pe.wait_ge(max_in[quad], 16 * PARTS * (t + 1))
                        shifted_tile(t, s, 2 * par + quad, 0)
                        shifted_tile(t, s, 2 * par + quad, 1)
                        if not last:
                            for r in range(QT):
                                score_tile(2 * t + 2 + quad, 2 * (1 - par) + quad, s % QT, r)
                        shifted_tile(t, s, 2 * par + quad, 2)
                        shifted_tile(t, s, 2 * par + quad, 3)
                        if s > 0:
                            weigh(t, par, s - 1)
                        elif not first:
                            weigh(t - 1, 1 - par, STEPS - 1)
                        if s == 1:
                            max_transpose(2 * t + 1)
                        if s == 2 and not first:
                            out_transpose(2 * t - 1, 2 * t + 2)
                        if s == 5 and not last:
                            max_transpose(2 * t + 2)
                        if s == 6:
                            out_transpose(2 * t, 2 * t + 2 if last else 2 * t + 3)

                for quad in range(2):
                    pe.wait_ge(qk_in[quad], loads(0, 0))
                    for h in range(QH):
                        for qt in range(QT):
                            score_tile(quad, quad, h, qt)
                max_transpose(0)
                over_groups(pe, group, 1, 1)
                weigh(GROUPS - 1, 1, STEPS - 1)
                out_transpose(2 * GROUPS - 1, 2 * GROUPS)

        m.clear_sems()


def fetch_outputs(sp, heads, a_tile, b, qt, a_in, aT_done):
    j = QT * b + qt
    wait(sp, aT_done, j - 1)
    src = heads[:, bass.ds(b * (QT * C), QT * C)].rearrange("p (g q c) -> p g q c", g=KT, q=QT)[:, :, qt, :]
    sp.dma_start(a_tile[:, qt % 2, :].rearrange("p (g c) -> p g c", g=KT), src).then_inc(a_in[qt % 2], 16)


def outputs_in(b, qt):
    return 16 * (b * (QT // 2) + qt // 2 + 1)


def low_part(dve, out, bank, high):
    return dve.tensor_tensor(out, bank, high, ALU.subtract)


def post0_phase(nc, io, X, heads, const):
    with ExitStack() as stack:
        m = Memory(nc, stack, "post0")
        wo_raw = m.sb("wo_raw", [P, KT, C])
        codes = m.sb("codes", [P, KT, C], I32)
        scales = m.sb("scales", [P, KT, C])
        wf_raw = m.sb("wf_raw", [P, KT, C])
        w_hi = m.sb("w_hi", [P, 2, KT, C], F32R)
        w_lo = m.sb("w_lo", [P, 2, KT, C], F32R)
        bias = m.sb("bias", [P, 2, C])
        eps = m.sb("eps", [P, 1])
        gate = m.sb("gate", [P, 1])
        a_tile = m.sb("a_tile", [P, 2, C])
        aT_hi = m.sb("aT_hi", [P, 2, C], F32R)
        aT_lo = m.sb("aT_lo", [P, 2, C], F32R)
        xT_hi = m.sb("xT_hi", [P, 2, C], F32R)
        xT_lo = m.sb("xT_lo", [P, 2, C], F32R)
        xn = m.sb("xn", [P, 2, C])
        stats = m.sb("stats", [P, 6])
        mean_var = m.sb("mean_var", [P, 2])
        std = m.sb("std", [P, 1])
        rstd = m.sb("rstd", [P, 1])

        aT_bank, xT_bank = m.bank("aT"), m.bank("xT")
        o_bank = [m.bank(f"o{i}") for i in range(2)]
        f_bank = [m.bank(f"f{i}") for i in range(2)]

        w_in = [m.sem(f"w_in{i}") for i in range(2)]
        bias_in, eps_set, dequant = m.sem("bias_in"), m.sem("eps_set"), m.sem("dequant")
        w_hi_done, w_lo_done = m.sem("w_hi_done"), m.sem("w_lo_done")
        a_in = [m.sem(f"a_in{i}") for i in range(2)]
        aT_done, ah_done, al_done = m.sem("aT_done"), m.sem("ah_done"), m.sem("al_done")
        xT_done, xh_done, xl_done = m.sem("xT_done"), m.sem("xh_done"), m.sem("xl_done")
        o_done, f_done = m.sem("o_done"), m.sem("f_done")
        add_step, ln_step, std_done, xn_done = m.sem("add_step"), m.sem("ln_step"), m.sem("std_done"), m.sem("xn_done")
        o_read, f_read, x_final = m.sem("o_read"), m.sem("f_read"), m.sem("x_final")

        def xtile(j):
            return X[:, bass.ds(j * C, C)]

        with nc.Block() as block:

            @block.sync
            def _(sp):
                fetch_outputs(sp, heads, a_tile, 0, 0, a_in, aT_done)
                fetch_outputs(sp, heads, a_tile, 0, 1, a_in, aT_done)
                sp.dma_start(wo_raw[:, :, :], io["L0_attn_attn_ow"].rearrange("(k p) n -> p k n", p=P)).then_inc(w_in[0], 16)
                sp.dma_start(codes[:, :, :], io["L0_ffn_q_vals"].rearrange("(k p) n -> p k n", p=P)).then_inc(w_in[1], 16)
                for k in range(KT):
                    for s in range(4):
                        sp.dma_start(scales[32 * s:32 * s + 32, k, :],
                                     io["L0_ffn_q_scales"][4 * k + s:4 * k + s + 1, :].to_broadcast([32, C]))\
                          .then_inc(w_in[1], 16)
                sp.dma_start(bias[:, 0, :], io["L0_attn_attn_ob"].to_broadcast([P, C])).then_inc(bias_in, 16)
                sp.dma_start(bias[:, 1, :], io["L0_ffn_bias"].to_broadcast([P, C])).then_inc(bias_in, 16)

                def tile(b, qt, one, two):
                    if two:
                        fetch_outputs(sp, heads, a_tile, b + (qt + 2) // QT, (qt + 2) % QT, a_in, aT_done)

                over_batches(sp, tile)

            @block.scalar
            def _(act):
                def high(out, bank, ready, j, done):
                    act.wait_ge(ready, j + 1)
                    act.activation(out, bank, ACT.Copy).then_inc(done, 1)

                def ln_std(j):
                    act.wait_ge(ln_step, 3 * j + 2)
                    act.activation(std[:, :], mean_var[:, 1:2], ACT.Sqrt, bias=eps[:, 0:1]).then_inc(std_done, 1)

                def tile(b, qt, one, two):
                    j, par = QT * b + qt, qt % 2
                    high(xT_hi[:, par, :], xT_bank[:, :], xT_done, j, xh_done)
                    if two:
                        high(aT_hi[:, par, :], aT_bank[:, :], aT_done, j + 2, ah_done)
                    if one:
                        ln_std(j + 1)

                act.wait_ge(w_in[0], 16)
                act.activation(w_hi[:, 0, :, :], wo_raw[:, :, :], ACT.Copy).then_inc(w_hi_done, 1)
                act.wait_ge(eps_set, 1)
                high(aT_hi[:, 0, :], aT_bank[:, :], aT_done, 0, ah_done)
                high(aT_hi[:, 1, :], aT_bank[:, :], aT_done, 1, ah_done)
                act.wait_ge(dequant, 2)
                act.activation(w_hi[:, 1, :, :], wf_raw[:, :, :], ACT.Copy).then_inc(w_hi_done, 1)
                ln_std(0)
                over_batches(act, tile)

            @block.vector
            def _(dve):
                dve.memset(eps[:, :], EPS).then_inc(eps_set, 1)

                def low(out, bank, hi, ready, j, done):
                    dve.wait_ge(ready, j + 1)
                    low_part(dve, out, bank, hi).then_inc(done, 1)

                def attended(j, par):
                    dve.wait_ge(o_done, j + 1)
                    dve.tensor_tensor(xtile(j), o_bank[par][:, :], xtile(j), ALU.add).then_inc(o_read, 1)
                    dve.wait_ge(o_read, j + 1)
                    dve.tensor_tensor(xtile(j), xtile(j), bias[:, 0, :], ALU.add).then_inc(add_step, 1)
                    gated_wait(dve, gate, add_step, j + 1)
                    dve.bn_stats(stats[:, :], xtile(j)).then_inc(ln_step, 1)
                    gated_wait(dve, gate, ln_step, 3 * j + 1)
                    dve.bn_aggr(mean_var[:, :], stats[:, :]).then_inc(ln_step, 1)
                    dve.wait_ge(std_done, j + 1)
                    dve.reciprocal(rstd[:, :], std[:, :]).then_inc(ln_step, 1)
                    dve.wait_ge(ln_step, 3 * j + 3)
                    wait(dve, xT_done, j - 1)
                    dve.tensor_scalar(xn[:, par, :], xtile(j), mean_var[:, 0:1], rstd[:, 0:1],
                                      ALU.subtract, ALU.mult).then_inc(xn_done, 1)

                def final(j, par):
                    dve.wait_ge(f_done, j + 1)
                    dve.tensor_tensor(xtile(j), f_bank[par][:, :], xtile(j), ALU.add).then_inc(f_read, 1)
                    dve.wait_ge(f_read, j + 1)
                    dve.tensor_tensor(xtile(j), xtile(j), bias[:, 1, :], ALU.add).then_inc(x_final, 1)

                def tile(b, qt, one, two):
                    j, par = QT * b + qt, qt % 2
                    low(xT_lo[:, par, :], xT_bank[:, :], xT_hi[:, par, :], xh_done, j, xl_done)
                    if one:
                        attended(j + 1, 1 - par)
                    if two:
                        low(aT_lo[:, par, :], aT_bank[:, :], aT_hi[:, par, :], ah_done, j + 2, al_done)
                    final(j, par)

                low(aT_lo[:, 0, :], aT_bank[:, :], aT_hi[:, 0, :], ah_done, 0, al_done)
                dve.wait_ge(w_hi_done, 1)
                low_part(dve, w_lo[:, 0, :, :], wo_raw[:, :, :], w_hi[:, 0, :, :]).then_inc(w_lo_done, 1)
                low(aT_lo[:, 1, :], aT_bank[:, :], aT_hi[:, 1, :], ah_done, 1, al_done)
                dve.wait_ge(w_in[1], 16 * 17)
                dve.tensor_scalar(wf_raw[:, :, :], codes[:, :, :], -128.0, None, ALU.add).then_inc(dequant, 1)
                dve.wait_ge(dequant, 1)
                dve.tensor_tensor(wf_raw[:, :, :], wf_raw[:, :, :], scales[:, :, :], ALU.mult).then_inc(dequant, 1)
                dve.wait_ge(w_hi_done, 2)
                low_part(dve, w_lo[:, 1, :, :], wf_raw[:, :, :], w_hi[:, 1, :, :]).then_inc(w_lo_done, 1)
                dve.wait_ge(bias_in, 32)
                attended(0, 0)
                over_batches(dve, tile)

            @block.tensor
            def _(pe):
                ident = const[:, IDENT:IDENT + P]

                def a_transpose(b, qt):
                    wait(pe, al_done, QT * b + qt)
                    pe.wait_ge(a_in[qt % 2], outputs_in(b, qt))
                    for g in range(KT):
                        t = pe.transpose(aT_bank[:, g * P:(g + 1) * P], a_tile[:, qt % 2, g * P:(g + 1) * P], ident)
                    t.then_inc(aT_done, 1)

                def product(bank, hi, lo, w, done):
                    for k in range(KT):
                        mm = three_pass(pe, bank[:, :], hi[:, k * P:(k + 1) * P], lo[:, k * P:(k + 1) * P],
                                        w_hi[:, w, k, :], w_lo[:, w, k, :], k == 0, k == KT - 1)
                    mm.then_inc(done, 1)

                def attended(j, par):
                    pe.wait_ge(al_done, j + 1)
                    wait(pe, o_read, j - 1)
                    product(o_bank[par], aT_hi[:, par, :], aT_lo[:, par, :], 0, o_done)

                def tile(b, qt, one, two):
                    j, par = QT * b + qt, qt % 2
                    pe.wait_ge(xn_done, j + 1)
                    wait(pe, xl_done, j)
                    for k in range(KT):
                        t = pe.transpose(xT_bank[:, k * P:(k + 1) * P], xn[:, par, k * P:(k + 1) * P], ident)
                    t.then_inc(xT_done, 1)
                    if one:
                        attended(j + 1, 1 - par)
                    if two:
                        a_transpose(b + (qt + 2) // QT, (qt + 2) % QT)
                    pe.wait_ge(xl_done, j + 1)
                    wait(pe, f_read, j - 1)
                    product(f_bank[par], xT_hi[:, par, :], xT_lo[:, par, :], 1, f_done)

                a_transpose(0, 0)
                pe.wait_ge(w_lo_done, 1)
                attended(0, 0)
                a_transpose(0, 1)
                pe.wait_ge(w_lo_done, 2)
                over_batches(pe, tile)

        m.clear_sems()


def post1_phase(nc, io, X, heads, const, out):
    with ExitStack() as stack:
        m = Memory(nc, stack, "post1")
        wo_raw = m.sb("wo_raw", [P, KT, C])
        bits = m.sb("bits", [P, 3, KT, C], U8)
        wo_hi = m.sb("wo_hi", [P, KT, C], F32R)
        wo_lo = m.sb("wo_lo", [P, KT, C], F32R)
        signs = m.sb("signs", [P, 3, KT, C], F32R)
        s_in = m.sb("s_in", [P, 3])
        s2x = m.sb("s2x", [P, 3])
        eps = m.sb("eps", [P, 1])
        gate = m.sb("gate", [P, 1])
        a_tile = m.sb("a_tile", [P, 2, C])
        aT_hi = m.sb("aT_hi", [P, 2, C], F32R)
        aT_lo = m.sb("aT_lo", [P, 2, C], F32R)
        act_hi = m.sb("act_hi", [P, 3, KT, T], F32R)
        act_lo = m.sb("act_lo", [P, 3, KT, T], F32R)
        relu = m.sb("relu", [P, 2, T])
        xn = m.sb("xn", [P, QT, C])
        stats = m.sb("stats", [P, 6])
        mean_var = m.sb("mean_var", [P, 2])
        std = m.sb("std", [P, 1])
        rstd = m.sb("rstd", [P, 1])

        aT_bank = m.bank("aT")
        xT_bank = [m.bank(f"xT{i}") for i in range(2)]
        o_bank = [m.bank(f"o{i}") for i in range(2)]
        h_bank = [m.bank(f"h{i}") for i in range(2)]

        w_in = [m.sem(f"w_in{i}") for i in range(3)]
        eps_set, s_ready, signs_done = m.sem("eps_set"), m.sem("s_ready"), m.sem("signs_done")
        w_hi_done, w_lo_done = m.sem("w_hi_done"), m.sem("w_lo_done")
        a_in = [m.sem(f"a_in{i}") for i in range(2)]
        aT_done, ah_done, al_done = m.sem("aT_done"), m.sem("ah_done"), m.sem("al_done")
        xT_done, xh_done, xl_done = m.sem("xT_done"), m.sem("xh_done"), m.sem("xl_done")
        o_done, o_read = m.sem("o_done"), m.sem("o_read")
        ln_step, std_done, xn_done = m.sem("ln_step"), m.sem("std_done"), m.sem("xn_done")
        h_done, hh_done, relu_done, hl_done = m.sem("h_done"), m.sem("hh_done"), m.sem("relu_done"), m.sem("hl_done")
        x_final, x_out = m.sem("x_final"), m.sem("x_out")
        BANKS = 3 * QT

        def xtile(j):
            return X[:, bass.ds(j * C, C)]

        with nc.Block() as block:

            def over(eng, batch):
                batch(0, True)
                with eng.Fori(1, B - 1) as b:
                    batch(b, True)
                batch(B - 1, False)

            @block.sync
            def _(sp):
                fetch_outputs(sp, heads, a_tile, 0, 0, a_in, aT_done)
                fetch_outputs(sp, heads, a_tile, 0, 1, a_in, aT_done)
                sp.dma_start(wo_raw[:, :, :], io["L1_attn_wo"].rearrange("(k p) n -> p k n", p=P)).then_inc(w_in[0], 16)
                for n in range(3):
                    sp.dma_start(bits[:, n, :, :], io[f"L1_ffn_k{n}"].rearrange("(k p) n -> p k n", p=P))\
                      .then_inc(w_in[1], 16)
                    sp.dma_start(s_in[:, n:n + 1], io[f"L1_ffn_s{n}"].to_broadcast([P, 1])).then_inc(w_in[2], 16)

                for qt in range(2, QT):
                    fetch_outputs(sp, heads, a_tile, 0, qt, a_in, aT_done)

                def batch(b, more):
                    if more:
                        for qt in range(QT):
                            fetch_outputs(sp, heads, a_tile, b + 1, qt, a_in, aT_done)
                    sp.wait_ge(x_final, QT * b + QT)
                    sp.dma_start(out[bass.ds(b, 1)].rearrange("o (t p) c -> p (o t) c", p=P),
                                 X[:, bass.ds(b * (QT * C), QT * C)].rearrange("p (t c) -> p t c", t=QT))\
                      .then_inc(x_out, 16)

                over(sp, batch)
                sp.wait_ge(x_out, 16 * B)

            @block.scalar
            def _(act):
                def a_high(j, par):
                    act.wait_ge(aT_done, j + 1)
                    act.activation(aT_hi[:, par, :], aT_bank[:, :], ACT.Copy).then_inc(ah_done, 1)

                def ln_std(j):
                    act.wait_ge(ln_step, 3 * j + 2)
                    act.activation(std[:, :], mean_var[:, 1:2], ACT.Sqrt, bias=eps[:, 0:1]).then_inc(std_done, 1)

                def layer_high(b, n):
                    for k in range(KT):
                        act.wait_ge(h_done, BANKS * b + KT * n + k + 1)
                        act.activation(act_hi[:, n + 1, k, :], h_bank[k % 2][:, :], ACT.Relu, scale=s2x[:, n:n + 1])\
                           .then_inc(hh_done, 1)

                def turn_high(b):
                    for qt in range(QT):
                        act.wait_ge(xT_done, QT * b + qt + 1)
                        act.activation(act_hi[:, 0, :, qt * P:(qt + 1) * P],
                                       xT_bank[qt % 2][:, :].rearrange("p (k t) -> p k t", k=KT), ACT.Copy)\
                           .then_inc(xh_done, 1)

                def batch(b, more):
                    j = QT * (b + 1)
                    turn_high(b)
                    if more:
                        a_high(j, 0)
                    layer_high(b, 0)
                    if more:
                        ln_std(j)
                        a_high(j + 1, 1)
                    layer_high(b, 1)
                    if more:
                        ln_std(j + 1)
                        a_high(j + 2, 0)
                        a_high(j + 3, 1)
                        ln_std(j + 2)
                        ln_std(j + 3)

                act.wait_ge(w_in[0], 16)
                act.activation(wo_hi[:, :, :], wo_raw[:, :, :], ACT.Copy).then_inc(w_hi_done, 1)
                act.wait_ge(eps_set, 1)
                act.wait_ge(s_ready, 1)
                a_high(0, 0)
                for j in range(QT):
                    if j + 1 < QT:
                        a_high(j + 1, (j + 1) % 2)
                    ln_std(j)
                over(act, batch)

            @block.vector
            def _(dve):
                dve.memset(eps[:, :], EPS).then_inc(eps_set, 1)
                dve.wait_ge(w_in[2], 48)
                dve.tensor_scalar(s2x[:, :], s_in[:, :], 2.0, None, ALU.mult).then_inc(s_ready, 1)

                def a_low(j, par):
                    dve.wait_ge(ah_done, j + 1)
                    low_part(dve, aT_lo[:, par, :], aT_bank[:, :], aT_hi[:, par, :]).then_inc(al_done, 1)

                def attended(j, par):
                    dve.wait_ge(o_done, j + 1)
                    dve.tensor_tensor(xtile(j), o_bank[par % 2][:, :], xtile(j), ALU.add).then_inc(o_read, 1)
                    gated_wait(dve, gate, o_read, j + 1)
                    dve.bn_stats(stats[:, :], xtile(j)).then_inc(ln_step, 1)
                    gated_wait(dve, gate, ln_step, 3 * j + 1)
                    dve.bn_aggr(mean_var[:, :], stats[:, :]).then_inc(ln_step, 1)
                    dve.wait_ge(std_done, j + 1)
                    dve.reciprocal(rstd[:, :], std[:, :]).then_inc(ln_step, 1)
                    dve.wait_ge(ln_step, 3 * j + 3)
                    dve.tensor_scalar(xn[:, par, :], xtile(j), mean_var[:, 0:1], rstd[:, 0:1],
                                      ALU.subtract, ALU.mult).then_inc(xn_done, 1)

                def layer_low(b, n):
                    for k in range(KT):
                        use = 2 * KT * b + KT * n + k
                        dve.wait_ge(hh_done, use + 1)
                        dve.tensor_scalar(relu[:, k % 2, :], h_bank[k % 2][:, :], s2x[:, n:n + 1], 0.0, ALU.mult, ALU.max)\
                           .then_inc(relu_done, 1)
                        dve.wait_ge(relu_done, use + 1)
                        low_part(dve, act_lo[:, n + 1, k, :], relu[:, k % 2, :], act_hi[:, n + 1, k, :])\
                            .then_inc(hl_done, 1)

                def batch(b, more):
                    j = QT * (b + 1)
                    for qt in range(QT):
                        dve.wait_ge(xh_done, QT * b + qt + 1)
                        low_part(dve, act_lo[:, 0, :, qt * P:(qt + 1) * P],
                                 xT_bank[qt % 2][:, :].rearrange("p (k t) -> p k t", k=KT),
                                 act_hi[:, 0, :, qt * P:(qt + 1) * P]).then_inc(xl_done, 1)
                    if more:
                        a_low(j, 0)
                    layer_low(b, 0)
                    if more:
                        attended(j, 0)
                        a_low(j + 1, 1)
                    layer_low(b, 1)
                    if more:
                        attended(j + 1, 1)
                        a_low(j + 2, 0)
                    for qt in range(QT):
                        dve.wait_ge(h_done, BANKS * b + 2 * KT + qt + 1)
                        dve.scalar_tensor_tensor(xtile(QT * b + qt), h_bank[qt % 2][:, :], s_in[:, 2:3],
                                                 xtile(QT * b + qt), ALU.mult, ALU.add).then_inc(x_final, 1)
                    if more:
                        a_low(j + 3, 1)
                        attended(j + 2, 2)
                        attended(j + 3, 3)

                a_low(0, 0)
                dve.wait_ge(w_hi_done, 1)
                low_part(dve, wo_lo[:, :, :], wo_raw[:, :, :], wo_hi[:, :, :]).then_inc(w_lo_done, 1)
                dve.wait_ge(w_in[1], 48)
                for j in range(QT):
                    if j + 1 < QT:
                        a_low(j + 1, (j + 1) % 2)
                    attended(j, j)
                    if j < 3:
                        for k in range(KT):
                            mul = const[:, SGN_MUL + k:SGN_MUL + k + 1] if j else 2.0
                            add = const[:, SGN_ADD + k:SGN_ADD + k + 1] if j else -1.0
                            dve.tensor_scalar(signs[:, j, k, :], bits[:, j, k, :], mul, add, ALU.mult, ALU.add)\
                               .then_inc(signs_done, 1)
                over(dve, batch)

            @block.tensor
            def _(pe):
                ident = const[:, IDENT:IDENT + P]

                def a_transpose(b, qt):
                    wait(pe, al_done, QT * b + qt)
                    pe.wait_ge(a_in[qt % 2], outputs_in(b, qt))
                    for g in range(KT):
                        t = pe.transpose(aT_bank[:, g * P:(g + 1) * P], a_tile[:, qt % 2, g * P:(g + 1) * P], ident)
                    t.then_inc(aT_done, 1)

                def attended(j, par):
                    pe.wait_ge(al_done, j + 1)
                    wait(pe, o_read, j - 1)
                    for k in range(KT):
                        mm = three_pass(pe, o_bank[par][:, :], aT_hi[:, par, k * P:(k + 1) * P],
                                        aT_lo[:, par, k * P:(k + 1) * P], wo_hi[:, k, :], wo_lo[:, k, :],
                                        k == 0, k == KT - 1)
                    mm.then_inc(o_done, 1)

                def bank_free(b, use):
                    if use < 2:
                        wait(pe, x_final, QT * b - 1 + use)
                    elif use < 2 * KT + 2:
                        pe.wait_ge(hl_done, 2 * KT * b + use - 1)
                    else:
                        pe.wait_ge(x_final, QT * b + use - 2 * KT - 1)

                def layer(b, n):
                    for o in range(KT):
                        bank_free(b, KT * n + o)
                        for k in range(KT):
                            if n:
                                pe.wait_ge(hl_done, 2 * KT * b + KT * (n - 1) + k + 1)
                            w = signs[:, n, k, o * P:(o + 1) * P]
                            pe.matmul(h_bank[o % 2][:, :], w, act_hi[:, n, k, :], start=(k == 0), stop=False)
                            mm = pe.matmul(h_bank[o % 2][:, :], w, act_lo[:, n, k, :], start=False, stop=(k == KT - 1))
                        mm.then_inc(h_done, 1)

                def last_layer(b):
                    for qt in range(QT):
                        bank_free(b, 2 * KT + qt)
                        for k in range(KT):
                            pe.wait_ge(hl_done, 2 * KT * b + KT + k + 1)
                            w = signs[:, 2, k, :]
                            pe.matmul(h_bank[qt % 2][:, :], act_hi[:, 2, k, qt * P:(qt + 1) * P], w,
                                      start=(k == 0), stop=False)
                            mm = pe.matmul(h_bank[qt % 2][:, :], act_lo[:, 2, k, qt * P:(qt + 1) * P], w,
                                           start=False, stop=(k == KT - 1))
                        mm.then_inc(h_done, 1)

                def turn(b):
                    for qt in range(QT):
                        pe.wait_ge(xn_done, QT * b + qt + 1)
                        wait(pe, xl_done, QT * b + qt - 1)
                        for k in range(KT):
                            t = pe.transpose(xT_bank[qt % 2][:, k * P:(k + 1) * P], xn[:, qt, k * P:(k + 1) * P], ident)
                        t.then_inc(xT_done, 1)

                def batch(b, more):
                    j = QT * (b + 1)
                    turn(b)
                    if more:
                        a_transpose(b + 1, 0)
                    pe.wait_ge(xl_done, QT * b + QT)
                    layer(b, 0)
                    if more:
                        attended(j, 0)
                        a_transpose(b + 1, 1)
                    layer(b, 1)
                    if more:
                        attended(j + 1, 1)
                        a_transpose(b + 1, 2)
                    last_layer(b)
                    if more:
                        attended(j + 2, 0)
                        a_transpose(b + 1, 3)
                        attended(j + 3, 1)

                a_transpose(0, 0)
                pe.wait_ge(w_lo_done, 1)
                for j in range(QT):
                    if j + 1 < QT:
                        a_transpose(0, j + 1)
                    attended(j, j % 2)
                pe.wait_ge(signs_done, 3 * KT)
                over(pe, batch)


def build(nc, io, out, phases=6):
    parts_dram = [nc.dram_tensor(f"qk_parts{i}", [GROUPS, 2, PARTS, P, T], BF16, kind="Internal").ap() for i in range(2)]
    with ExitStack() as ctx:
        m = Memory(nc, ctx, "main")
        X = m.sb("x", [P, TILES * C])
        const = m.sb("const", [P, CONSTS])
        const_in = m.sem("const_in")
        with nc.Block() as block:
            @block.sync
            def _(sp):
                sp.dma_start(const[:, :], io["consts"]).then_inc(const_in, 16)
                sp.wait_ge(const_in, 16)
        heads = m.sb("heads", [P, TILES * C])
        for layer in range(2):
            if phases > 3 * layer:
                pre_phase(nc, layer, io, X, heads, parts_dram[layer], const)
            if phases > 3 * layer + 1:
                attention_phase(nc, layer, heads, parts_dram[layer], const)
            if layer == 0 and phases > 2:
                post0_phase(nc, io, X, heads, const)
            if layer == 1 and phases > 5:
                post1_phase(nc, io, X, heads, const, out)


TURNED = ("L0_ffn_q_scales", "L0_ffn_q_vals", "L1_attn_wq", "L1_attn_wk", "L1_attn_wv")
ROWS = ("L0_attn_attn_qkvb", "L0_attn_attn_ob", "L0_ffn_bias", "L1_ffn_s0", "L1_ffn_s1", "L1_ffn_s2")


def lay_out(inputs):
    arrays = {}
    for name, a in inputs.items():
        a = np.asarray(a)
        if name in TURNED:
            a = a.reshape(C, -1).T
        elif name == "L1_attn_wo":
            a = a.T
        elif name in ROWS:
            a = a.reshape(1, -1)
        arrays[name] = np.ascontiguousarray(a)
    arrays["consts"] = table_of_constants()
    return arrays


def kernel(**inputs):
    import concourse.bacc as bacc
    from concourse.bass_utils import run_bass_kernel_spmd

    nc = bacc.Bacc("TRN2", target_bir_lowering=False, num_devices=1)
    arrays = lay_out(inputs)
    io = {name: nc.dram_tensor(f"in_{name}", a.shape, mybir.dt.from_np(a.dtype), kind="ExternalInput").ap()
          for name, a in arrays.items()}
    out = nc.dram_tensor("out", (B, T, C), F32, kind="ExternalOutput").ap()
    build(nc, io, out)
    r = run_bass_kernel_spmd(nc, [{f"in_{name}": a for name, a in arrays.items()}], core_ids=[0])
    return r.results[0]["out"]
```

```python
from contextlib import ExitStack

import numpy as np

import concourse.bass as bass
from concourse import mybir

B, T, C = 4, 512, 512
HEADS = 32
HD = C // HEADS
P = 128
KT = C // P
QT = T // P
TILES = B * QT
GROUPS = B * KT
GH = P // HD
QH = 4
PARTS = 3
NEG = -1e30
SCALE = HD ** -0.5
EPS = 1e-5
EXC = round(C * 0.8)
INH = 0.8 / (1.0 - 0.8)

Q_BLOCKS = (0, 1, 2, 0, 1, 0)
K_BLOCKS = (0, 0, 0, 1, 1, 2)
QK_ROWS = HD * len(Q_BLOCKS)
MAX_ROWS = QK_ROWS + PARTS

ALU = mybir.AluOpType
ACT = mybir.ActivationFunctionType
F32 = mybir.dt.float32
F32R = mybir.dt.float32r
BF16 = mybir.dt.bfloat16
I32 = mybir.dt.int32
U8 = mybir.dt.uint8
AX_X = mybir.AxisListType.X

IDENT, MASK_S, MASK_ST = 0, P, 2 * P
COS, SIN, NSIN = 3 * P, 3 * P + QT, 3 * P + 2 * QT
SGN_MUL, SGN_ADD = 3 * P + 3 * QT, 3 * P + 3 * QT + KT
CONSTS = 3 * P + 3 * QT + 2 * KT


def table_of_constants():
    c = np.zeros((P, CONSTS), np.float32)
    r = np.arange(P)
    c[:, IDENT:IDENT + P] = np.eye(P)
    c[:, MASK_S:MASK_S + P] = np.where(r[None, :] > r[:, None], NEG, 0.0)
    c[:, MASK_ST:MASK_ST + P] = np.where(r[:, None] > r[None, :], NEG, 0.0)
    pos = np.arange(T, dtype=np.float32).reshape(QT, P).T
    c[:, COS:COS + QT] = np.cos(pos)
    c[:, SIN:SIN + QT] = np.sin(pos)
    c[:, NSIN:NSIN + QT] = -np.sin(pos)
    w = np.where(np.arange(C) < EXC, 1.0, -INH).astype(np.float32).reshape(KT, P).T
    c[:, SGN_MUL:SGN_MUL + KT] = 2.0 * w
    c[:, SGN_ADD:SGN_ADD + KT] = -w
    return c


def wait(eng, sem, value):
    if not (isinstance(value, int) and value <= 0):
        eng.wait_ge(sem, value)


def gated_wait(dve, gate, sem, value):
    dve.wait_ge(sem, value)
    dve.memset(gate[:, :], 0.0)


class Memory:

    def __init__(self, nc, ctx, tag, side="left"):
        self.nc, self.ctx, self.tag, self.side, self.sems = nc, ctx, tag, side, []

    def sb(self, name, shape, dt=F32):
        return self.ctx.enter_context(self.nc.sbuf_tensor(f"{self.tag}_{name}", shape, dt, side=self.side))

    def bank(self, name):
        return self.ctx.enter_context(self.nc.psum_tensor(f"{self.tag}_{name}", [P, 512], F32))

    def sem(self, name):
        s = self.ctx.enter_context(self.nc.semaphore(f"{self.tag}_{name}"))
        self.sems.append(s)
        return s

    def clear_sems(self):
        with self.nc.Block() as block:
            @block.sync
            def _(sp):
                for s in self.sems:
                    sp.sem_clear(s)


def three_pass(pe, out, lhs_hi, lhs_lo, rhs_hi, rhs_lo, first, last):
    pe.matmul(out, lhs_hi, rhs_hi, start=first, stop=False)
    pe.matmul(out, lhs_hi, rhs_lo, start=False, stop=False)
    return pe.matmul(out, lhs_lo, rhs_hi, start=False, stop=last)


def over_batches(eng, tile):
    for qt in range(QT):
        tile(0, qt, True, True)
    with eng.Fori(1, B - 1) as b:
        for qt in range(QT):
            tile(b, qt, True, True)
    for qt in range(QT):
        tile(B - 1, qt, qt < QT - 1, qt < QT - 2)


class QkvWeights:

    def __init__(self, nc, stack, layer, side):
        m = Memory(nc, stack, f"qkv{layer}", side)
        self.hi = m.sb("w_hi", [P, 3, KT, C], F32R)
        self.lo = m.sb("w_lo", [P, 3, KT, C], F32R)


def pre_phase(nc, layer, io, X, V, parts_dram, const, weights):
    rope = layer == 1
    W3 = 3 * C
    w_hi, w_lo = weights.hi, weights.lo
    with ExitStack() as ctx:
        m = Memory(nc, ctx, f"pre{layer}")
        if not rope:
            w_raw = m.sb("w_raw", [P, 2, KT, C])
            bias = m.sb("bias", [P, W3])
        eps = m.sb("eps", [P, 1])
        gate = m.sb("gate", [P, 1])
        xn = m.sb("xn", [P, 2, C])
        xT_hi = m.sb("xT_hi", [P, 2, C], F32R)
        xT_lo = m.sb("xT_lo", [P, 2, C], F32R)
        stats = m.sb("stats", [P, 2, 6])
        mean_var = m.sb("mean_var", [P, 2, 2])
        std = m.sb("std", [P, 2, 1])
        rstd = m.sb("rstd", [P, 2, 1])
        qk = m.sb("qk", [P, 2, 2, C])
        turned = m.sb("turned", [P, 2, C])
        rest = m.sb("rest", [P, 2, C])
        parts = m.sb("parts", [P, 2, 2, PARTS, KT, 2 * P], BF16)

        xT_bank = m.bank("xT")
        out_bank = [m.bank(n) for n in ("q", "k", "v")]
        qkT_bank = [m.bank("qT"), m.bank("kT")]

        w_in = [m.sem(f"w_in{i}") for i in range(2)]
        bias_in, x_in = m.sem("bias_in"), m.sem("x_in")
        eps_set, w_hi_done, w_lo_done = m.sem("eps_set"), m.sem("w_hi_done"), m.sem("w_lo_done")
        ln_step, std_done, xn_done = m.sem("ln_step"), m.sem("std_done"), m.sem("xn_done")
        xT_done, xh_done, xl_done = m.sem("xT_done"), m.sem("xh_done"), m.sem("xl_done")
        mm_done = [m.sem(f"mm_{n}") for n in "qkv"]
        turn_done = [m.sem(f"turn_{n}") for n in "qk"]
        ev_done = [m.sem(f"evac_{n}") for n in "qkv"]
        qkT_done = [m.sem(f"{n}T_done") for n in "qk"]
        h_done = [m.sem(f"{n}h_done") for n in "qk"]
        r_done = [m.sem(f"{n}r_done") for n in "qk"]
        m_done = [m.sem(f"{n}m_done") for n in "qk"]
        l_done = [m.sem(f"{n}l_done") for n in "qk"]
        parts_out = [m.sem(f"parts_out{n}") for n in range(2)]

        x_dram = io["L0_attn_x"].rearrange("b (t p) c -> b p t c", p=P)

        def xtile(j):
            return X[:, bass.ds(j * C, C)]

        def vslice(b, kt):
            return V[:, bass.ds(b * (QT * C), QT * C)].rearrange("p (g k c) -> p g k c", g=KT, k=QT)[:, :, kt, :]

        with nc.Block() as block:

            @block.sync
            def _(sp):
                if not rope:
                    def load_x(j):
                        wait(sp, x_in, 16 * j)
                        sp.dma_start(xtile(j), x_dram[j // QT][:, j % QT, :]).then_inc(x_in, 16)

                    def load_weights(n):
                        if n == 2:
                            sp.wait_ge(w_lo_done, 1)
                        sp.dma_start(w_raw[:, n % 2, :, :], w_dram[:, :, n * C:(n + 1) * C]).then_inc(w_in[n % 2], 16)

                    w_dram = io["L0_attn_attn_qkvw"].rearrange("(k p) n -> p k n", p=P)
                    load_x(0)
                    load_weights(0)
                    load_weights(1)
                    load_x(1)
                    sp.dma_start(bias[:, :], io["L0_attn_attn_qkvb"].to_broadcast([P, W3])).then_inc(bias_in, 16)
                    load_weights(2)
                    for j in range(2, TILES):
                        load_x(j)
                with sp.Fori(0, B) as b:
                    for pair in range(2):
                        for n in range(2):
                            sp.wait_ge(l_done[n], 4 * b + 2 * pair + 2)
                            for part in range(PARTS):
                                dst = parts_dram[bass.ds(4 * b, KT), n, part, :, pair * 256:pair * 256 + 256]
                                sp.dma_start(dst.rearrange("g p t -> p g t"), parts[:, pair, n, part, :, :])\
                                  .then_inc(parts_out[pair], 16)
                for pair in range(2):
                    sp.wait_ge(parts_out[pair], B * 96)

            @block.scalar
            def _(act):

                def ln_std(j, par):
                    act.wait_ge(ln_step, 3 * j + 2)
                    act.activation(std[:, par, :], mean_var[:, par, 1:2], ACT.Sqrt, bias=eps[:, 0:1])\
                       .then_inc(std_done, 1)

                def x_high(j, par):
                    act.wait_ge(xT_done, j + 1)
                    act.activation(xT_hi[:, par, :], xT_bank[:, :], ACT.Copy).then_inc(xh_done, 1)

                def tile(b, kt, xt, ln):
                    j = 4 * b + kt
                    if xt:
                        x_high(j + 1, (kt + 1) % 2)
                    if rope:
                        for n in range(2):
                            act.wait_ge(mm_done[n], j + 1)
                            act.activation(turned[:, n, :], out_bank[n][:, :], ACT.Copy,
                                           scale=const[:, COS + kt:COS + kt + 1]).then_inc(turn_done[n], 1)
                    if ln:
                        ln_std(j + 2, kt % 2)
                    if rope:
                        act.wait_ge(mm_done[2], j + 1)
                        act.activation(vslice(b, kt), out_bank[2][:, :].rearrange("p (g c) -> p g c", g=KT), ACT.Copy)\
                           .then_inc(ev_done[2], 1)
                    pair, at = kt // 2, kt % 2 * P
                    for n in range(2):
                        act.wait_ge(qkT_done[n], j + 1)
                        if kt % 2 == 0:
                            wait(act, parts_out[pair], 96 * b)
                        act.activation(parts[:, pair, n, 0, :, at:at + P],
                                       qkT_bank[n][:, :].rearrange("p (g t) -> p g t", g=KT), ACT.Copy)\
                           .then_inc(h_done[n], 1)
                        act.wait_ge(r_done[n], j + 1)
                        act.activation(parts[:, pair, n, 1, :, at:at + P],
                                       rest[:, n, :].rearrange("p (g t) -> p g t", g=KT), ACT.Copy)\
                           .then_inc(m_done[n], 1)

                act.wait_ge(eps_set, 1)
                ln_std(0, 0)
                x_high(0, 0)
                if not rope:
                    for n in range(3):
                        act.wait_ge(w_in[n % 2], 16 * (n // 2 + 1))
                        act.activation(w_hi[:, n, :, :], w_raw[:, n % 2, :, :], ACT.Copy).then_inc(w_hi_done, 1)
                        if n == 1:
                            ln_std(1, 1)
                else:
                    ln_std(1, 1)
                over_batches(act, tile)

            @block.vector
            def _(dve):
                dve.memset(eps[:, :], EPS).then_inc(eps_set, 1)

                def ln(j, par):
                    if layer == 0:
                        gated_wait(dve, gate, x_in, 16 * j + 16)
                    dve.bn_stats(stats[:, par, :], xtile(j)).then_inc(ln_step, 1)
                    gated_wait(dve, gate, ln_step, 3 * j + 1)
                    dve.bn_aggr(mean_var[:, par, :], stats[:, par, :]).then_inc(ln_step, 1)
                    dve.wait_ge(std_done, j + 1)
                    dve.reciprocal(rstd[:, par, :], std[:, par, :]).then_inc(ln_step, 1)
                    dve.wait_ge(ln_step, 3 * j + 3)
                    wait(dve, xT_done, j - 1)
                    dve.tensor_scalar(xn[:, par, :], xtile(j), mean_var[:, par, 0:1], rstd[:, par, 0:1],
                                      ALU.subtract, ALU.mult).then_inc(xn_done, 1)

                def x_low(j, par):
                    dve.wait_ge(xh_done, j + 1)
                    dve.tensor_tensor(xT_lo[:, par, :], xT_bank[:, :], xT_hi[:, par, :], ALU.subtract)\
                       .then_inc(xl_done, 1)

                def evacuate(b, kt, n):
                    j = 4 * b + kt
                    par = kt % 2
                    dve.wait_ge(mm_done[n], j + 1)
                    if n == 2:
                        dve.tensor_tensor(vslice(b, kt), out_bank[2][:, :].rearrange("p (g c) -> p g c", g=KT),
                                          bias[:, 2 * C:3 * C].rearrange("p (g c) -> p g c", g=KT), ALU.add)\
                           .then_inc(ev_done[2], 1)
                    elif not rope:
                        dve.tensor_tensor(qk[:, n, par, :], out_bank[n][:, :], bias[:, n * C:(n + 1) * C], ALU.add)\
                           .then_inc(ev_done[n], 1)
                    else:
                        dve.wait_ge(turn_done[n], j + 1)
                        x = out_bank[n][:, :].rearrange("p (i e) -> p e i", e=2)
                        t = turned[:, n, :].rearrange("p (i e) -> p e i", e=2)
                        o = qk[:, n, par, :].rearrange("p (i e) -> p e i", e=2)
                        dve.scalar_tensor_tensor(o[:, 0, :], x[:, 1, :], const[:, NSIN + kt:NSIN + kt + 1],
                                                 t[:, 0, :], ALU.mult, ALU.add)
                        dve.scalar_tensor_tensor(o[:, 1, :], x[:, 0, :], const[:, SIN + kt:SIN + kt + 1],
                                                 t[:, 1, :], ALU.mult, ALU.add).then_inc(ev_done[n], 1)

                def split(b, kt, n):
                    j = 4 * b + kt
                    pair, at = kt // 2, kt % 2 * P
                    piece = rest[:, n, :].rearrange("p (g t) -> p g t", g=KT)
                    dve.wait_ge(h_done[n], j + 1)
                    dve.tensor_tensor(piece, qkT_bank[n][:, :].rearrange("p (g t) -> p g t", g=KT),
                                      parts[:, pair, n, 0, :, at:at + P], ALU.subtract).then_inc(r_done[n], 1)
                    dve.wait_ge(m_done[n], j + 1)
                    dve.tensor_tensor(parts[:, pair, n, 2, :, at:at + P], piece,
                                      parts[:, pair, n, 1, :, at:at + P], ALU.subtract).then_inc(l_done[n], 1)

                def tile(b, kt, next_x, next_ln):
                    j = 4 * b + kt
                    if next_x:
                        x_low(j + 1, (kt + 1) % 2)
                    evacuate(b, kt, 0)
                    evacuate(b, kt, 1)
                    if next_ln:
                        ln(j + 2, kt % 2)
                    if not rope:
                        evacuate(b, kt, 2)
                    split(b, kt, 0)
                    split(b, kt, 1)

                ln(0, 0)
                x_low(0, 0)
                if not rope:
                    for n in range(3):
                        dve.wait_ge(w_hi_done, n + 1)
                        dve.tensor_tensor(w_lo[:, n, :, :], w_raw[:, n % 2, :, :], w_hi[:, n, :, :], ALU.subtract)\
                           .then_inc(w_lo_done, 1)
                        if n == 1:
                            ln(1, 1)
                else:
                    ln(1, 1)
                if not rope:
                    dve.wait_ge(bias_in, 16)
                over_batches(dve, tile)

            @block.tensor
            def _(pe):
                ident = const[:, IDENT:IDENT + P]

                def x_transpose(j, par):
                    pe.wait_ge(xn_done, j + 1)
                    wait(pe, xl_done, j)
                    for k in range(KT):
                        t = pe.transpose(xT_bank[:, k * P:(k + 1) * P], xn[:, par, k * P:(k + 1) * P], ident)
                    t.then_inc(xT_done, 1)

                def project(j, par, n):
                    wait(pe, ev_done[n], j)
                    if not rope and isinstance(j, int) and j == 0:
                        pe.wait_ge(w_lo_done, n + 1)
                    for k in range(KT):
                        mm = three_pass(pe, out_bank[n][:, :], xT_hi[:, par, k * P:(k + 1) * P],
                                        xT_lo[:, par, k * P:(k + 1) * P], w_hi[:, n, k, :],
                                        w_lo[:, n, k, :], k == 0, k == KT - 1)
                    mm.then_inc(mm_done[n], 1)

                def qk_transpose(j, par, n):
                    pe.wait_ge(ev_done[n], j + 1)
                    wait(pe, r_done[n], j)
                    for g in range(KT):
                        t = pe.transpose(qkT_bank[n][:, g * P:(g + 1) * P], qk[:, n, par, g * P:(g + 1) * P], ident)
                    t.then_inc(qkT_done[n], 1)

                def tile(b, kt, next_x, _):
                    j, par = 4 * b + kt, kt % 2
                    first = isinstance(j, int) and j == 0
                    if next_x and not first:
                        x_transpose(j + 1, 1 - par)
                    pe.wait_ge(xl_done, j + 1)
                    project(j, par, 0)
                    if first:
                        x_transpose(1, 1)
                    project(j, par, 1)
                    qk_transpose(j, par, 0)
                    project(j, par, 2)
                    qk_transpose(j, par, 1)

                x_transpose(0, 0)
                over_batches(pe, tile)

        m.clear_sems()


def split_by_pool(pool, hi, lo, raw, step, n):
    pool.tensor_scalar(hi, raw, 1.0, None, ALU.mult).then_inc(step, 1)
    pool.wait_ge(step, n + 1)
    pool.tensor_tensor(lo, raw, hi, ALU.subtract).then_inc(step, 1)
    pool.wait_ge(step, n + 2)


def token_tile(heads, b, qt):
    return heads[:, bass.ds(b * (QT * C), QT * C)].rearrange("p (g q c) -> p g q c", g=KT, q=QT)[:, :, qt, :]


class Post0Weights:
    def __init__(self, nc, stack):
        m = Memory(nc, stack, "post0w")
        self.hi = m.sb("w_hi", [P, 2, KT, C], F32R)
        self.lo = m.sb("w_lo", [P, 2, KT, C], F32R)
        self.bias = m.sb("bias", [P, 2, C])
        self.a_tile = m.sb("a_tile", [P, 2, C])

    def stage(self, m):
        self.raw = m.sb("w_raw", [P, 2, KT, C])
        self.codes = m.sb("codes", [P, KT, C], I32)
        self.scales = m.sb("scales", [P, KT, C])
        self.w_in = [m.sem(f"w_in{i}") for i in range(3)]
        self.step, self.bias_added = m.sem("w_step"), m.sem("bias_added")

    def load(self, sp, io):
        sp.dma_start(self.raw[:, 0, :, :], io["L0_attn_attn_ow"].rearrange("(k p) n -> p k n", p=P)).then_inc(self.w_in[0], 16)
        sp.dma_start(self.codes[:, :, :], io["L0_ffn_q_vals"].rearrange("(k p) n -> p k n", p=P)).then_inc(self.w_in[1], 16)
        for k in range(KT):
            for s in range(4):
                sp.dma_start(self.scales[32 * s:32 * s + 32, k, :],
                             io["L0_ffn_q_scales"][4 * k + s:4 * k + s + 1, :].to_broadcast([32, C]))\
                  .then_inc(self.w_in[1], 16)
        for n, name in enumerate(("L0_attn_attn_ob", "L0_ffn_bias")):
            sp.dma_start(self.bias[:, n, :], io[name].to_broadcast([P, C])).then_inc(self.w_in[2], 16)

    def prepare(self, pool, part, const):
        if part == 0:
            pool.wait_ge(self.w_in[0], 16)
            split_by_pool(pool, self.hi[:, 0, :, :], self.lo[:, 0, :, :], self.raw[:, 0, :, :], self.step, 0)
            pool.wait_ge(self.w_in[2], 32)
        elif part == 1:
            pool.wait_ge(self.w_in[1], 16 * 17)
            pool.tensor_scalar(self.raw[:, 1, :, :], self.codes[:, :, :], -128.0, None, ALU.add).then_inc(self.step, 1)
            pool.wait_ge(self.step, 3)
            pool.tensor_tensor(self.raw[:, 1, :, :], self.raw[:, 1, :, :], self.scales[:, :, :], ALU.mult)\
                .then_inc(self.step, 1)
            pool.wait_ge(self.step, 4)
        else:
            split_by_pool(pool, self.hi[:, 1, :, :], self.lo[:, 1, :, :], self.raw[:, 1, :, :], self.step, 4)

    def add_bias(self, pool, t, X):
        x = X[:, bass.ds(t * C, C)]
        pool.tensor_tensor(x, x, self.bias[:, 0, :], ALU.add)


class Post1Weights:
    def __init__(self, nc, stack):
        m = Memory(nc, stack, "post1w")
        self.hi = m.sb("w_hi", [P, KT, C], F32R)
        self.lo = m.sb("w_lo", [P, KT, C], F32R)
        self.signs = m.sb("signs", [P, 3, KT, C], F32R)
        self.s_in = m.sb("s_in", [P, 3])
        self.s2x = m.sb("s2x", [P, 3])
        self.a_tile = m.sb("a_tile", [P, 2, C])

    def stage(self, m):
        self.raw = m.sb("w_raw", [P, KT, C])
        self.bits = m.sb("bits", [P, 3, KT, C], U8)
        self.w_in = [m.sem(f"w_in{i}") for i in range(2)]
        self.step = m.sem("w_step")

    def load(self, sp, io):
        sp.dma_start(self.raw[:, :, :], io["L1_attn_wo"].rearrange("(k p) n -> p k n", p=P)).then_inc(self.w_in[0], 16)
        for n in range(3):
            sp.dma_start(self.bits[:, n, :, :], io[f"L1_ffn_k{n}"].rearrange("(k p) n -> p k n", p=P))\
              .then_inc(self.w_in[1], 16)
            sp.dma_start(self.s_in[:, n:n + 1], io[f"L1_ffn_s{n}"].to_broadcast([P, 1])).then_inc(self.w_in[1], 16)

    def prepare(self, pool, part, const):
        if part == 0:
            pool.wait_ge(self.w_in[0], 16)
            split_by_pool(pool, self.hi[:, :, :], self.lo[:, :, :], self.raw[:, :, :], self.step, 0)
            pool.wait_ge(self.w_in[1], 96)
            pool.tensor_scalar(self.s2x[:, :], self.s_in[:, :], 2.0, None, ALU.mult)
        for n in ((), (0,), (1, 2))[part]:
            for k in range(KT):
                mul = const[:, SGN_MUL + k:SGN_MUL + k + 1] if n else 2.0
                add = const[:, SGN_ADD + k:SGN_ADD + k + 1] if n else -1.0
                pool.tensor_scalar(self.signs[:, n, k, :], self.bits[:, n, k, :], mul, add, ALU.mult, ALU.add)


def attention_phase(nc, layer, io, X, heads, parts_dram, const, post):
    causal = layer == 1
    STEPS = 2 * QT
    SPAN = 1 if causal else 2
    with ExitStack() as stack:
        m = Memory(nc, stack, f"att{layer}", "right")
        q_rows = m.sb("q_rows", [P, 4, QH, T], BF16)
        k_rows = m.sb("k_rows", [P, 4, QH, T], BF16)
        v_group = m.sb("v_group", [P, 2, QT, GH, 2 * HD])
        probs = m.sb("probs", [P, 2, QH, T])
        row_max = m.sb("row_max", [P, 2, QT, QH])
        max_rest = m.sb("max_rest", [P, QT, QH])
        zeros = m.sb("zeros", [P, QT, QH])
        max_parts = m.sb("max_parts", [P, QT, PARTS, QH], BF16)
        max_rows = m.sb("max_rows", [PARTS * QH, 2, T], BF16)
        sums = m.sb("sums", [P, QT, QH])
        o_rows = m.sb("o_rows", [P, T])
        identb = m.sb("identb", [P, P], BF16)
        maskb = m.sb("maskb", [P, 2, P], BF16)

        if causal:
            s_wide, s_narrow, s_both = m.bank("s_3"), m.bank("s_1"), m.bank("s_0_2")
            s_bank = [s_both[:, 3 * P:], s_narrow[:, 0:2 * P], s_both[:, 0:3 * P], s_wide[:, :]]
        else:
            s_banks = stack.enter_context(nc.psum_tensor(f"att{layer}_s", [P, QT, 512], F32))
            s_bank = [s_banks[:, qt, :] for qt in range(QT)]
        S_ORDER = (0, 2, 1, 3) if causal else (0, 1, 2, 3)

        def with_bank(i):
            return max(i + 1, 2) if causal else i - i % SPAN + SPAN

        ST_BANKS = 3 if causal else 2
        st_bank = [m.bank(f"st{i}") for i in range(ST_BANKS)]
        o_bank = m.bank("o")
        t_bank = m.bank("t")
        t_half = t_bank[:, :].bitcast(BF16)

        consts_set, ones_set = m.sem("consts_set"), m.sem("ones_set")
        qk_in = [m.sem(f"qk_in{i}") for i in range(4)]
        s_tile, s_max = m.sem("s_tile"), m.sem("s_max")
        part_step, parts_ready, maxT_done = m.sem("part_step"), m.sem("parts_ready"), m.sem("maxT_done")
        max_copied = m.sem("max_copied")
        max_in = [m.sem(f"max_in{i}") for i in range(2)]
        st_tile, exp_done, pv_done = m.sem("st_tile"), m.sem("exp_done"), m.sem("pv_done")
        v_ready, o_copied, oT_done = m.sem("v_ready"), m.sem("o_copied"), m.sem("oT_done")
        sums_done, ctx_done = m.sem("sums_done"), m.sem("ctx_done")
        QK_DMAS = 2 * len(Q_BLOCKS)

        def st_use(s, h):
            slot = 4 * (s % 2) + h
            last = max(i for i in range(slot - 8, slot) if i % 8 % ST_BANKS == slot % ST_BANKS)
            return st_bank[slot % ST_BANKS], slot - last

        def loads(t, par):
            return 8 * QK_DMAS * (t - par) + 16 * QK_DMAS

        post.stage(m)
        a_in = m.sem("a_in")

        with nc.Block() as block:

            def over_groups(eng, group, head, tail):
                for t in range(head):
                    group(t, t % 2)
                pairs = (GROUPS - head - tail) // 2
                with eng.Fori(0, pairs) as i:
                    group(2 * i + head, head % 2)
                    group(2 * i + head + 1, (head + 1) % 2)
                for t in range(head + 2 * pairs, GROUPS):
                    group(t, t % 2)

            @block.sync
            def _(sp):
                def load(t, par, quad):
                    buf = 2 * par + quad
                    for rows, n, blocks in ((q_rows, 0, Q_BLOCKS), (k_rows, 1, K_BLOCKS)):
                        for i, part in enumerate(blocks):
                            src = parts_dram[bass.ds(t, 1), n, part, quad * 64:quad * 64 + 64, :]
                            sp.dma_start(rows[i * HD:(i + 1) * HD, buf, :, :],
                                         src.rearrange("o (h d) t -> d (o h) t", d=HD)).then_inc(qk_in[buf], 16)

                def place_max(v, par, quad):
                    sp.wait_ge(max_copied, v + 1)
                    for part in range(PARTS):
                        sp.dma_start(q_rows[QK_ROWS + part:QK_ROWS + part + 1, 2 * par + quad, :, :],
                                     max_rows[part * QH:(part + 1) * QH, quad, :]).then_inc(max_in[quad], 16)

                def group(t, par):
                    static = isinstance(t, int)
                    place_max(2 * t + 1, par, 1)
                    if not static or t + 2 < GROUPS:
                        sp.wait_ge(st_tile, 16 * (2 * t + 1))
                        load(t + 2, par, 0)
                    if not static or t + 1 < GROUPS:
                        place_max(2 * t + 2, 1 - par, 0)
                    if not static or t + 2 < GROUPS:
                        sp.wait_ge(st_tile, 16 * (2 * t + 2))
                        load(t + 2, par, 1)

                for t in range(2):
                    for quad in range(2):
                        load(t, t, quad)
                post.load(sp, io)
                place_max(0, 0, 0)
                over_groups(sp, group, 1, 3)
                sp.wait_ge(ctx_done, 2 * KT)
                for qt in range(2):
                    sp.dma_start(post.a_tile[:, qt, :].rearrange("p (g c) -> p g c", g=KT),
                                 token_tile(heads, 0, qt)).then_inc(a_in, 16)
                sp.wait_ge(a_in, 32)

            @block.gpsimd
            def _(pool):
                for par in range(2):
                    pool.memset(v_group[:, par, :, :, :], 1.0).then_inc(ones_set, 1)
                for buf in range(4):
                    pool.wait_ge(ones_set, 2 + buf)
                    pool.memset(k_rows[QK_ROWS:MAX_ROWS, buf, :, :], -1.0).then_inc(ones_set, 1)
                pool.wait_ge(ones_set, 6)
                pool.memset(zeros[:, :, :], 0.0).then_inc(ones_set, 1)
                pool.wait_ge(ones_set, 7)

                def max_split(v, quad):
                    pool.wait_ge(s_max, 16 * (v + 1))
                    wait(pool, maxT_done, v)
                    pool.tensor_tensor(max_parts[:, :, 0, :], row_max[:, quad, :, :], zeros[:, :, :], ALU.add)\
                        .then_inc(part_step, 1)
                    pool.wait_ge(part_step, 3 * v + 1)
                    pool.tensor_tensor(max_rest[:, :, :], row_max[:, quad, :, :], max_parts[:, :, 0, :], ALU.subtract)\
                        .then_inc(part_step, 1)
                    pool.wait_ge(part_step, 3 * v + 2)
                    pool.tensor_tensor(max_parts[:, :, 1, :], max_rest[:, :, :], zeros[:, :, :], ALU.add)\
                        .then_inc(part_step, 1)
                    pool.wait_ge(part_step, 3 * v + 3)
                    pool.tensor_tensor(max_parts[:, :, 2, :], max_rest[:, :, :], max_parts[:, :, 1, :], ALU.subtract)\
                        .then_inc(parts_ready, 1)

                def group(t, par):
                    wait(pool, pv_done, STEPS * (t - 1))
                    src = heads[:, bass.ds(t * C, C)].rearrange("p (k h d) -> p k h d", k=QT, h=GH)
                    for k in range(QT):
                        copy = pool.tensor_copy(v_group[:, par, k, :, 0:HD], src[:, k, :, :])
                    copy.then_inc(v_ready, 1)
                    if isinstance(t, int) and t < 3:
                        post.prepare(pool, t, const)
                    if not causal:
                        post.add_bias(pool, t, X)
                    if not isinstance(t, int) or t + 1 < GROUPS:
                        max_split(2 * t + 2, 0)
                        max_split(2 * t + 3, 1)

                max_split(0, 0)
                max_split(1, 1)
                over_groups(pool, group, 3, 1)

            @block.vector
            def _(dve):
                dve.tensor_copy(identb[:, :], const[:, IDENT:IDENT + P]).then_inc(consts_set, 1)
                dve.tensor_copy(maskb[:, :, :], const[:, MASK_S:MASK_S + 2 * P].rearrange("p (a c) -> p a c", a=2))\
                   .then_inc(consts_set, 1)

                def head_max(v, quad, h):
                    for i in range(0, QT, SPAN):
                        qt = S_ORDER[i]
                        dve.wait_ge(s_tile, 16 * v + 4 * h + with_bank(i))
                        src = s_bank[qt] if causal else s_banks[:, qt:qt + SPAN, :]
                        dve.reduce_max(row_max[:, quad, qt:qt + SPAN, h:h + 1], src, AX_X)\
                           .then_inc(s_max, SPAN)

                def normalize(v, t, quad):
                    dve.wait_ge(oT_done, v + 1)
                    o = t_bank[:, :].rearrange("p (q h d) -> p q h d", q=QT, h=QH)
                    dve.reciprocal(sums[:, :, :], o[:, :, :, HD]).then_inc(sums_done, 1)
                    dve.wait_ge(sums_done, v + 1)
                    dst = heads[:, bass.ds(t * C, C)].rearrange("p (q c) -> p q c", q=QT)
                    dst = dst[:, :, quad * 64:quad * 64 + 64].rearrange("p q (h d) -> p q h d", h=QH)
                    inv = sums[:, :, :].unsqueeze(3).to_broadcast([P, QT, QH, HD])
                    dve.tensor_tensor(dst, o[:, :, :, 0:HD], inv, ALU.mult).then_inc(ctx_done, 1)

                def group(t, par):
                    static = isinstance(t, int)
                    for s in range(STEPS):
                        if not static or t + 1 < GROUPS:
                            head_max(2 * t + 2 + s // QH, s // QH, s % QH)
                        if s == 2 and not (static and t == 0):
                            normalize(2 * t - 1, t - 1, 1)
                        if s == 6:
                            normalize(2 * t, t, 0)

                for s in range(STEPS):
                    head_max(s // QH, s // QH, s % QH)
                over_groups(dve, group, 1, 1)
                normalize(2 * GROUPS - 1, GROUPS - 1, 1)

            @block.scalar
            def _(act):
                def copy_max(v, quad):
                    act.wait_ge(maxT_done, v + 1)
                    act.activation(max_rows[:, quad, :], t_half[0:PARTS * QH, 0:T], ACT.Copy).then_inc(max_copied, 1)

                def copy_out(v, step):
                    act.wait_ge(pv_done, step + 1)
                    act.activation(o_rows[:, :], o_bank[:, :], ACT.Copy).then_inc(o_copied, 1)

                def group(t, par):
                    first = isinstance(t, int) and t == 0
                    last = isinstance(t, int) and t + 1 == GROUPS
                    for s in range(STEPS):
                        k = s % QT
                        q0 = k * P if causal else 0
                        for h in range(QH):
                            act.wait_ge(st_tile, 4 * STEPS * t + 4 * s + h + 1)
                            act.activation(probs[:, s % 2, h, q0:T], st_use(s, h)[0][:, q0:T], ACT.Exp, scale=SCALE)\
                               .then_inc(exp_done, 1)
                            if s == 1 and h == 0 and not first:
                                copy_out(2 * t - 1, STEPS * t - 1)
                            if s == 2 and h == 0:
                                copy_max(2 * t + 1, 1)
                            if s == 5 and h == 0:
                                copy_out(2 * t, STEPS * t + 3)
                            if s == 6 and h == 0 and not last:
                                copy_max(2 * t + 2, 0)

                copy_max(0, 0)
                over_groups(act, group, 1, 1)
                copy_out(2 * GROUPS - 1, STEPS * GROUPS - 1)

            @block.tensor
            def _(pe):
                pe.wait_ge(consts_set, 2)

                def score_tile(v, buf, h, i):
                    qt = S_ORDER[i]
                    n = (qt + 1) * P if causal else T
                    wait(pe, s_max, 16 * v + 4 * h - QT + with_bank(i))
                    mm = pe.matmul(s_bank[qt], q_rows[0:QK_ROWS, buf, h, qt * P:(qt + 1) * P],
                                   k_rows[0:QK_ROWS, buf, h, 0:n], start=True, stop=not causal)
                    if causal:
                        mm = pe.matmul(s_bank[qt][:, n - P:n], identb[:, :], maskb[:, 0, :], start=False, stop=True)
                    mm.then_inc(s_tile, 1)

                def shifted_tile(t, s, buf, h):
                    k = s % QT
                    q0 = k * P if causal else 0
                    bank, back = st_use(s, h)
                    wait(pe, exp_done, 4 * STEPS * t + 4 * s + h - back + 1)
                    mm = pe.matmul(bank[:, q0:T], k_rows[0:MAX_ROWS, buf, h, k * P:(k + 1) * P],
                                   q_rows[0:MAX_ROWS, buf, h, q0:T], start=True, stop=not causal)
                    if causal:
                        mm = pe.matmul(bank[:, q0:q0 + P], identb[:, :], maskb[:, 1, :], start=False, stop=True)
                    mm.then_inc(st_tile, 1)

                def weigh(t, par, s):
                    k = s % QT
                    q0 = k * P if causal else 0
                    step = STEPS * t + s
                    if k == 0:
                        wait(pe, o_copied, 2 * t + s // QT)
                        pe.wait_ge(v_ready, t + 1)
                    pe.wait_ge(exp_done, 4 * step + 4)
                    for h in range(QH):
                        mm = pe.matmul(o_bank[32 * h:32 * h + 32, q0:T], v_group[:, par, k, s // QT * QH + h, :],
                                       probs[:, s % 2, h, q0:T], start=(k == 0), stop=(k == QT - 1))
                    mm.then_inc(pv_done, 1)

                def max_transpose(v):
                    pe.wait_ge(parts_ready, v + 1)
                    wait(pe, max_copied, v)
                    wait(pe, ctx_done, v - 2)
                    for qt in range(QT):
                        t = pe.transpose(t_half[0:PARTS * QH, qt * P:(qt + 1) * P],
                                         max_parts[:, qt, :, :], identb[:, :])
                    t.then_inc(maxT_done, 1)

                def out_transpose(v, maxima):
                    pe.wait_ge(o_copied, v + 1)
                    pe.wait_ge(max_copied, maxima)
                    wait(pe, ctx_done, v)
                    for qt in range(QT):
                        t = pe.transpose(t_bank[:, qt * P:(qt + 1) * P], o_rows[:, qt * P:(qt + 1) * P],
                                         const[:, IDENT:IDENT + P])
                    t.then_inc(oT_done, 1)

                def group(t, par):
                    first = isinstance(t, int) and t == 0
                    last = isinstance(t, int) and t + 1 == GROUPS
                    for s in range(STEPS):
                        quad = s // QT
                        if s % QT == 0:
                            if not last:
                                pe.wait_ge(qk_in[2 * (1 - par) + quad], loads(t + 1, 1 - par))
                            pe.wait_ge(max_in[quad], 16 * PARTS * (t + 1))
                        for h in range(ST_BANKS):
                            shifted_tile(t, s, 2 * par + quad, h)
                        if not last:
                            for i in range(QT):
                                score_tile(2 * t + 2 + quad, 2 * (1 - par) + quad, s % QT, i)
                        for h in range(ST_BANKS, QH):
                            shifted_tile(t, s, 2 * par + quad, h)
                        if s > 0:
                            weigh(t, par, s - 1)
                        elif not first:
                            weigh(t - 1, 1 - par, STEPS - 1)
                        if s == 1:
                            max_transpose(2 * t + 1)
                        if s == 2 and not first:
                            out_transpose(2 * t - 1, 2 * t + 2)
                        if s == 5 and not last:
                            max_transpose(2 * t + 2)
                        if s == 6:
                            out_transpose(2 * t, 2 * t + 2 if last else 2 * t + 3)

                for quad in range(2):
                    pe.wait_ge(qk_in[quad], loads(0, 0))
                    for h in range(QH):
                        for i in range(QT):
                            score_tile(quad, quad, h, i)
                pe.wait_ge(ones_set, 6)
                max_transpose(0)
                over_groups(pe, group, 1, 1)
                weigh(GROUPS - 1, 1, STEPS - 1)
                out_transpose(2 * GROUPS - 1, 2 * GROUPS)

        m.clear_sems()


def fetch_outputs(sp, heads, a_tile, b, qt, a_in, aT_done):
    j = QT * b + qt
    wait(sp, aT_done, j - 1)
    sp.dma_start(a_tile[:, qt % 2, :].rearrange("p (g c) -> p g c", g=KT), token_tile(heads, b, qt))\
      .then_inc(a_in[qt % 2], 16)


def outputs_in(b, qt):
    return 16 * (b * (QT // 2) + qt // 2)


def low_part(dve, out, bank, high):
    return dve.tensor_tensor(out, bank, high, ALU.subtract)


def post0_phase(nc, io, X, heads, const, weights, qkv):
    w_hi, w_lo, bias, a_tile = weights.hi, weights.lo, weights.bias, weights.a_tile
    with ExitStack() as stack:
        m = Memory(nc, stack, "post0")
        eps = m.sb("eps", [P, 1])
        gate = m.sb("gate", [P, 1])
        aT_hi = m.sb("aT_hi", [P, 2, C], F32R)
        aT_lo = m.sb("aT_lo", [P, 2, C], F32R)
        xT_hi = m.sb("xT_hi", [P, 2, C], F32R)
        xT_lo = m.sb("xT_lo", [P, 2, C], F32R)
        xn = m.sb("xn", [P, 2, C])
        stats = m.sb("stats", [P, 6])
        mean_var = m.sb("mean_var", [P, 2])
        std = m.sb("std", [P, 1])
        rstd = m.sb("rstd", [P, 1])
        next_raw = m.sb("next_raw", [P, KT, C])

        aT_bank, xT_bank = m.bank("aT"), m.bank("xT")
        o_bank = [m.bank(f"o{i}") for i in range(2)]
        f_bank = [m.bank(f"f{i}") for i in range(2)]

        eps_set, next_in, next_split = m.sem("eps_set"), m.sem("next_in"), m.sem("next_split")
        a_in = [m.sem(f"a_in{i}") for i in range(2)]
        aT_done, ah_done, al_done = m.sem("aT_done"), m.sem("ah_done"), m.sem("al_done")
        xT_done, xh_done, xl_done = m.sem("xT_done"), m.sem("xh_done"), m.sem("xl_done")
        o_done, f_done = m.sem("o_done"), m.sem("f_done")
        ln_step, std_done, xn_done = m.sem("ln_step"), m.sem("std_done"), m.sem("xn_done")
        o_read, bias_added, x_final = m.sem("o_read"), m.sem("bias_added"), m.sem("x_final")

        def xtile(j):
            return X[:, bass.ds(j * C, C)]

        with nc.Block() as block:

            @block.sync
            def _(sp):
                def load_next(n):
                    wait(sp, next_split, 2 * n)
                    name = ("L1_attn_wq", "L1_attn_wk", "L1_attn_wv")[n]
                    sp.dma_start(next_raw[:, :, :], io[name].rearrange("(k p) n -> p k n", p=P)).then_inc(next_in, 16)

                def tile(b, qt, one, two):
                    if two:
                        fetch_outputs(sp, heads, a_tile, b + (qt + 2) // QT, (qt + 2) % QT, a_in, aT_done)
                    if isinstance(b, int) and b == 0 and qt % 2 == 0:
                        load_next(qt // 2)
                    if isinstance(b, int) and b == B - 1 and qt == 0:
                        load_next(2)

                over_batches(sp, tile)

            @block.gpsimd
            def _(pool):
                def split_next(n):
                    pool.wait_ge(next_in, 16 * (n + 1))
                    split_by_pool(pool, qkv.hi[:, n, :, :], qkv.lo[:, n, :, :], next_raw[:, :, :], next_split, 2 * n)

                def tile(b, qt, one, two):
                    j = QT * b + qt
                    pool.wait_ge(xn_done, j + 1)
                    pool.tensor_tensor(xtile(j), xtile(j), bias[:, 1, :], ALU.add).then_inc(bias_added, 1)
                    if isinstance(b, int) and b == 0 and qt in (1, 3):
                        split_next(qt // 2)
                    if isinstance(b, int) and b == B - 1 and qt == 1:
                        split_next(2)

                over_batches(pool, tile)

            @block.scalar
            def _(act):
                def high(out, bank, ready, j, done):
                    act.wait_ge(ready, j + 1)
                    act.activation(out, bank, ACT.Copy).then_inc(done, 1)

                def a_high(j, par):
                    high(aT_hi[:, par, :], aT_bank[:, :], aT_done, j, ah_done)

                def ln_std(j):
                    act.wait_ge(ln_step, 3 * j + 2)
                    act.activation(std[:, :], mean_var[:, 1:2], ACT.Sqrt, bias=eps[:, 0:1]).then_inc(std_done, 1)

                def tile(b, qt, one, two):
                    j, par = QT * b + qt, qt % 2
                    if two:
                        a_high(j + 2, par)
                    high(xT_hi[:, par, :], xT_bank[:, :], xT_done, j, xh_done)
                    if one:
                        ln_std(j + 1)

                a_high(0, 0)
                a_high(1, 1)
                act.wait_ge(eps_set, 1)
                ln_std(0)
                over_batches(act, tile)

            @block.vector
            def _(dve):
                dve.memset(eps[:, :], EPS).then_inc(eps_set, 1)

                def a_low(j, par):
                    dve.wait_ge(ah_done, j + 1)
                    low_part(dve, aT_lo[:, par, :], aT_bank[:, :], aT_hi[:, par, :]).then_inc(al_done, 1)

                def attended(j, par):
                    dve.wait_ge(o_done, j + 1)
                    dve.tensor_tensor(xtile(j), o_bank[par][:, :], xtile(j), ALU.add).then_inc(o_read, 1)
                    gated_wait(dve, gate, o_read, j + 1)
                    dve.bn_stats(stats[:, :], xtile(j)).then_inc(ln_step, 1)
                    gated_wait(dve, gate, ln_step, 3 * j + 1)
                    dve.bn_aggr(mean_var[:, :], stats[:, :]).then_inc(ln_step, 1)

                def normalized(j, par):
                    dve.wait_ge(std_done, j + 1)
                    dve.reciprocal(rstd[:, :], std[:, :]).then_inc(ln_step, 1)
                    dve.wait_ge(ln_step, 3 * j + 3)
                    wait(dve, xT_done, j - 1)
                    dve.tensor_scalar(xn[:, par, :], xtile(j), mean_var[:, 0:1], rstd[:, 0:1],
                                      ALU.subtract, ALU.mult).then_inc(xn_done, 1)

                def final(j, par):
                    dve.wait_ge(bias_added, j + 1)
                    dve.wait_ge(f_done, j + 1)
                    dve.tensor_tensor(xtile(j), f_bank[par][:, :], xtile(j), ALU.add).then_inc(x_final, 1)

                def tile(b, qt, one, two):
                    j, par = QT * b + qt, qt % 2
                    if one:
                        attended(j + 1, 1 - par)
                    if two:
                        a_low(j + 2, par)
                    if one:
                        normalized(j + 1, 1 - par)
                    dve.wait_ge(xh_done, j + 1)
                    low_part(dve, xT_lo[:, par, :], xT_bank[:, :], xT_hi[:, par, :]).then_inc(xl_done, 1)
                    if not (isinstance(j, int) and j == 0):
                        final(j - 1, 1 - par)

                a_low(0, 0)
                a_low(1, 1)
                attended(0, 0)
                normalized(0, 0)
                over_batches(dve, tile)
                final(TILES - 1, (TILES - 1) % 2)

            @block.tensor
            def _(pe):
                ident = const[:, IDENT:IDENT + P]

                def a_transpose(b, qt):
                    wait(pe, al_done, QT * b + qt)
                    wait(pe, a_in[qt % 2], outputs_in(b, qt))
                    for g in range(KT):
                        t = pe.transpose(aT_bank[:, g * P:(g + 1) * P], a_tile[:, qt % 2, g * P:(g + 1) * P], ident)
                    t.then_inc(aT_done, 1)

                def x_transpose(j, par):
                    pe.wait_ge(xn_done, j + 1)
                    wait(pe, xl_done, j)
                    for k in range(KT):
                        t = pe.transpose(xT_bank[:, k * P:(k + 1) * P], xn[:, par, k * P:(k + 1) * P], ident)
                    t.then_inc(xT_done, 1)

                def product(bank, hi, lo, w, done):
                    for k in range(KT):
                        mm = three_pass(pe, bank[:, :], hi[:, k * P:(k + 1) * P], lo[:, k * P:(k + 1) * P],
                                        w_hi[:, w, k, :], w_lo[:, w, k, :], k == 0, k == KT - 1)
                    mm.then_inc(done, 1)

                def attended(j, par):
                    pe.wait_ge(al_done, j + 1)
                    wait(pe, o_read, j - 1)
                    product(o_bank[par], aT_hi[:, par, :], aT_lo[:, par, :], 0, o_done)

                def dequantized(j, par):
                    pe.wait_ge(xl_done, j + 1)
                    wait(pe, x_final, j - 1)
                    product(f_bank[par], xT_hi[:, par, :], xT_lo[:, par, :], 1, f_done)

                def tile(b, qt, one, two):
                    j, par = QT * b + qt, qt % 2
                    if one:
                        attended(j + 1, 1 - par)
                    if two:
                        a_transpose(b + (qt + 2) // QT, (qt + 2) % QT)
                    x_transpose(j, par)
                    if not (isinstance(j, int) and j == 0):
                        dequantized(j - 1, 1 - par)

                a_transpose(0, 0)
                a_transpose(0, 1)
                attended(0, 0)
                over_batches(pe, tile)
                dequantized(TILES - 1, (TILES - 1) % 2)

        m.clear_sems()


def post1_phase(nc, X, heads, const, out, weights):
    a_tile, signs, s_in, s2x = weights.a_tile, weights.signs, weights.s_in, weights.s2x
    with ExitStack() as stack:
        m = Memory(nc, stack, "post1", "right")
        eps = m.sb("eps", [P, 1])
        gate = m.sb("gate", [P, 1])
        aT_hi = m.sb("aT_hi", [P, 2, C], F32R)
        aT_lo = m.sb("aT_lo", [P, 2, C], F32R)
        act_hi = m.sb("act_hi", [P, 3, KT, T], F32R)
        act_lo = m.sb("act_lo", [P, 3, KT, T], F32R)
        relu = m.sb("relu", [P, KT, T])
        xn = m.sb("xn", [P, QT, C])
        stats = m.sb("stats", [P, 6])
        mean_var = m.sb("mean_var", [P, 2])
        std = m.sb("std", [P, 1])
        rstd = m.sb("rstd", [P, 1])

        aT_bank = m.bank("aT")
        xT_bank = [m.bank(f"xT{i}") for i in range(2)]
        o_bank = [m.bank(f"o{i}") for i in range(2)]
        h_bank = [m.bank(f"h{i}") for i in range(2)]

        eps_set = m.sem("eps_set")
        a_in = [m.sem(f"a_in{i}") for i in range(2)]
        aT_done, ah_done, al_done = m.sem("aT_done"), m.sem("ah_done"), m.sem("al_done")
        xT_done, xh_done, xl_done = m.sem("xT_done"), m.sem("xh_done"), m.sem("xl_done")
        o_done, o_read = m.sem("o_done"), m.sem("o_read")
        ln_step, std_done, xn_done = m.sem("ln_step"), m.sem("std_done"), m.sem("xn_done")
        h_done, relu_done, hh_done, hl_done = m.sem("h_done"), m.sem("relu_done"), m.sem("hh_done"), m.sem("hl_done")
        x_final, x_out = m.sem("x_final"), m.sem("x_out")
        BANKS = 3 * QT

        def xtile(j):
            return X[:, bass.ds(j * C, C)]

        with nc.Block() as block:

            def over(eng, batch):
                batch(0, True)
                with eng.Fori(1, B - 1) as b:
                    batch(b, True)
                batch(B - 1, False)

            @block.sync
            def _(sp):
                for qt in range(2, QT):
                    fetch_outputs(sp, heads, a_tile, 0, qt, a_in, aT_done)

                def batch(b, more):
                    if more:
                        for qt in range(QT):
                            fetch_outputs(sp, heads, a_tile, b + 1, qt, a_in, aT_done)
                    for qt in range(QT):
                        sp.wait_ge(x_final, QT * b + qt + 1)
                        sp.dma_start(out[bass.ds(b, 1), qt * P:(qt + 1) * P, :].rearrange("o p c -> (o p) c"),
                                     xtile(QT * b + qt)).then_inc(x_out, 16)

                over(sp, batch)
                sp.wait_ge(x_out, 16 * TILES)

            @block.scalar
            def _(act):
                def a_high(j, par):
                    act.wait_ge(aT_done, j + 1)
                    act.activation(aT_hi[:, par, :], aT_bank[:, :], ACT.Copy).then_inc(ah_done, 1)

                def ln_std(j):
                    act.wait_ge(ln_step, 3 * j + 2)
                    act.activation(std[:, :], mean_var[:, 1:2], ACT.Sqrt, bias=eps[:, 0:1]).then_inc(std_done, 1)

                def layer_high(b, n, features):
                    for k in features:
                        use = 2 * KT * b + KT * n + k
                        act.wait_ge(h_done, BANKS * b + KT * n + k + 1)
                        wait(act, hl_done, use - KT + 1)
                        act.activation(relu[:, k, :], h_bank[k % 2][:, :], ACT.Relu, scale=s2x[:, n:n + 1])\
                           .then_inc(relu_done, 1)
                        act.wait_ge(relu_done, use + 1)
                        act.activation(act_hi[:, n + 1, k, :], relu[:, k, :], ACT.Copy).then_inc(hh_done, 1)

                def turn_high(b):
                    for qt in range(QT):
                        act.wait_ge(xT_done, QT * b + qt + 1)
                        act.activation(act_hi[:, 0, :, qt * P:(qt + 1) * P],
                                       xT_bank[qt % 2][:, :].rearrange("p (k t) -> p k t", k=KT), ACT.Copy)\
                           .then_inc(xh_done, 1)

                def batch(b, more):
                    j = QT * (b + 1)
                    if more:
                        a_high(j, 0)
                    turn_high(b)
                    if more:
                        a_high(j + 1, 1)
                        ln_std(j)
                    layer_high(b, 0, range(KT))
                    if more:
                        a_high(j + 2, 0)
                        ln_std(j + 1)
                    layer_high(b, 1, range(KT // 2))
                    if more:
                        a_high(j + 3, 1)
                        ln_std(j + 2)
                    layer_high(b, 1, range(KT // 2, KT))
                    if more:
                        ln_std(j + 3)

                a_high(0, 0)
                a_high(1, 1)
                act.wait_ge(eps_set, 1)
                for j in range(QT):
                    if j + 2 < QT:
                        a_high(j + 2, j % 2)
                    ln_std(j)
                over(act, batch)

            @block.vector
            def _(dve):
                dve.memset(eps[:, :], EPS).then_inc(eps_set, 1)

                def a_low(j, par):
                    dve.wait_ge(ah_done, j + 1)
                    low_part(dve, aT_lo[:, par, :], aT_bank[:, :], aT_hi[:, par, :]).then_inc(al_done, 1)

                def attended(j, par):
                    dve.wait_ge(o_done, j + 1)
                    dve.tensor_tensor(xtile(j), o_bank[par % 2][:, :], xtile(j), ALU.add).then_inc(o_read, 1)
                    gated_wait(dve, gate, o_read, j + 1)
                    dve.bn_stats(stats[:, :], xtile(j)).then_inc(ln_step, 1)
                    gated_wait(dve, gate, ln_step, 3 * j + 1)
                    dve.bn_aggr(mean_var[:, :], stats[:, :]).then_inc(ln_step, 1)

                def normalized(j, par):
                    dve.wait_ge(std_done, j + 1)
                    dve.reciprocal(rstd[:, :], std[:, :]).then_inc(ln_step, 1)
                    dve.wait_ge(ln_step, 3 * j + 3)
                    dve.tensor_scalar(xn[:, par, :], xtile(j), mean_var[:, 0:1], rstd[:, 0:1],
                                      ALU.subtract, ALU.mult).then_inc(xn_done, 1)

                def layer_low(b, n, features):
                    for k in features:
                        dve.wait_ge(hh_done, 2 * KT * b + KT * n + k + 1)
                        low_part(dve, act_lo[:, n + 1, k, :], relu[:, k, :], act_hi[:, n + 1, k, :])\
                            .then_inc(hl_done, 1)

                def batch(b, more):
                    j = QT * (b + 1)
                    if more:
                        a_low(j, 0)
                    for qt in range(QT):
                        dve.wait_ge(xh_done, QT * b + qt + 1)
                        low_part(dve, act_lo[:, 0, :, qt * P:(qt + 1) * P],
                                 xT_bank[qt % 2][:, :].rearrange("p (k t) -> p k t", k=KT),
                                 act_hi[:, 0, :, qt * P:(qt + 1) * P]).then_inc(xl_done, 1)
                    if more:
                        attended(j, 0)
                        a_low(j + 1, 1)
                        normalized(j, 0)
                    layer_low(b, 0, range(KT))
                    if more:
                        attended(j + 1, 1)
                        a_low(j + 2, 0)
                        normalized(j + 1, 1)
                    layer_low(b, 1, range(KT // 2))
                    if more:
                        attended(j + 2, 2)
                        a_low(j + 3, 1)
                        normalized(j + 2, 2)
                    layer_low(b, 1, range(KT // 2, KT))
                    if more:
                        attended(j + 3, 3)
                        normalized(j + 3, 3)
                    for qt in range(QT):
                        dve.wait_ge(h_done, BANKS * b + 2 * KT + qt + 1)
                        dve.scalar_tensor_tensor(xtile(QT * b + qt), h_bank[qt % 2][:, :], s_in[:, 2:3],
                                                 xtile(QT * b + qt), ALU.mult, ALU.add).then_inc(x_final, 1)

                a_low(0, 0)
                a_low(1, 1)
                for j in range(QT):
                    attended(j, j)
                    if j + 2 < QT:
                        a_low(j + 2, j % 2)
                    normalized(j, j)
                over(dve, batch)

            @block.tensor
            def _(pe):
                ident = const[:, IDENT:IDENT + P]

                def a_transpose(b, qt):
                    wait(pe, al_done, QT * b + qt)
                    wait(pe, a_in[qt % 2], outputs_in(b, qt))
                    for g in range(KT):
                        t = pe.transpose(aT_bank[:, g * P:(g + 1) * P], a_tile[:, qt % 2, g * P:(g + 1) * P], ident)
                    t.then_inc(aT_done, 1)

                def attended(j, par):
                    pe.wait_ge(al_done, j + 1)
                    wait(pe, o_read, j - 1)
                    for k in range(KT):
                        mm = three_pass(pe, o_bank[par][:, :], aT_hi[:, par, k * P:(k + 1) * P],
                                        aT_lo[:, par, k * P:(k + 1) * P], weights.hi[:, k, :], weights.lo[:, k, :],
                                        k == 0, k == KT - 1)
                    mm.then_inc(o_done, 1)

                def bank_free(b, use):
                    if use < 2:
                        wait(pe, x_final, QT * b - 1 + use)
                    elif use < 2 * KT + 2:
                        pe.wait_ge(relu_done, 2 * KT * b + use - 1)
                    else:
                        pe.wait_ge(x_final, QT * b + use - 2 * KT - 1)

                def layer(b, n, outputs):
                    for o in outputs:
                        bank_free(b, KT * n + o)
                        for k in range(KT):
                            if n:
                                pe.wait_ge(hl_done, 2 * KT * b + KT * (n - 1) + k + 1)
                            w = signs[:, n, k, o * P:(o + 1) * P]
                            pe.matmul(h_bank[o % 2][:, :], w, act_hi[:, n, k, :], start=(k == 0), stop=False)
                            mm = pe.matmul(h_bank[o % 2][:, :], w, act_lo[:, n, k, :], start=False, stop=(k == KT - 1))
                        mm.then_inc(h_done, 1)

                def last_layer(b):
                    for qt in range(QT):
                        bank_free(b, 2 * KT + qt)
                        for k in range(KT):
                            pe.wait_ge(hl_done, 2 * KT * b + KT + k + 1)
                            w = signs[:, 2, k, :]
                            pe.matmul(h_bank[qt % 2][:, :], act_hi[:, 2, k, qt * P:(qt + 1) * P], w,
                                      start=(k == 0), stop=False)
                            mm = pe.matmul(h_bank[qt % 2][:, :], act_lo[:, 2, k, qt * P:(qt + 1) * P], w,
                                           start=False, stop=(k == KT - 1))
                        mm.then_inc(h_done, 1)

                def turn(b):
                    for qt in range(QT):
                        pe.wait_ge(xn_done, QT * b + qt + 1)
                        wait(pe, xl_done, QT * b + qt - 1)
                        for k in range(KT):
                            t = pe.transpose(xT_bank[qt % 2][:, k * P:(k + 1) * P], xn[:, qt, k * P:(k + 1) * P], ident)
                        t.then_inc(xT_done, 1)

                def batch(b, more):
                    j = QT * (b + 1)
                    if more:
                        a_transpose(b + 1, 0)
                    turn(b)
                    if more:
                        attended(j, 0)
                        a_transpose(b + 1, 1)
                    pe.wait_ge(xl_done, QT * b + QT)
                    layer(b, 0, range(KT))
                    if more:
                        attended(j + 1, 1)
                        a_transpose(b + 1, 2)
                    layer(b, 1, range(KT // 2))
                    if more:
                        attended(j + 2, 0)
                        a_transpose(b + 1, 3)
                    layer(b, 1, range(KT // 2, KT))
                    if more:
                        attended(j + 3, 1)
                    last_layer(b)

                a_transpose(0, 0)
                a_transpose(0, 1)
                for j in range(QT):
                    attended(j, j % 2)
                    if j + 2 < QT:
                        a_transpose(0, j + 2)
                over(pe, batch)


def build(nc, io, out, phases=6):
    parts_dram = [nc.dram_tensor(f"qk_parts{i}", [GROUPS, 2, PARTS, P, T], BF16, kind="Internal").ap() for i in range(2)]
    with ExitStack() as ctx:
        m = Memory(nc, ctx, "main")
        X = m.sb("x", [P, TILES * C])
        const = m.sb("const", [P, CONSTS])
        const_in = m.sem("const_in")
        with nc.Block() as block:
            @block.sync
            def _(sp):
                sp.dma_start(const[:, :], io["consts"]).then_inc(const_in, 16)
                sp.wait_ge(const_in, 16)
        heads = m.sb("heads", [P, TILES * C])
        with ExitStack() as stack:
            pre_phase(nc, 0, io, X, heads, parts_dram[0], const, QkvWeights(nc, stack, 0, "right"))
        with ExitStack() as qkv_stack:
            with ExitStack() as stack:
                post = Post0Weights(nc, stack)
                if phases > 1:
                    attention_phase(nc, 0, io, X, heads, parts_dram[0], const, post)
                qkv = QkvWeights(nc, qkv_stack, 1, "right")
                if phases > 2:
                    post0_phase(nc, io, X, heads, const, post, qkv)
            if phases > 3:
                pre_phase(nc, 1, io, X, heads, parts_dram[1], const, qkv)
        with ExitStack() as stack:
            post = Post1Weights(nc, stack)
            if phases > 4:
                attention_phase(nc, 1, io, X, heads, parts_dram[1], const, post)
            if phases > 5:
                post1_phase(nc, X, heads, const, out, post)


TURNED = ("L0_ffn_q_scales", "L0_ffn_q_vals", "L1_attn_wq", "L1_attn_wk", "L1_attn_wv")
ROWS = ("L0_attn_attn_qkvb", "L0_attn_attn_ob", "L0_ffn_bias", "L1_ffn_s0", "L1_ffn_s1", "L1_ffn_s2")


def lay_out(inputs):
    arrays = {}
    for name, a in inputs.items():
        a = np.asarray(a)
        if name in TURNED:
            a = a.reshape(C, -1).T
        elif name == "L1_attn_wo":
            a = a.T
        elif name in ROWS:
            a = a.reshape(1, -1)
        arrays[name] = np.ascontiguousarray(a)
    arrays["consts"] = table_of_constants()
    return arrays


def kernel(**inputs):
    import concourse.bacc as bacc
    from concourse.bass_utils import run_bass_kernel_spmd

    nc = bacc.Bacc("TRN2", target_bir_lowering=False, num_devices=1)
    arrays = lay_out(inputs)
    io = {name: nc.dram_tensor(f"in_{name}", a.shape, mybir.dt.from_np(a.dtype), kind="ExternalInput").ap()
          for name, a in arrays.items()}
    out = nc.dram_tensor("out", (B, T, C), F32, kind="ExternalOutput").ap()
    build(nc, io, out)
    r = run_bass_kernel_spmd(nc, [{f"in_{name}": a for name, a in arrays.items()}], core_ids=[0])
    return r.results[0]["out"]
```

```python
from contextlib import ExitStack

import numpy as np

import concourse.bass as bass
from concourse import mybir

B, T, C = 4, 512, 512
HEADS = 32
HD = C // HEADS
P = 128
KT = C // P
QT = T // P
TILES = B * QT
GROUPS = B * KT
GH = P // HD
QH = 4
PARTS = 3
NEG = -1e30
SCALE = HD ** -0.5
EPS = 1e-5
EXC = round(C * 0.8)
INH = 0.8 / (1.0 - 0.8)

Q_BLOCKS = (0, 1, 2, 0, 1, 0)
K_BLOCKS = (0, 0, 0, 1, 1, 2)
QK_ROWS = HD * len(Q_BLOCKS)
MAX_ROWS = QK_ROWS + PARTS

ALU = mybir.AluOpType
ACT = mybir.ActivationFunctionType
F32 = mybir.dt.float32
F32R = mybir.dt.float32r
BF16 = mybir.dt.bfloat16
I32 = mybir.dt.int32
U8 = mybir.dt.uint8
AX_X = mybir.AxisListType.X

IDENT, MASK = 0, P
COS, SIN, NSIN = 2 * P, 2 * P + QT, 2 * P + 2 * QT
SGN_MUL, SGN_ADD = 2 * P + 3 * QT, 2 * P + 3 * QT + KT
CONSTS = 2 * P + 3 * QT + 2 * KT


def table_of_constants():
    c = np.zeros((P, CONSTS), np.float32)
    r = np.arange(P)
    c[:, IDENT:IDENT + P] = np.eye(P)
    c[:, MASK:MASK + P] = np.where(r[None, :] > r[:, None], NEG, 0.0)
    pos = np.arange(T, dtype=np.float32).reshape(QT, P).T
    c[:, COS:COS + QT] = np.cos(pos)
    c[:, SIN:SIN + QT] = np.sin(pos)
    c[:, NSIN:NSIN + QT] = -np.sin(pos)
    w = np.where(np.arange(C) < EXC, 1.0, -INH).astype(np.float32).reshape(KT, P).T
    c[:, SGN_MUL:SGN_MUL + KT] = 2.0 * w
    c[:, SGN_ADD:SGN_ADD + KT] = -w
    return c


def wait(eng, sem, value):
    if not (isinstance(value, int) and value <= 0):
        eng.wait_ge(sem, value)


def gated_wait(eng, gate, sem, value):
    eng.wait_ge(sem, value)
    eng.memset(gate[:, :], 0.0)


class Memory:

    def __init__(self, nc, ctx, tag, side="left"):
        self.nc, self.ctx, self.tag, self.side, self.sems, self.sem_stack = nc, ctx, tag, side, [], ExitStack()

    def sb(self, name, shape, dt=F32):
        return self.ctx.enter_context(self.nc.sbuf_tensor(f"{self.tag}_{name}", shape, dt, side=self.side))

    def bank(self, name):
        return self.ctx.enter_context(self.nc.psum_tensor(f"{self.tag}_{name}", [P, 512], F32))

    def sem(self, name):
        s = self.sem_stack.enter_context(self.nc.semaphore(f"{self.tag}_{name}"))
        self.sems.append(s)
        return s

    def clear_sems(self, eng):
        for s in self.sems:
            eng.sem_clear(s)


def three_pass(pe, out, lhs_hi, lhs_lo, rhs_hi, rhs_lo, first, last):
    pe.matmul(out, lhs_hi, rhs_hi, start=first, stop=False)
    pe.matmul(out, lhs_hi, rhs_lo, start=False, stop=False)
    return pe.matmul(out, lhs_lo, rhs_hi, start=False, stop=last)


def over_batches(eng, tile):
    for qt in range(QT):
        tile(0, qt, True, True)
    with eng.Fori(1, B - 1) as b:
        for qt in range(QT):
            tile(b, qt, True, True)
    for qt in range(QT):
        tile(B - 1, qt, qt < QT - 1, qt < QT - 2)


def before(b, kt):
    return (b, kt - 1) if kt else (b - 1, QT - 1)


class QkvWeights:

    def __init__(self, nc, stack, layer, side):
        m = Memory(nc, stack, f"qkv{layer}", side)
        self.hi = m.sb("w_hi", [P, 3, KT, C], F32R)
        self.lo = m.sb("w_lo", [P, 3, KT, C], F32R)


def pre_phase(nc, previous, layer, io, X, V, parts_dram, parts_out, const, weights):
    rope = layer == 1
    W3 = 3 * C
    w_hi, w_lo = weights.hi, weights.lo
    with ExitStack() as ctx:
        m = Memory(nc, ctx, f"pre{layer}")
        if not rope:
            w_raw = m.sb("w_raw", [P, 2, KT, C])
            bias = m.sb("bias", [P, W3])
        eps = m.sb("eps", [P, 1])
        gate = m.sb("gate", [P, 1])
        xn = m.sb("xn", [P, 2, C])
        xT_hi = m.sb("xT_hi", [P, 2, C], F32R)
        xT_lo = m.sb("xT_lo", [P, 2, C], F32R)
        stats = m.sb("stats", [P, 2, 6])
        mean_var = m.sb("mean_var", [P, 2, 2])
        std = m.sb("std", [P, 2, 1])
        rstd = m.sb("rstd", [P, 2, 1])
        qk = m.sb("qk", [P, 2, 2, C])
        turned = m.sb("turned", [P, 2, C])
        rest = m.sb("rest", [P, 2, C])
        parts = m.sb("parts", [P, 2, 2, PARTS, KT, 2 * P], BF16)

        xT_bank = m.bank("xT")
        out_bank = [m.bank(n) for n in ("q", "k", "v")]
        qkT_bank = [m.bank("qT"), m.bank("kT")]

        w_in = [m.sem(f"w_in{i}") for i in range(2)]
        bias_in, x_in = m.sem("bias_in"), m.sem("x_in")
        eps_set, w_hi_done, w_lo_done = m.sem("eps_set"), m.sem("w_hi_done"), m.sem("w_lo_done")
        ln_step, std_done, xn_done = m.sem("ln_step"), m.sem("std_done"), m.sem("xn_done")
        xT_done, xh_done, xl_done = m.sem("xT_done"), m.sem("xh_done"), m.sem("xl_done")
        mm_done = [m.sem(f"mm_{n}") for n in "qkv"]
        turn_done = [m.sem(f"turn_{n}") for n in "qk"]
        ev_done = [m.sem(f"evac_{n}") for n in "qkv"]
        qkT_done = [m.sem(f"{n}T_done") for n in "qk"]
        h_done = [m.sem(f"{n}h_done") for n in "qk"]
        r_done = [m.sem(f"{n}r_done") for n in "qk"]
        m_done = [m.sem(f"{n}m_done") for n in "qk"]
        l_done = [m.sem(f"{n}l_done") for n in "qk"]
        const_in = m.sem("const_in")

        x_dram = io["L0_attn_x"].rearrange("b (t p) c -> b p t c", p=P)

        def xtile(j):
            return X[:, bass.ds(j * C, C)]

        def last(j):
            return isinstance(j, int) and j == TILES - 1

        def vslice(b, kt):
            return V[:, bass.ds(b * (QT * C), QT * C)].rearrange("p (g k c) -> p g k c", g=KT, k=QT)[:, :, kt, :]

        with nc.Block() as block:

            @block.gpsimd
            def _(pool):
                if previous:
                    previous.clear_sems(pool)

            @block.sync
            def _(sp):
                if not rope:
                    def load_x(j):
                        wait(sp, x_in, 16 * j)
                        sp.dma_start(xtile(j), x_dram[j // QT][:, j % QT, :]).then_inc(x_in, 16)

                    def load_weights(n):
                        if n == 2:
                            sp.wait_ge(w_lo_done, KT)
                        sp.dma_start(w_raw[:, n % 2, :, :], w_dram[:, :, n * C:(n + 1) * C]).then_inc(w_in[n % 2], 16)

                    w_dram = io["L0_attn_attn_qkvw"].rearrange("(k p) n -> p k n", p=P)
                    load_x(0)
                    sp.dma_start(const[:, :], io["consts"]).then_inc(const_in, 16)
                    load_weights(0)
                    load_weights(1)
                    load_x(1)
                    sp.dma_start(bias[:, :], io["L0_attn_attn_qkvb"].to_broadcast([P, W3])).then_inc(bias_in, 16)
                    load_weights(2)
                    for j in range(2, TILES):
                        load_x(j)
                with sp.Fori(0, B) as b:
                    for pair in range(2):
                        for n in range(2):
                            sp.wait_ge(l_done[n], 4 * b + 2 * pair + 2)
                            for part in range(PARTS):
                                dst = parts_dram[bass.ds(4 * b, KT), n, part, :, pair * 256:pair * 256 + 256]
                                sp.dma_start(dst.rearrange("g p t -> p g t"), parts[:, pair, n, part, :, :])\
                                  .then_inc(parts_out[pair], 16)
                for pair in range(2):
                    sp.wait_ge(parts_out[pair], (B - 1) * 96)

            @block.scalar
            def _(act):

                def ln_std(j, par):
                    act.wait_ge(ln_step, 3 * j + 2)
                    act.activation(std[:, par, :], mean_var[:, par, 1:2], ACT.Sqrt, bias=eps[:, 0:1])\
                       .then_inc(std_done, 1)

                def x_high(j, par):
                    act.wait_ge(xT_done, j + 1)
                    act.activation(xT_hi[:, par, :], xT_bank[:, :], ACT.Copy).then_inc(xh_done, 1)

                def turn(j, kt, n):
                    if rope:
                        act.wait_ge(mm_done[n], j + 1)
                        act.activation(turned[:, n, :], out_bank[n][:, :], ACT.Copy,
                                       scale=const[:, COS + kt:COS + kt + 1]).then_inc(turn_done[n], 1)

                def split(b, kt, n):
                    j = 4 * b + kt
                    pair, at = kt // 2, kt % 2 * P
                    act.wait_ge(qkT_done[n], j + 1)
                    if kt % 2 == 0:
                        wait(act, parts_out[pair], 96 * b)
                    act.activation(parts[:, pair, n, 0, :, at:at + P],
                                   qkT_bank[n][:, :].rearrange("p (g t) -> p g t", g=KT), ACT.Copy)\
                       .then_inc(h_done[n], 1)
                    act.wait_ge(r_done[n], j + 1)
                    act.activation(parts[:, pair, n, 1, :, at:at + P],
                                   rest[:, n, :].rearrange("p (g t) -> p g t", g=KT), ACT.Copy)\
                       .then_inc(m_done[n], 1)

                def tile(b, kt, xt, ln):
                    j = 4 * b + kt
                    turn(j, kt, 0)
                    if xt:
                        x_high(j + 1, (kt + 1) % 2)
                    if not (isinstance(j, int) and j == 0):
                        split(*before(b, kt), 1)
                    turn(j, kt, 1)
                    if ln:
                        ln_std(j + 2, kt % 2)
                    if last(j):
                        split(b, kt, 0)
                        split(b, kt, 1)
                    if rope:
                        act.wait_ge(mm_done[2], j + 1)
                        act.activation(vslice(b, kt), out_bank[2][:, :].rearrange("p (g c) -> p g c", g=KT), ACT.Copy)\
                           .then_inc(ev_done[2], 1)
                    if not last(j):
                        split(b, kt, 0)

                act.wait_ge(eps_set, 1)
                act.activation(std[:, 1, :], eps[:, :], ACT.Sqrt)
                ln_std(0, 0)
                x_high(0, 0)
                if not rope:
                    for n in range(3):
                        act.wait_ge(w_in[n % 2], 16 * (n // 2 + 1))
                        for k in range(KT):
                            act.activation(w_hi[:, n, k, :], w_raw[:, n % 2, k, :], ACT.Copy).then_inc(w_hi_done, 1)
                        if n == 1:
                            ln_std(1, 1)
                else:
                    ln_std(1, 1)
                over_batches(act, tile)

            @block.vector
            def _(dve):
                dve.memset(eps[:, :], EPS).then_inc(eps_set, 1)

                def ln(j, par):
                    if layer == 0:
                        gated_wait(dve, gate, x_in, 16 * j + 16)
                    dve.bn_stats(stats[:, par, :], xtile(j)).then_inc(ln_step, 1)
                    gated_wait(dve, gate, ln_step, 3 * j + 1)
                    dve.bn_aggr(mean_var[:, par, :], stats[:, par, :]).then_inc(ln_step, 1)
                    dve.wait_ge(std_done, j + 1)
                    dve.reciprocal(rstd[:, par, :], std[:, par, :]).then_inc(ln_step, 1)
                    dve.wait_ge(ln_step, 3 * j + 3)
                    wait(dve, xT_done, j - 1)
                    dve.tensor_scalar(xn[:, par, :], xtile(j), mean_var[:, par, 0:1], rstd[:, par, 0:1],
                                      ALU.subtract, ALU.mult).then_inc(xn_done, 1)

                def x_low(j, par):
                    dve.wait_ge(xh_done, j + 1)
                    dve.tensor_tensor(xT_lo[:, par, :], xT_bank[:, :], xT_hi[:, par, :], ALU.subtract)\
                       .then_inc(xl_done, 1)

                def evacuate(b, kt, n):
                    j = 4 * b + kt
                    par = kt % 2
                    dve.wait_ge(mm_done[n], j + 1)
                    if n == 2:
                        dve.tensor_tensor(vslice(b, kt), out_bank[2][:, :].rearrange("p (g c) -> p g c", g=KT),
                                          bias[:, 2 * C:3 * C].rearrange("p (g c) -> p g c", g=KT), ALU.add)\
                           .then_inc(ev_done[2], 1)
                    elif not rope:
                        dve.tensor_tensor(qk[:, n, par, :], out_bank[n][:, :], bias[:, n * C:(n + 1) * C], ALU.add)\
                           .then_inc(ev_done[n], 1)
                    else:
                        dve.wait_ge(turn_done[n], j + 1)
                        x = out_bank[n][:, :].rearrange("p (i e) -> p e i", e=2)
                        t = turned[:, n, :].rearrange("p (i e) -> p e i", e=2)
                        o = qk[:, n, par, :].rearrange("p (i e) -> p e i", e=2)
                        dve.scalar_tensor_tensor(o[:, 0, :], x[:, 1, :], const[:, NSIN + kt:NSIN + kt + 1],
                                                 t[:, 0, :], ALU.mult, ALU.add)
                        dve.scalar_tensor_tensor(o[:, 1, :], x[:, 0, :], const[:, SIN + kt:SIN + kt + 1],
                                                 t[:, 1, :], ALU.mult, ALU.add).then_inc(ev_done[n], 1)

                def split(b, kt, n):
                    j = 4 * b + kt
                    pair, at = kt // 2, kt % 2 * P
                    piece = rest[:, n, :].rearrange("p (g t) -> p g t", g=KT)
                    dve.wait_ge(h_done[n], j + 1)
                    dve.tensor_tensor(piece, qkT_bank[n][:, :].rearrange("p (g t) -> p g t", g=KT),
                                      parts[:, pair, n, 0, :, at:at + P], ALU.subtract).then_inc(r_done[n], 1)
                    dve.wait_ge(m_done[n], j + 1)
                    dve.tensor_tensor(parts[:, pair, n, 2, :, at:at + P], piece,
                                      parts[:, pair, n, 1, :, at:at + P], ALU.subtract).then_inc(l_done[n], 1)

                def tile(b, kt, next_x, next_ln):
                    j = 4 * b + kt
                    evacuate(b, kt, 0)
                    if next_x:
                        x_low(j + 1, (kt + 1) % 2)
                    if not (isinstance(j, int) and j == 0):
                        split(*before(b, kt), 1)
                    evacuate(b, kt, 1)
                    if next_ln:
                        ln(j + 2, kt % 2)
                    if last(j):
                        split(b, kt, 0)
                        split(b, kt, 1)
                    if not rope:
                        evacuate(b, kt, 2)
                    if not last(j):
                        split(b, kt, 0)

                ln(0, 0)
                x_low(0, 0)
                if not rope:
                    for n in range(3):
                        for k in range(KT):
                            dve.wait_ge(w_hi_done, KT * n + k + 1)
                            dve.tensor_tensor(w_lo[:, n, k, :], w_raw[:, n % 2, k, :], w_hi[:, n, k, :], ALU.subtract)\
                               .then_inc(w_lo_done, 1)
                        if n == 1:
                            ln(1, 1)
                else:
                    ln(1, 1)
                if not rope:
                    dve.wait_ge(const_in, 16)
                    dve.wait_ge(bias_in, 16)
                over_batches(dve, tile)

            @block.tensor
            def _(pe):
                ident = const[:, IDENT:IDENT + P]

                def x_transpose(j, par):
                    pe.wait_ge(xn_done, j + 1)
                    wait(pe, xl_done, j)
                    for k in range(KT):
                        t = pe.transpose(xT_bank[:, k * P:(k + 1) * P], xn[:, par, k * P:(k + 1) * P], ident)
                    t.then_inc(xT_done, 1)

                def project(j, par, n):
                    wait(pe, ev_done[n], j)
                    for k in range(KT):
                        if not rope and isinstance(j, int) and j == 0:
                            pe.wait_ge(w_lo_done, KT * n + k + 1)
                        mm = three_pass(pe, out_bank[n][:, :], xT_hi[:, par, k * P:(k + 1) * P],
                                        xT_lo[:, par, k * P:(k + 1) * P], w_hi[:, n, k, :],
                                        w_lo[:, n, k, :], k == 0, k == KT - 1)
                    mm.then_inc(mm_done[n], 1)

                def qk_transpose(j, par, n):
                    pe.wait_ge(ev_done[n], j + 1)
                    wait(pe, r_done[n], j)
                    for g in range(KT):
                        t = pe.transpose(qkT_bank[n][:, g * P:(g + 1) * P], qk[:, n, par, g * P:(g + 1) * P], ident)
                    t.then_inc(qkT_done[n], 1)

                def tile(b, kt, next_x, _):
                    j, par = 4 * b + kt, kt % 2
                    first = isinstance(j, int) and j == 0
                    pe.wait_ge(xl_done, j + 1)
                    project(j, par, 0)
                    if next_x:
                        x_transpose(j + 1, 1 - par)
                    if not first:
                        qk_transpose(j - 1, 1 - par, 1)
                    project(j, par, 1)
                    if last(j):
                        qk_transpose(j, par, 0)
                        qk_transpose(j, par, 1)
                    project(j, par, 2)
                    if not last(j):
                        qk_transpose(j, par, 0)

                if not rope:
                    pe.wait_ge(const_in, 16)
                x_transpose(0, 0)
                over_batches(pe, tile)

        return m


def split_by_pool(pool, hi, lo, raw, step, n):
    pool.tensor_scalar(hi, raw, 1.0, None, ALU.mult).then_inc(step, 1)
    pool.wait_ge(step, n + 1)
    pool.tensor_tensor(lo, raw, hi, ALU.subtract).then_inc(step, 1)
    pool.wait_ge(step, n + 2)


def token_tile(heads, b, qt):
    return heads[:, bass.ds(b * (QT * C), QT * C)].rearrange("p (g q c) -> p g q c", g=KT, q=QT)[:, :, qt, :]


class Post0Weights:
    def __init__(self, nc, stack):
        m = Memory(nc, stack, "post0w")
        self.hi = m.sb("w_hi", [P, 2, KT, C], F32R)
        self.lo = m.sb("w_lo", [P, 2, KT, C], F32R)
        self.bias = m.sb("bias", [P, 2, C])
        self.a_tile = m.sb("a_tile", [P, 2, C])

    def stage(self, m):
        self.raw = m.sb("w_raw", [P, 2, KT, C])
        self.codes = m.sb("codes", [P, KT, C], I32)
        self.scales = m.sb("scales", [P, KT, C])
        self.w_in = [m.sem(f"w_in{i}") for i in range(3)]
        self.step = m.sem("w_step")

    def load(self, sp, io):
        sp.dma_start(self.raw[:, 0, :, :], io["L0_attn_attn_ow"].rearrange("(k p) n -> p k n", p=P)).then_inc(self.w_in[0], 16)
        sp.dma_start(self.codes[:, :, :], io["L0_ffn_q_vals"].rearrange("(k p) n -> p k n", p=P)).then_inc(self.w_in[1], 16)
        for k in range(KT):
            for s in range(4):
                sp.dma_start(self.scales[32 * s:32 * s + 32, k, :],
                             io["L0_ffn_q_scales"][4 * k + s:4 * k + s + 1, :].to_broadcast([32, C]))\
                  .then_inc(self.w_in[1], 16)
        for n, name in enumerate(("L0_attn_attn_ob", "L0_ffn_bias")):
            sp.dma_start(self.bias[:, n, :], io[name].to_broadcast([P, C])).then_inc(self.w_in[2], 16)

    def prepare(self, pool, t, s, const):
        if (t, s) == (0, 0):
            pool.wait_ge(self.w_in[0], 16)
            split_by_pool(pool, self.hi[:, 0, :, :], self.lo[:, 0, :, :], self.raw[:, 0, :, :], self.step, 0)
            pool.wait_ge(self.w_in[2], 32)
        if (t, s) == (1, 0):
            pool.wait_ge(self.w_in[1], 16 * 17)
            pool.tensor_scalar(self.raw[:, 1, :, :], self.codes[:, :, :], -128.0, None, ALU.add).then_inc(self.step, 1)
            pool.wait_ge(self.step, 3)
            pool.tensor_tensor(self.raw[:, 1, :, :], self.raw[:, 1, :, :], self.scales[:, :, :], ALU.mult)\
                .then_inc(self.step, 1)
            pool.wait_ge(self.step, 4)
        if (t, s) == (2, 0):
            split_by_pool(pool, self.hi[:, 1, :, :], self.lo[:, 1, :, :], self.raw[:, 1, :, :], self.step, 4)

    def add_bias(self, pool, t, X):
        x = X[:, bass.ds(t * C, C)]
        pool.tensor_tensor(x, x, self.bias[:, 0, :], ALU.add)


class Post1Weights:
    def __init__(self, nc, stack):
        m = Memory(nc, stack, "post1w")
        self.hi = m.sb("w_hi", [P, KT, C], F32R)
        self.lo = m.sb("w_lo", [P, KT, C], F32R)
        self.signs = m.sb("signs", [P, 3, KT, C], F32R)
        self.s_in = m.sb("s_in", [P, 3])
        self.s2x = m.sb("s2x", [P, 3])
        self.a_tile = m.sb("a_tile", [P, 2, C])

    def stage(self, m):
        self.raw = m.sb("w_raw", [P, KT, C])
        self.bits = m.sb("bits", [P, 3, KT, C], U8)
        self.w_in = [m.sem(f"w_in{i}") for i in range(2)]
        self.step = m.sem("w_step")

    def load(self, sp, io):
        sp.dma_start(self.raw[:, :, :], io["L1_attn_wo"].rearrange("(k p) n -> p k n", p=P)).then_inc(self.w_in[0], 16)
        for n in range(3):
            sp.dma_start(self.bits[:, n, :, :], io[f"L1_ffn_k{n}"].rearrange("(k p) n -> p k n", p=P))\
              .then_inc(self.w_in[1], 16)
            sp.dma_start(self.s_in[:, n:n + 1], io[f"L1_ffn_s{n}"].to_broadcast([P, 1])).then_inc(self.w_in[1], 16)

    def prepare(self, pool, t, s, const):
        if t == 0 and s >= KT:
            k = s - KT
            pool.wait_ge(self.w_in[0], 16)
            split_by_pool(pool, self.hi[:, k, :], self.lo[:, k, :], self.raw[:, k, :], self.step, 2 * k)
        if t == 1 and s == 0:
            pool.wait_ge(self.w_in[1], 96)
            pool.tensor_scalar(self.s2x[:, :], self.s_in[:, :], 2.0, None, ALU.mult)
        if t == 1 or (t == 2 and s < KT):
            n, k = 2 * (t - 1) + s // KT, s % KT
            mul = const[:, SGN_MUL + k:SGN_MUL + k + 1] if n else 2.0
            add = const[:, SGN_ADD + k:SGN_ADD + k + 1] if n else -1.0
            pool.tensor_scalar(self.signs[:, n, k, :], self.bits[:, n, k, :], mul, add, ALU.mult, ALU.add)


def attention_phase(nc, previous, layer, io, X, heads, parts_dram, parts_out, const, post):
    causal = layer == 1
    STEPS = 2 * QT
    SPAN = 1 if causal else 2
    with ExitStack() as stack:
        m = Memory(nc, stack, f"att{layer}", "right")
        q_rows = m.sb("q_rows", [P, 4, QH, T], BF16)
        k_rows = m.sb("k_rows", [P, 4, QH, T], BF16)
        v_group = m.sb("v_group", [P, 2, QT, GH, 2 * HD])
        probs = m.sb("probs", [P, 2, QH, T])
        row_max = m.sb("row_max", [P, 2, QT, QH])
        max_rest = m.sb("max_rest", [P, QT, QH])
        zeros = m.sb("zeros", [P, QT, QH])
        gate = m.sb("gate", [P, STEPS])
        max_parts = m.sb("max_parts", [P, QT, PARTS, QH], BF16)
        max_rows = m.sb("max_rows", [PARTS * QH, 2, T], BF16)
        sums = m.sb("sums", [P, QT, QH])
        o_rows = m.sb("o_rows", [P, T])
        identb = m.sb("identb", [P, P], BF16)
        maskb = m.sb("maskb", [P, P], BF16)

        if causal:
            s_wide, s_narrow, s_both = m.bank("s_3"), m.bank("s_1"), m.bank("s_0_2")
            s_bank = [s_both[:, 3 * P:], s_narrow[:, 0:2 * P], s_both[:, 0:3 * P], s_wide[:, :]]
        else:
            s_banks = stack.enter_context(nc.psum_tensor(f"att{layer}_s", [P, QT, 512], F32))
            s_bank = [s_banks[:, qt, :] for qt in range(QT)]
        S_ORDER = (0, 2, 1, 3) if causal else (0, 1, 2, 3)

        def with_bank(i):
            return max(i + 1, 2) if causal else i - i % SPAN + SPAN

        ST_BANKS = 3 if causal else 2
        st_bank = [m.bank(f"st{i}") for i in range(ST_BANKS)]
        o_bank = m.bank("o")
        t_bank = m.bank("t")
        t_half = t_bank[:, :].bitcast(BF16)

        consts_set, ones_set = m.sem("consts_set"), m.sem("ones_set")
        qk_in = [m.sem(f"qk_in{i}") for i in range(4)]
        s_tile, s_max = m.sem("s_tile"), m.sem("s_max")
        part_step, parts_ready, maxT_done = m.sem("part_step"), m.sem("parts_ready"), m.sem("maxT_done")
        max_copied = m.sem("max_copied")
        max_in = [m.sem(f"max_in{i}") for i in range(2)]
        st_tile, exp_done, masked, pv_done = m.sem("st_tile"), m.sem("exp_done"), m.sem("masked"), m.sem("pv_done")
        v_ready, o_copied, oT_done = m.sem("v_ready"), m.sem("o_copied"), m.sem("oT_done")
        sums_done, ctx_done = m.sem("sums_done"), m.sem("ctx_done")
        QK_DMAS = 2 * len(Q_BLOCKS)

        def st_use(s, h):
            slot = 4 * (s % 2) + h
            last = max(i for i in range(slot - 8, slot) if i % 8 % ST_BANKS == slot % ST_BANKS)
            return st_bank[slot % ST_BANKS], slot - last

        def loads(t, par, quad):
            return 8 * QK_DMAS * (t - par) + (0 if par and quad else 16 * QK_DMAS)

        post.stage(m)
        a_in = m.sem("a_in")

        with nc.Block() as block:

            def over_groups(eng, group, head, tail):
                for t in range(head):
                    group(t, t % 2)
                pairs = (GROUPS - head - tail) // 2
                with eng.Fori(0, pairs) as i:
                    group(2 * i + head, head % 2)
                    group(2 * i + head + 1, (head + 1) % 2)
                for t in range(head + 2 * pairs, GROUPS):
                    group(t, t % 2)

            @block.sync
            def _(sp):
                def load(t, par, quad, quads=1):
                    buf = 2 * par + quad
                    for rows, n, blocks in ((q_rows, 0, Q_BLOCKS), (k_rows, 1, K_BLOCKS)):
                        for i, part in enumerate(blocks):
                            src = parts_dram[bass.ds(t, 1), n, part, quad * 64:(quad + quads) * 64, :]
                            dst = rows[i * HD:(i + 1) * HD, buf:buf + quads, :, :]
                            sp.dma_start(dst.rearrange("d u h t -> d (u h) t"),
                                         src.rearrange("o (h d) t -> d (o h) t", d=HD)).then_inc(qk_in[buf], 16)

                def place_max(v, par, quad):
                    sp.wait_ge(max_copied, v + 1)
                    for part in range(PARTS):
                        sp.dma_start(q_rows[QK_ROWS + part:QK_ROWS + part + 1, 2 * par + quad, :, :],
                                     max_rows[part * QH:(part + 1) * QH, quad, :]).then_inc(max_in[quad], 16)

                def group(t, par):
                    static = isinstance(t, int)
                    place_max(2 * t + 1, par, 1)
                    if not static or t + 2 < GROUPS:
                        sp.wait_ge(st_tile, 16 * (2 * t + 1))
                        load(t + 2, par, 0)
                    if not static or t + 1 < GROUPS:
                        place_max(2 * t + 2, 1 - par, 0)
                    if not static or t + 2 < GROUPS:
                        sp.wait_ge(st_tile, 16 * (2 * t + 2))
                        load(t + 2, par, 1)

                load(0, 0, 0)
                load(0, 0, 1)
                load(1, 1, 0, quads=2)
                for pair in range(2):
                    sp.wait_ge(parts_out[pair], B * 96)
                place_max(0, 0, 0)
                post.load(sp, io)
                over_groups(sp, group, 1, 3)
                sp.wait_ge(ctx_done, 2 * KT)
                for qt in range(2):
                    sp.dma_start(post.a_tile[:, qt, :].rearrange("p (g c) -> p g c", g=KT),
                                 token_tile(heads, 0, qt)).then_inc(a_in, 16)
                sp.wait_ge(a_in, 32)

            @block.gpsimd
            def _(pool):
                previous.clear_sems(pool)
                for par in range(2):
                    pool.memset(v_group[:, par, :, :, :], 1.0).then_inc(ones_set, 1)
                for buf in range(4):
                    pool.wait_ge(ones_set, 2 + buf)
                    pool.memset(k_rows[QK_ROWS:MAX_ROWS, buf, :, :], -1.0).then_inc(ones_set, 1)
                pool.wait_ge(ones_set, 6)
                pool.memset(zeros[:, :, :], 0.0).then_inc(ones_set, 1)
                pool.wait_ge(ones_set, 7)

                def max_split(v, quad):
                    pool.wait_ge(s_max, 16 * (v + 1))
                    wait(pool, maxT_done, v)
                    pool.tensor_tensor(max_parts[:, :, 0, :], row_max[:, quad, :, :], zeros[:, :, :], ALU.add)\
                        .then_inc(part_step, 1)
                    pool.wait_ge(part_step, 3 * v + 1)
                    pool.tensor_tensor(max_rest[:, :, :], row_max[:, quad, :, :], max_parts[:, :, 0, :], ALU.subtract)\
                        .then_inc(part_step, 1)
                    pool.wait_ge(part_step, 3 * v + 2)
                    pool.tensor_tensor(max_parts[:, :, 1, :], max_rest[:, :, :], zeros[:, :, :], ALU.add)\
                        .then_inc(part_step, 1)
                    pool.wait_ge(part_step, 3 * v + 3)
                    pool.tensor_tensor(max_parts[:, :, 2, :], max_rest[:, :, :], max_parts[:, :, 1, :], ALU.subtract)\
                        .then_inc(parts_ready, 1)

                def copy_values(t, par, k):
                    src = heads[:, bass.ds(t * C, C)].rearrange("p (k h d) -> p k h d", k=QT, h=GH)
                    pool.tensor_copy(v_group[:, par, k, :, 0:HD], src[:, k, :, :]).then_inc(v_ready, 1)

                def group(t, par):
                    for s in range(STEPS):
                        if causal:
                            pool.wait_ge(exp_done, 4 * STEPS * t + 4 * s + 4)
                            pool.tensor_tensor(gate[:, s:s + 1], zeros[:, 0, 0:1], zeros[:, 0, 1:2], ALU.add)
                            q0 = s % QT * P
                            diagonal = probs[:, s % 2, :, q0:q0 + P]
                            pool.affine_select(diagonal, diagonal, [[0, QH], [1, P]], ALU.is_ge, 0.0, base=0,
                                               channel_multiplier=-1).then_inc(masked, 1)
                        if isinstance(t, int) and t < 3:
                            post.prepare(pool, t, s, const)
                        if not causal and s == QT:
                            post.add_bias(pool, t, X)
                        if 1 < s < 2 + QT and (not isinstance(t, int) or t + 1 < GROUPS):
                            wait(pool, pv_done, STEPS * t)
                            copy_values(t + 1, 1 - par, s - 2)
                        if s % QH == QH - 1 and (not isinstance(t, int) or t + 1 < GROUPS):
                            max_split(2 * t + 2 + s // QH, s // QH)

                for k in range(QT):
                    copy_values(0, 0, k)
                max_split(0, 0)
                max_split(1, 1)
                over_groups(pool, group, 3, 1)

            @block.vector
            def _(dve):
                dve.tensor_copy(identb[:, :], const[:, IDENT:IDENT + P]).then_inc(consts_set, 1)
                dve.tensor_copy(maskb[:, :], const[:, MASK:MASK + P]).then_inc(consts_set, 1)

                def head_max(v, quad, h):
                    for i in range(0, QT, SPAN):
                        qt = S_ORDER[i]
                        dve.wait_ge(s_tile, 16 * v + 4 * h + with_bank(i))
                        src = s_bank[qt] if causal else s_banks[:, qt:qt + SPAN, :]
                        dve.reduce_max(row_max[:, quad, qt:qt + SPAN, h:h + 1], src, AX_X)\
                           .then_inc(s_max, SPAN)

                def normalize(v, t, quad):
                    dve.wait_ge(oT_done, v + 1)
                    o = t_bank[:, :].rearrange("p (q h d) -> p q h d", q=QT, h=QH)
                    dve.reciprocal(sums[:, :, :], o[:, :, :, HD]).then_inc(sums_done, 1)
                    dve.wait_ge(sums_done, v + 1)
                    dst = heads[:, bass.ds(t * C, C)].rearrange("p (q c) -> p q c", q=QT)
                    dst = dst[:, :, quad * 64:quad * 64 + 64].rearrange("p q (h d) -> p q h d", h=QH)
                    inv = sums[:, :, :].unsqueeze(3).to_broadcast([P, QT, QH, HD])
                    dve.tensor_tensor(dst, o[:, :, :, 0:HD], inv, ALU.mult).then_inc(ctx_done, 1)

                def group(t, par):
                    static = isinstance(t, int)
                    for s in range(STEPS):
                        if not static or t + 1 < GROUPS:
                            head_max(2 * t + 2 + s // QH, s // QH, s % QH)
                        if s == 2 and not (static and t == 0):
                            normalize(2 * t - 1, t - 1, 1)
                        if s == 6:
                            normalize(2 * t, t, 0)

                for s in range(STEPS):
                    head_max(s // QH, s // QH, s % QH)
                over_groups(dve, group, 1, 1)
                normalize(2 * GROUPS - 1, GROUPS - 1, 1)

            @block.scalar
            def _(act):
                MAX_AFTER = 3 if causal else 2

                def copy_max(v, quad):
                    act.wait_ge(maxT_done, v + 1)
                    act.activation(max_rows[:, quad, :], t_half[0:PARTS * QH, 0:T], ACT.Copy).then_inc(max_copied, 1)

                def copy_out(v, step):
                    act.wait_ge(pv_done, step + 1)
                    act.activation(o_rows[:, :], o_bank[:, :], ACT.Copy).then_inc(o_copied, 1)

                def group(t, par):
                    first = isinstance(t, int) and t == 0
                    last = isinstance(t, int) and t + 1 == GROUPS
                    for s in range(STEPS):
                        k = s % QT
                        q0 = k * P if causal else 0
                        for h in range(QH):
                            act.wait_ge(st_tile, 4 * STEPS * t + 4 * s + h + 1)
                            act.activation(probs[:, s % 2, h, q0:T], st_use(s, h)[0][:, q0:T], ACT.Exp, scale=SCALE)\
                               .then_inc(exp_done, 1)
                            if s == 1 and h == 0 and not first:
                                copy_out(2 * t - 1, STEPS * t - 1)
                            if s == 1 and h == MAX_AFTER:
                                copy_max(2 * t + 1, 1)
                            if s == 5 and h == 0:
                                copy_out(2 * t, STEPS * t + 3)
                            if s == 5 and h == MAX_AFTER and not last:
                                copy_max(2 * t + 2, 0)

                copy_max(0, 0)
                over_groups(act, group, 1, 1)
                copy_out(2 * GROUPS - 1, STEPS * GROUPS - 1)

            @block.tensor
            def _(pe):
                pe.wait_ge(consts_set, 2)

                def score_tile(v, buf, h, i):
                    qt = S_ORDER[i]
                    n = (qt + 1) * P if causal else T
                    wait(pe, s_max, 16 * v + 4 * h - QT + with_bank(i))
                    mm = pe.matmul(s_bank[qt], q_rows[0:QK_ROWS, buf, h, qt * P:(qt + 1) * P],
                                   k_rows[0:QK_ROWS, buf, h, 0:n], start=True, stop=not causal)
                    if causal:
                        mm = pe.matmul(s_bank[qt][:, n - P:n], identb[:, :], maskb[:, :], start=False, stop=True)
                    mm.then_inc(s_tile, 1)

                def shifted_tile(t, s, buf, h):
                    k = s % QT
                    q0 = k * P if causal else 0
                    bank, back = st_use(s, h)
                    wait(pe, exp_done, 4 * STEPS * t + 4 * s + h - back + 1)
                    mm = pe.matmul(bank[:, q0:T], k_rows[0:MAX_ROWS, buf, h, k * P:(k + 1) * P],
                                   q_rows[0:MAX_ROWS, buf, h, q0:T], start=True, stop=True)
                    mm.then_inc(st_tile, 1)

                def weigh(t, par, s):
                    k = s % QT
                    q0 = k * P if causal else 0
                    step = STEPS * t + s
                    if k == 0:
                        wait(pe, o_copied, 2 * t + s // QT)
                        pe.wait_ge(v_ready, QT * (t + 1))
                    if causal:
                        pe.wait_ge(masked, step + 1)
                    else:
                        pe.wait_ge(exp_done, 4 * step + 4)
                    for h in range(QH):
                        mm = pe.matmul(o_bank[32 * h:32 * h + 32, q0:T], v_group[:, par, k, s // QT * QH + h, :],
                                       probs[:, s % 2, h, q0:T], start=(k == 0), stop=(k == QT - 1))
                    mm.then_inc(pv_done, 1)

                def max_transpose(v):
                    pe.wait_ge(parts_ready, v + 1)
                    wait(pe, max_copied, v)
                    wait(pe, ctx_done, v - 2)
                    for qt in range(QT):
                        t = pe.transpose(t_half[0:PARTS * QH, qt * P:(qt + 1) * P],
                                         max_parts[:, qt, :, :], identb[:, :])
                    t.then_inc(maxT_done, 1)

                def out_transpose(v, maxima):
                    pe.wait_ge(o_copied, v + 1)
                    pe.wait_ge(max_copied, maxima)
                    wait(pe, ctx_done, v)
                    for qt in range(QT):
                        t = pe.transpose(t_bank[:, qt * P:(qt + 1) * P], o_rows[:, qt * P:(qt + 1) * P],
                                         const[:, IDENT:IDENT + P])
                    t.then_inc(oT_done, 1)

                def group(t, par):
                    first = isinstance(t, int) and t == 0
                    last = isinstance(t, int) and t + 1 == GROUPS
                    for s in range(STEPS):
                        quad = s // QT
                        if s % QT == 0:
                            if not last:
                                wait(pe, qk_in[2 * (1 - par) + quad], loads(t + 1, 1 - par, quad))
                            pe.wait_ge(max_in[quad], 16 * PARTS * (t + 1))
                        buf, ahead = 2 * par + quad, 2 * (1 - par) + quad
                        shifted_tile(t, s, buf, 0)
                        if not last:
                            for i in range(2 if causal else 3):
                                score_tile(2 * t + 2 + quad, ahead, s % QT, i)
                        shifted_tile(t, s, buf, 1)
                        if causal:
                            if not last:
                                score_tile(2 * t + 2 + quad, ahead, s % QT, 2)
                            shifted_tile(t, s, buf, 2)
                        if not last:
                            score_tile(2 * t + 2 + quad, ahead, s % QT, 3)
                        shifted_tile(t, s, buf, 3 if causal else 2)
                        if s > 0:
                            weigh(t, par, s - 1)
                        elif not first:
                            weigh(t - 1, 1 - par, STEPS - 1)
                        if not causal:
                            shifted_tile(t, s, buf, 3)
                        if s == 0:
                            max_transpose(2 * t + 1)
                        if s == 2 and not first:
                            out_transpose(2 * t - 1, 2 * t + 2)
                        if s == 4 and not last:
                            max_transpose(2 * t + 2)
                        if s == 6:
                            out_transpose(2 * t, 2 * t + 2 if last else 2 * t + 3)

                for quad in range(2):
                    pe.wait_ge(qk_in[quad], loads(0, 0, quad))
                    for h in range(QH):
                        for i in range(QT):
                            score_tile(quad, quad, h, i)
                        if (quad, h) == (1, 1):
                            max_transpose(0)
                pe.wait_ge(ones_set, 6)
                over_groups(pe, group, 1, 1)
                weigh(GROUPS - 1, 1, STEPS - 1)
                out_transpose(2 * GROUPS - 1, 2 * GROUPS)

        return m


def fetch_outputs(sp, heads, a_tile, b, qt, a_in, aT_done):
    j = QT * b + qt
    wait(sp, aT_done, j - 1)
    sp.dma_start(a_tile[:, qt % 2, :].rearrange("p (g c) -> p g c", g=KT), token_tile(heads, b, qt))\
      .then_inc(a_in[qt % 2], 16)


def outputs_in(b, qt):
    return 16 * (b * (QT // 2) + qt // 2)


def low_part(dve, out, bank, high):
    return dve.tensor_tensor(out, bank, high, ALU.subtract)


def post0_phase(nc, previous, io, X, heads, const, weights, qkv):
    w_hi, w_lo, bias, a_tile = weights.hi, weights.lo, weights.bias, weights.a_tile
    with ExitStack() as stack:
        m = Memory(nc, stack, "post0")
        eps = m.sb("eps", [P, 1])
        gate = m.sb("gate", [P, 1])
        aT_hi = m.sb("aT_hi", [P, 2, C], F32R)
        aT_lo = m.sb("aT_lo", [P, 2, C], F32R)
        xT_hi = m.sb("xT_hi", [P, 2, C], F32R)
        xT_lo = m.sb("xT_lo", [P, 2, C], F32R)
        xn = m.sb("xn", [P, 2, C])
        stats = m.sb("stats", [P, 6])
        mean_var = m.sb("mean_var", [P, 2])
        std = m.sb("std", [P, 1])
        rstd = m.sb("rstd", [P, 1])
        next_raw = m.sb("next_raw", [P, 2, KT, C])

        aT_bank, xT_bank = m.bank("aT"), m.bank("xT")
        o_bank = [m.bank(f"o{i}") for i in range(2)]
        f_bank = [m.bank(f"f{i}") for i in range(2)]

        eps_set, next_in, next_split = m.sem("eps_set"), m.sem("next_in"), m.sem("next_split")
        a_in = [m.sem(f"a_in{i}") for i in range(2)]
        aT_done, ah_done, al_done = m.sem("aT_done"), m.sem("ah_done"), m.sem("al_done")
        xT_done, xh_done, xl_done = m.sem("xT_done"), m.sem("xh_done"), m.sem("xl_done")
        o_done, f_done = m.sem("o_done"), m.sem("f_done")
        ln_step, std_done, xn_done = m.sem("ln_step"), m.sem("std_done"), m.sem("xn_done")
        o_read, bias_added, x_final = m.sem("o_read"), m.sem("bias_added"), m.sem("x_final")

        def xtile(j):
            return X[:, bass.ds(j * C, C)]

        with nc.Block() as block:

            @block.sync
            def _(sp):
                def load_next(n):
                    wait(sp, next_split, 2 * n - 2)
                    name = ("L1_attn_wq", "L1_attn_wk", "L1_attn_wv")[n]
                    sp.dma_start(next_raw[:, n % 2, :, :], io[name].rearrange("(k p) n -> p k n", p=P)).then_inc(next_in, 16)

                def tile(b, qt, one, two):
                    if two:
                        fetch_outputs(sp, heads, a_tile, b + (qt + 2) // QT, (qt + 2) % QT, a_in, aT_done)
                    if isinstance(b, int) and b == B - 1 and qt == 0:
                        load_next(2)

                load_next(0)
                load_next(1)
                over_batches(sp, tile)

            @block.gpsimd
            def _(pool):
                previous.clear_sems(pool)
                def next_high(n):
                    pool.wait_ge(next_in, 16 * (n + 1))
                    pool.tensor_scalar(qkv.hi[:, n, :, :], next_raw[:, n % 2, :, :], 1.0, None, ALU.mult)\
                        .then_inc(next_split, 1)

                def next_low(n):
                    pool.wait_ge(next_split, 2 * n + 1)
                    pool.tensor_tensor(qkv.lo[:, n, :, :], next_raw[:, n % 2, :, :], qkv.hi[:, n, :, :], ALU.subtract)\
                        .then_inc(next_split, 1)

                def tile(b, qt, one, two):
                    j = QT * b + qt
                    pool.wait_ge(xn_done, j + 1)
                    pool.tensor_tensor(xtile(j), xtile(j), bias[:, 1, :], ALU.add).then_inc(bias_added, 1)
                    if isinstance(b, int) and b == 0:
                        if qt == 1:
                            next_high(0)
                        if qt == 2:
                            next_low(0)
                        if qt == 3:
                            next_high(1)
                    if isinstance(b, int) and b == B - 1:
                        if qt == 0:
                            next_low(1)
                        if qt == 1:
                            next_high(2)
                        if qt == 2:
                            next_low(2)

                over_batches(pool, tile)

            @block.scalar
            def _(act):
                def high(out, bank, ready, j, done):
                    act.wait_ge(ready, j + 1)
                    act.activation(out, bank, ACT.Copy).then_inc(done, 1)

                def a_high(j, par):
                    high(aT_hi[:, par, :], aT_bank[:, :], aT_done, j, ah_done)

                def ln_std(j):
                    act.wait_ge(ln_step, 3 * j + 2)
                    act.activation(std[:, :], mean_var[:, 1:2], ACT.Sqrt, bias=eps[:, 0:1]).then_inc(std_done, 1)

                def tile(b, qt, one, two):
                    j, par = QT * b + qt, qt % 2
                    if two:
                        a_high(j + 2, par)
                    high(xT_hi[:, par, :], xT_bank[:, :], xT_done, j, xh_done)
                    if one:
                        ln_std(j + 1)

                a_high(0, 0)
                a_high(1, 1)
                act.wait_ge(eps_set, 1)
                ln_std(0)
                over_batches(act, tile)

            @block.vector
            def _(dve):
                dve.memset(eps[:, :], EPS).then_inc(eps_set, 1)

                def a_low(j, par):
                    dve.wait_ge(ah_done, j + 1)
                    low_part(dve, aT_lo[:, par, :], aT_bank[:, :], aT_hi[:, par, :]).then_inc(al_done, 1)

                def attended(j, par):
                    dve.wait_ge(o_done, j + 1)
                    dve.tensor_tensor(xtile(j), o_bank[par][:, :], xtile(j), ALU.add).then_inc(o_read, 1)
                    gated_wait(dve, gate, o_read, j + 1)
                    dve.bn_stats(stats[:, :], xtile(j)).then_inc(ln_step, 1)
                    gated_wait(dve, gate, ln_step, 3 * j + 1)
                    dve.bn_aggr(mean_var[:, :], stats[:, :]).then_inc(ln_step, 1)

                def normalized(j, par):
                    dve.wait_ge(std_done, j + 1)
                    dve.reciprocal(rstd[:, :], std[:, :]).then_inc(ln_step, 1)
                    dve.wait_ge(ln_step, 3 * j + 3)
                    wait(dve, xT_done, j - 1)
                    dve.tensor_scalar(xn[:, par, :], xtile(j), mean_var[:, 0:1], rstd[:, 0:1],
                                      ALU.subtract, ALU.mult).then_inc(xn_done, 1)

                def final(j, par):
                    dve.wait_ge(bias_added, j + 1)
                    dve.wait_ge(f_done, j + 1)
                    dve.tensor_tensor(xtile(j), f_bank[par][:, :], xtile(j), ALU.add).then_inc(x_final, 1)

                def tile(b, qt, one, two):
                    j, par = QT * b + qt, qt % 2
                    if one:
                        attended(j + 1, 1 - par)
                    if two:
                        a_low(j + 2, par)
                    if one:
                        normalized(j + 1, 1 - par)
                    dve.wait_ge(xh_done, j + 1)
                    low_part(dve, xT_lo[:, par, :], xT_bank[:, :], xT_hi[:, par, :]).then_inc(xl_done, 1)
                    if not (isinstance(j, int) and j == 0):
                        final(j - 1, 1 - par)

                a_low(0, 0)
                a_low(1, 1)
                attended(0, 0)
                normalized(0, 0)
                over_batches(dve, tile)
                final(TILES - 1, (TILES - 1) % 2)

            @block.tensor
            def _(pe):
                ident = const[:, IDENT:IDENT + P]

                def a_transpose(b, qt):
                    wait(pe, al_done, QT * b + qt)
                    wait(pe, a_in[qt % 2], outputs_in(b, qt))
                    for g in range(KT):
                        t = pe.transpose(aT_bank[:, g * P:(g + 1) * P], a_tile[:, qt % 2, g * P:(g + 1) * P], ident)
                    t.then_inc(aT_done, 1)

                def x_transpose(j, par):
                    pe.wait_ge(xn_done, j + 1)
                    wait(pe, xl_done, j)
                    for k in range(KT):
                        t = pe.transpose(xT_bank[:, k * P:(k + 1) * P], xn[:, par, k * P:(k + 1) * P], ident)
                    t.then_inc(xT_done, 1)

                def product(bank, hi, lo, w, done):
                    for k in range(KT):
                        mm = three_pass(pe, bank[:, :], hi[:, k * P:(k + 1) * P], lo[:, k * P:(k + 1) * P],
                                        w_hi[:, w, k, :], w_lo[:, w, k, :], k == 0, k == KT - 1)
                    mm.then_inc(done, 1)

                def attended(j, par):
                    pe.wait_ge(al_done, j + 1)
                    wait(pe, o_read, j - 1)
                    product(o_bank[par], aT_hi[:, par, :], aT_lo[:, par, :], 0, o_done)

                def dequantized(j, par):
                    pe.wait_ge(xl_done, j + 1)
                    wait(pe, x_final, j - 1)
                    product(f_bank[par], xT_hi[:, par, :], xT_lo[:, par, :], 1, f_done)

                def tile(b, qt, one, two):
                    j, par = QT * b + qt, qt % 2
                    if one:
                        attended(j + 1, 1 - par)
                    if two:
                        a_transpose(b + (qt + 2) // QT, (qt + 2) % QT)
                    x_transpose(j, par)
                    if not (isinstance(j, int) and j == 0):
                        dequantized(j - 1, 1 - par)

                a_transpose(0, 0)
                a_transpose(0, 1)
                attended(0, 0)
                over_batches(pe, tile)
                dequantized(TILES - 1, (TILES - 1) % 2)

        return m


def post1_phase(nc, previous, X, heads, const, out, weights):
    a_tile, signs, s_in, s2x = weights.a_tile, weights.signs, weights.s_in, weights.s2x
    with ExitStack() as stack:
        m = Memory(nc, stack, "post1", "right")
        eps = m.sb("eps", [P, 1])
        gate = m.sb("gate", [P, 1])
        aT_hi = m.sb("aT_hi", [P, 2, C], F32R)
        aT_lo = m.sb("aT_lo", [P, 2, C], F32R)
        act_hi = m.sb("act_hi", [P, 3, KT, T], F32R)
        act_lo = m.sb("act_lo", [P, 3, KT, T], F32R)
        relu = m.sb("relu", [P, KT, T])
        xn = m.sb("xn", [P, QT, C])
        stats = m.sb("stats", [P, 6])
        mean_var = m.sb("mean_var", [P, 2])
        std = m.sb("std", [P, 1])
        rstd = m.sb("rstd", [P, 1])

        aT_bank = m.bank("aT")
        xT_bank = [m.bank(f"xT{i}") for i in range(3)]
        o_bank = [m.bank(f"o{i}") for i in range(2)]
        h_bank = [m.bank(f"h{i}") for i in range(2)]

        eps_set = m.sem("eps_set")
        a_in = [m.sem(f"a_in{i}") for i in range(2)]
        aT_done, ah_done, al_done = m.sem("aT_done"), m.sem("ah_done"), m.sem("al_done")
        xT_done, xh_done, xl_done = m.sem("xT_done"), m.sem("xh_done"), m.sem("xl_done")
        o_done, o_read = m.sem("o_done"), m.sem("o_read")
        ln_step, std_done, xn_done = m.sem("ln_step"), m.sem("std_done"), m.sem("xn_done")
        h_done, relu_done, hh_done, hl_done = m.sem("h_done"), m.sem("relu_done"), m.sem("hh_done"), m.sem("hl_done")
        x_final, x_out = m.sem("x_final"), m.sem("x_out")
        BANKS = 3 * QT

        def xtile(j):
            return X[:, bass.ds(j * C, C)]

        with nc.Block() as block:

            def over(eng, batch):
                batch(0, True)
                with eng.Fori(1, B - 1) as b:
                    batch(b, True)
                batch(B - 1, False)

            @block.sync
            def _(sp):
                for qt in range(2, QT):
                    fetch_outputs(sp, heads, a_tile, 0, qt, a_in, aT_done)

                def batch(b, more):
                    if more:
                        for qt in range(QT):
                            fetch_outputs(sp, heads, a_tile, b + 1, qt, a_in, aT_done)

                over(sp, batch)

            @block.gpsimd
            def _(pool):
                previous.clear_sems(pool)
                def batch(b, more):
                    for qt in range(QT):
                        pool.wait_ge(x_final, QT * b + qt + 1)
                        pool.dma_start(out[bass.ds(b, 1), qt * P:(qt + 1) * P, :].rearrange("o p c -> (o p) c"),
                                       xtile(QT * b + qt)).then_inc(x_out, 16)

                over(pool, batch)
                pool.wait_ge(x_out, 16 * TILES)

            @block.scalar
            def _(act):
                def a_high(j, par):
                    act.wait_ge(aT_done, j + 1)
                    act.activation(aT_hi[:, par, :], aT_bank[:, :], ACT.Copy).then_inc(ah_done, 1)

                def ln_std(j):
                    act.wait_ge(ln_step, 3 * j + 2)
                    act.activation(std[:, :], mean_var[:, 1:2], ACT.Sqrt, bias=eps[:, 0:1]).then_inc(std_done, 1)

                def layer_high(b, n, features):
                    for k in features:
                        use = 2 * KT * b + KT * n + k
                        act.wait_ge(h_done, BANKS * b + KT * n + k + 1)
                        wait(act, hl_done, use - KT + 1)
                        act.activation(relu[:, k, :], h_bank[k % 2][:, :], ACT.Relu, scale=s2x[:, n:n + 1])\
                           .then_inc(relu_done, 1)
                        act.wait_ge(relu_done, use + 1)
                        act.activation(act_hi[:, n + 1, k, :], relu[:, k, :], ACT.Copy).then_inc(hh_done, 1)

                def turn_high(b):
                    for qt in range(QT):
                        act.wait_ge(xT_done, QT * b + qt + 1)
                        act.activation(act_hi[:, 0, :, qt * P:(qt + 1) * P],
                                       xT_bank[qt % 3][:, :].rearrange("p (k t) -> p k t", k=KT), ACT.Copy)\
                           .then_inc(xh_done, 1)

                def batch(b, more):
                    j = QT * (b + 1)
                    if more:
                        a_high(j, 0)
                    turn_high(b)
                    if more:
                        a_high(j + 1, 1)
                        ln_std(j)
                    layer_high(b, 0, range(KT))
                    if more:
                        a_high(j + 2, 0)
                        ln_std(j + 1)
                    layer_high(b, 1, range(KT // 2))
                    if more:
                        a_high(j + 3, 1)
                        ln_std(j + 2)
                    layer_high(b, 1, range(KT // 2, KT))
                    if more:
                        ln_std(j + 3)

                a_high(0, 0)
                a_high(1, 1)
                act.wait_ge(eps_set, 1)
                for j in range(QT):
                    if j + 2 < QT:
                        a_high(j + 2, j % 2)
                    ln_std(j)
                over(act, batch)

            @block.vector
            def _(dve):
                dve.memset(eps[:, :], EPS).then_inc(eps_set, 1)

                def a_low(j, par):
                    dve.wait_ge(ah_done, j + 1)
                    low_part(dve, aT_lo[:, par, :], aT_bank[:, :], aT_hi[:, par, :]).then_inc(al_done, 1)

                def attended(j, par):
                    dve.wait_ge(o_done, j + 1)
                    dve.tensor_tensor(xtile(j), o_bank[par % 2][:, :], xtile(j), ALU.add).then_inc(o_read, 1)
                    gated_wait(dve, gate, o_read, j + 1)
                    dve.bn_stats(stats[:, :], xtile(j)).then_inc(ln_step, 1)
                    gated_wait(dve, gate, ln_step, 3 * j + 1)
                    dve.bn_aggr(mean_var[:, :], stats[:, :]).then_inc(ln_step, 1)

                def normalized(j, par):
                    dve.wait_ge(std_done, j + 1)
                    dve.reciprocal(rstd[:, :], std[:, :]).then_inc(ln_step, 1)
                    dve.wait_ge(ln_step, 3 * j + 3)
                    dve.tensor_scalar(xn[:, par, :], xtile(j), mean_var[:, 0:1], rstd[:, 0:1],
                                      ALU.subtract, ALU.mult).then_inc(xn_done, 1)

                def layer_low(b, n, features):
                    for k in features:
                        dve.wait_ge(hh_done, 2 * KT * b + KT * n + k + 1)
                        low_part(dve, act_lo[:, n + 1, k, :], relu[:, k, :], act_hi[:, n + 1, k, :])\
                            .then_inc(hl_done, 1)

                def batch(b, more):
                    j = QT * (b + 1)
                    if more:
                        a_low(j, 0)
                    for qt in range(QT):
                        dve.wait_ge(xh_done, QT * b + qt + 1)
                        low_part(dve, act_lo[:, 0, :, qt * P:(qt + 1) * P],
                                 xT_bank[qt % 3][:, :].rearrange("p (k t) -> p k t", k=KT),
                                 act_hi[:, 0, :, qt * P:(qt + 1) * P]).then_inc(xl_done, 1)
                    if more:
                        attended(j, 0)
                        a_low(j + 1, 1)
                        normalized(j, 0)
                    layer_low(b, 0, range(KT))
                    if more:
                        attended(j + 1, 1)
                        a_low(j + 2, 0)
                        normalized(j + 1, 1)
                    layer_low(b, 1, range(KT // 2))
                    if more:
                        attended(j + 2, 2)
                        a_low(j + 3, 1)
                        normalized(j + 2, 2)
                    layer_low(b, 1, range(KT // 2, KT))
                    if more:
                        attended(j + 3, 3)
                        normalized(j + 3, 3)
                    for qt in range(QT):
                        dve.wait_ge(h_done, BANKS * b + 2 * KT + qt + 1)
                        dve.scalar_tensor_tensor(xtile(QT * b + qt), h_bank[qt % 2][:, :], s_in[:, 2:3],
                                                 xtile(QT * b + qt), ALU.mult, ALU.add).then_inc(x_final, 1)

                a_low(0, 0)
                a_low(1, 1)
                for j in range(QT):
                    attended(j, j)
                    if j + 2 < QT:
                        a_low(j + 2, j % 2)
                    normalized(j, j)
                over(dve, batch)

            @block.tensor
            def _(pe):
                ident = const[:, IDENT:IDENT + P]

                def a_transpose(b, qt):
                    wait(pe, al_done, QT * b + qt)
                    wait(pe, a_in[qt % 2], outputs_in(b, qt))
                    for g in range(KT):
                        t = pe.transpose(aT_bank[:, g * P:(g + 1) * P], a_tile[:, qt % 2, g * P:(g + 1) * P], ident)
                    t.then_inc(aT_done, 1)

                def attended(j, par):
                    pe.wait_ge(al_done, j + 1)
                    wait(pe, o_read, j - 1)
                    for k in range(KT):
                        mm = three_pass(pe, o_bank[par][:, :], aT_hi[:, par, k * P:(k + 1) * P],
                                        aT_lo[:, par, k * P:(k + 1) * P], weights.hi[:, k, :], weights.lo[:, k, :],
                                        k == 0, k == KT - 1)
                    mm.then_inc(o_done, 1)

                def bank_free(b, use):
                    if use < 2:
                        wait(pe, x_final, QT * b - 1 + use)
                    elif use < 2 * KT + 2:
                        pe.wait_ge(relu_done, 2 * KT * b + use - 1)
                    else:
                        pe.wait_ge(x_final, QT * b + use - 2 * KT - 1)

                def layer(b, n, outputs):
                    for o in outputs:
                        bank_free(b, KT * n + o)
                        for k in range(KT):
                            if n:
                                pe.wait_ge(hl_done, 2 * KT * b + KT * (n - 1) + k + 1)
                            w = signs[:, n, k, o * P:(o + 1) * P]
                            pe.matmul(h_bank[o % 2][:, :], w, act_hi[:, n, k, :], start=(k == 0), stop=False)
                            mm = pe.matmul(h_bank[o % 2][:, :], w, act_lo[:, n, k, :], start=False, stop=(k == KT - 1))
                        mm.then_inc(h_done, 1)

                def last_layer(b):
                    for qt in range(QT):
                        bank_free(b, 2 * KT + qt)
                        for k in range(KT):
                            pe.wait_ge(hl_done, 2 * KT * b + KT + k + 1)
                            w = signs[:, 2, k, :]
                            pe.matmul(h_bank[qt % 2][:, :], act_hi[:, 2, k, qt * P:(qt + 1) * P], w,
                                      start=(k == 0), stop=False)
                            mm = pe.matmul(h_bank[qt % 2][:, :], act_lo[:, 2, k, qt * P:(qt + 1) * P], w,
                                           start=False, stop=(k == KT - 1))
                        mm.then_inc(h_done, 1)

                def turn(b):
                    for qt in range(QT):
                        pe.wait_ge(xn_done, QT * b + qt + 1)
                        if qt == 3:
                            pe.wait_ge(xl_done, QT * b + 1)
                        for k in range(KT):
                            t = pe.transpose(xT_bank[qt % 3][:, k * P:(k + 1) * P], xn[:, qt, k * P:(k + 1) * P], ident)
                        t.then_inc(xT_done, 1)

                def batch(b, more):
                    j = QT * (b + 1)
                    if more:
                        a_transpose(b + 1, 0)
                    turn(b)
                    if more:
                        attended(j, 0)
                        a_transpose(b + 1, 1)
                    pe.wait_ge(xl_done, QT * b + QT)
                    layer(b, 0, range(KT))
                    if more:
                        attended(j + 1, 1)
                        a_transpose(b + 1, 2)
                    layer(b, 1, range(KT // 2))
                    if more:
                        attended(j + 2, 0)
                        a_transpose(b + 1, 3)
                    layer(b, 1, range(KT // 2, KT))
                    if more:
                        attended(j + 3, 1)
                    last_layer(b)

                a_transpose(0, 0)
                a_transpose(0, 1)
                for j in range(QT):
                    attended(j, j % 2)
                    if j + 2 < QT:
                        a_transpose(0, j + 2)
                over(pe, batch)

        return m


def build(nc, io, out):
    parts_dram = [nc.dram_tensor(f"qk_parts{i}", [GROUPS, 2, PARTS, P, T], BF16, kind="Internal").ap() for i in range(2)]
    with ExitStack() as ctx:
        m = Memory(nc, ctx, "main")
        X = m.sb("x", [P, TILES * C])
        const = m.sb("const", [P, CONSTS])
        parts_out = [[m.sem(f"parts_out{i}{n}") for n in range(2)] for i in range(2)]
        heads = m.sb("heads", [P, TILES * C])
        with ExitStack() as stack:
            pre = pre_phase(nc, None, 0, io, X, heads, parts_dram[0], parts_out[0], const,
                            QkvWeights(nc, stack, 0, "right"))
        with ExitStack() as qkv_stack:
            with ExitStack() as stack:
                weights = Post0Weights(nc, stack)
                attention = attention_phase(nc, pre, 0, io, X, heads, parts_dram[0], parts_out[0], const, weights)
                pre.sem_stack.close()
                qkv = QkvWeights(nc, qkv_stack, 1, "right")
                post = post0_phase(nc, attention, io, X, heads, const, weights, qkv)
                attention.sem_stack.close()
            pre = pre_phase(nc, post, 1, io, X, heads, parts_dram[1], parts_out[1], const, qkv)
            post.sem_stack.close()
        with ExitStack() as stack:
            weights = Post1Weights(nc, stack)
            attention = attention_phase(nc, pre, 1, io, X, heads, parts_dram[1], parts_out[1], const, weights)
            pre.sem_stack.close()
            post = post1_phase(nc, attention, X, heads, const, out, weights)
            attention.sem_stack.close()
            post.sem_stack.close()


TURNED = ("L0_ffn_q_scales", "L0_ffn_q_vals", "L1_attn_wq", "L1_attn_wk", "L1_attn_wv")
ROWS = ("L0_attn_attn_qkvb", "L0_attn_attn_ob", "L0_ffn_bias", "L1_ffn_s0", "L1_ffn_s1", "L1_ffn_s2")


def lay_out(inputs):
    arrays = {}
    for name, a in inputs.items():
        a = np.asarray(a)
        if name in TURNED:
            a = a.reshape(C, -1).T
        elif name == "L1_attn_wo":
            a = a.T
        elif name in ROWS:
            a = a.reshape(1, -1)
        arrays[name] = np.ascontiguousarray(a)
    arrays["consts"] = table_of_constants()
    return arrays


def kernel(**inputs):
    import concourse.bacc as bacc
    from concourse.bass_utils import run_bass_kernel_spmd

    nc = bacc.Bacc("TRN2", target_bir_lowering=False, num_devices=1)
    arrays = lay_out(inputs)
    io = {name: nc.dram_tensor(f"in_{name}", a.shape, mybir.dt.from_np(a.dtype), kind="ExternalInput").ap()
          for name, a in arrays.items()}
    out = nc.dram_tensor("out", (B, T, C), F32, kind="ExternalOutput").ap()
    build(nc, io, out)
    r = run_bass_kernel_spmd(nc, [{f"in_{name}": a for name, a in arrays.items()}], core_ids=[0])
    return r.results[0]["out"]
```
